# Optimizing a Trainium2 kernel written in Bass

```python
import numpy as np
import jax
import jax.numpy as jnp

def _softmax(x, axis=-1):
    return jax.nn.softmax(x, axis=axis)
def _gelu(x):
    return jax.nn.gelu(x, approximate=True)
def _silu(x):
    return jax.nn.silu(x)
def _sigmoid(x):
    return jax.nn.sigmoid(x)
def _layernorm(x, axis=-1, eps=1e-5):
    m = jnp.mean(x, axis=axis, keepdims=True)
    v = jnp.var(x, axis=axis, keepdims=True)
    return (x - m) / jnp.sqrt(v + eps)
def _scatter_add(tgt, idx, src, axis=0):
    return tgt.at[idx].add(src)
def _segment_sum(src, seg, n):
    return jax.ops.segment_sum(src, seg, n)

kernel_name = 'mk_metaformer_d1_conv_nhwc384_47ad5f'

def setup_inputs(seed: int = 0):
    np.random.seed(seed)
    _w = jnp.asarray
    def _rec_inputs():
        import jax
        import jax.numpy as jnp
        _gk = jax.random.key(seed)
        x = -0.001003 + 1 * jax.random.normal(jax.random.fold_in(_gk, 1), (4, 32, 32, 384), jnp.float32)
        return x
    x = _rec_inputs()
    def _L0_conv_setup():
        import jax, jax.numpy as jnp
        import numpy as np
        from jax import lax
        B, H, W = (4, 32, 32)
        NC, HEADS, HC, G = (384, 6, 64, 6)
        GC = NC // G
        GH = HEADS // G
        KK = 3
        OUT_DIM = 384

        def _bilinear_sample(image, warp):
            Bq, C = (image.shape[0], image.shape[-1])
            img = jnp.pad(image, ((0, 0), (1, 1), (1, 1), (0, 0)))
            Hp, Wp = (img.shape[1], img.shape[2])
            qshape = warp.shape
            w = warp.reshape(Bq, -1, 2) + 0.5
            qx, qy = (w[..., 0], w[..., 1])
            fy = jnp.clip(jnp.floor(qy), 0.0, Hp - 2)
            fx = jnp.clip(jnp.floor(qx), 0.0, Wp - 2)
            ay = jnp.clip(qy - fy, 0.0, 1.0)[..., None]
            ax = jnp.clip(qx - fx, 0.0, 1.0)[..., None]
            y0 = fy.astype(jnp.int32)
            x0 = fx.astype(jnp.int32)
            bidx = jnp.arange(Bq)[:, None]
            tl = img[bidx, y0, x0]
            tr = img[bidx, y0, x0 + 1]
            bl = img[bidx, y0 + 1, x0]
            br = img[bidx, y0 + 1, x0 + 1]
            top = tl + ax * (tr - tl)
            bot = bl + ax * (br - bl)
            out = top + ay * (bot - top)
            return out.reshape(*qshape[:-1], C)
        key = jax.random.key(seed)
        ks = jax.random.split(key, 16)
        s = 0.02
        inp = {'x': jax.random.normal(ks[0], (B, H, W, NC), jnp.float32), 'w_q': jax.random.normal(ks[1], (NC, NC), jnp.float32) * s, 'b_q': jnp.zeros((NC,), jnp.float32), 'w_off0': jax.random.normal(ks[2], (KK, KK, NC // G, NC), jnp.float32) * s, 'b_off0': jnp.zeros((NC,), jnp.float32), 'ln_g': jnp.ones((NC,), jnp.float32), 'ln_b': jnp.zeros((NC,), jnp.float32), 'w_offp': jax.random.normal(ks[3], (GC, 2), jnp.float32) * s, 'w_k': jax.random.normal(ks[4], (NC, NC), jnp.float32) * s, 'b_k': jnp.zeros((NC,), jnp.float32), 'w_v': jax.random.normal(ks[5], (NC, NC), jnp.float32) * s, 'b_v': jnp.zeros((NC,), jnp.float32), 'w_out': jax.random.normal(ks[6], (NC, OUT_DIM), jnp.float32) * s, 'b_out': jnp.zeros((OUT_DIM,), jnp.float32), 'rpe': jax.random.normal(ks[7], (2 * H - 1, 2 * W - 1, HEADS), jnp.float32) * 0.01}
        return inp
    _L0_conv_all = _L0_conv_setup()
    _L0_conv_in = {k: v for k, v in _L0_conv_all.items() if k in ('w_q', 'b_q', 'w_off0', 'b_off0', 'ln_g', 'ln_b', 'w_offp', 'w_k', 'b_k', 'w_v', 'b_v', 'w_out', 'b_out', 'rpe', )}
    del _L0_conv_all

    def _L0_ffn_setup():
        import jax, jax.numpy as jnp
        import numpy as np
        NUM_EXPERTS = 4
        TOP_K = 2
        DIM = 384
        HID = 4 * DIM
        key = jax.random.key(seed)
        ks = jax.random.split(key, 5)
        B, S = (16, 2048)
        scale_in = 1.0 / np.sqrt(DIM)
        scale_hid = 1.0 / np.sqrt(HID)
        return {'x': jax.random.normal(ks[0], (B, S, DIM), dtype=jnp.float32), 'gate_w': jax.random.normal(ks[1], (DIM, NUM_EXPERTS), dtype=jnp.float32) * scale_in, 'gate_b': jnp.zeros((NUM_EXPERTS,), dtype=jnp.float32), 'w1': jax.random.normal(ks[2], (NUM_EXPERTS, DIM, HID), dtype=jnp.float32) * scale_in, 'b1': jnp.zeros((NUM_EXPERTS, HID), dtype=jnp.float32), 'w2': jax.random.normal(ks[3], (NUM_EXPERTS, HID, DIM), dtype=jnp.float32) * scale_hid, 'b2': jnp.zeros((NUM_EXPERTS, DIM), dtype=jnp.float32)}
    _L0_ffn_all = _L0_ffn_setup()
    _L0_ffn_in = {k: v for k, v in _L0_ffn_all.items() if k in ('gate_w', 'gate_b', 'w1', 'b1', 'w2', 'b2', )}
    del _L0_ffn_all

    return {
        "x": x,
        "L0_conv_w_q": _L0_conv_in["w_q"],
        "L0_conv_b_q": _L0_conv_in["b_q"],
        "L0_conv_w_off0": _L0_conv_in["w_off0"],
        "L0_conv_b_off0": _L0_conv_in["b_off0"],
        "L0_conv_ln_g": _L0_conv_in["ln_g"],
        "L0_conv_ln_b": _L0_conv_in["ln_b"],
        "L0_conv_w_offp": _L0_conv_in["w_offp"],
        "L0_conv_w_k": _L0_conv_in["w_k"],
        "L0_conv_b_k": _L0_conv_in["b_k"],
        "L0_conv_w_v": _L0_conv_in["w_v"],
        "L0_conv_b_v": _L0_conv_in["b_v"],
        "L0_conv_w_out": _L0_conv_in["w_out"],
        "L0_conv_b_out": _L0_conv_in["b_out"],
        "L0_conv_rpe": _L0_conv_in["rpe"],
        "L0_ffn_gate_w": _L0_ffn_in["gate_w"],
        "L0_ffn_gate_b": _L0_ffn_in["gate_b"],
        "L0_ffn_w1": _L0_ffn_in["w1"],
        "L0_ffn_b1": _L0_ffn_in["b1"],
        "L0_ffn_w2": _L0_ffn_in["w2"],
        "L0_ffn_b2": _L0_ffn_in["b2"],
    }

def reference(x, L0_conv_w_q, L0_conv_b_q, L0_conv_w_off0, L0_conv_b_off0, L0_conv_ln_g, L0_conv_ln_b, L0_conv_w_offp, L0_conv_w_k, L0_conv_b_k, L0_conv_w_v, L0_conv_b_v, L0_conv_w_out, L0_conv_b_out, L0_conv_rpe, L0_ffn_gate_w, L0_ffn_gate_b, L0_ffn_w1, L0_ffn_b1, L0_ffn_w2, L0_ffn_b2):
    import jax
    import jax.numpy as jnp
    def _L0_conv_ref(x, w_q, b_q, w_off0, b_off0, ln_g, ln_b, w_offp, w_k, b_k, w_v, b_v, w_out, b_out, rpe):
        import jax, jax.numpy as jnp
        import numpy as np
        from jax import lax
        B, H, W = (4, 32, 32)
        NC, HEADS, HC, G = (384, 6, 64, 6)
        GC = NC // G
        GH = HEADS // G
        KK = 3
        OUT_DIM = 384

        def _bilinear_sample(image, warp):
            Bq, C = (image.shape[0], image.shape[-1])
            img = jnp.pad(image, ((0, 0), (1, 1), (1, 1), (0, 0)))
            Hp, Wp = (img.shape[1], img.shape[2])
            qshape = warp.shape
            w = warp.reshape(Bq, -1, 2) + 0.5
            qx, qy = (w[..., 0], w[..., 1])
            fy = jnp.clip(jnp.floor(qy), 0.0, Hp - 2)
            fx = jnp.clip(jnp.floor(qx), 0.0, Wp - 2)
            ay = jnp.clip(qy - fy, 0.0, 1.0)[..., None]
            ax = jnp.clip(qx - fx, 0.0, 1.0)[..., None]
            y0 = fy.astype(jnp.int32)
            x0 = fx.astype(jnp.int32)
            bidx = jnp.arange(Bq)[:, None]
            tl = img[bidx, y0, x0]
            tr = img[bidx, y0, x0 + 1]
            bl = img[bidx, y0 + 1, x0]
            br = img[bidx, y0 + 1, x0 + 1]
            top = tl + ax * (tr - tl)
            bot = bl + ax * (br - bl)
            out = top + ay * (bot - top)
            return out.reshape(*qshape[:-1], C)
        Bq, Hq, Wq, _ = x.shape
        n = Hq * Wq
        scale = HC ** (-0.5)
        q = jnp.einsum('bhwc,cd->bhwd', x, w_q) + b_q
        o = lax.conv_general_dilated(q, w_off0, (1, 1), 'SAME', dimension_numbers=('NHWC', 'HWIO', 'NHWC'), feature_group_count=G) + b_off0
        mu = o.mean(-1, keepdims=True)
        var = ((o - mu) ** 2).mean(-1, keepdims=True)
        o = (o - mu) * lax.rsqrt(var + 0.001) * ln_g + ln_b
        o = jax.nn.gelu(o, approximate=False)
        o = o.reshape(Bq, Hq, Wq, G, GC).transpose(0, 3, 1, 2, 4).reshape(Bq * G, Hq, Wq, GC)
        offset = jnp.einsum('bhwc,ct->bhwt', o, w_offp)
        offset = jnp.tanh(offset) * jnp.array([Hq / 2.0, Wq / 2.0], x.dtype)
        yy, xx = jnp.meshgrid(jnp.arange(Hq), jnp.arange(Wq), indexing='ij')
        ref = jnp.stack([xx, yy], -1).astype(x.dtype)
        pos = offset + ref
        xg = x.reshape(Bq, Hq, Wq, G, GC).transpose(0, 3, 1, 2, 4).reshape(Bq * G, Hq, Wq, GC)
        xs = _bilinear_sample(xg, pos)
        xs = xs.reshape(Bq, G, n, GC).transpose(0, 2, 1, 3).reshape(Bq, n, NC)
        k = (xs @ w_k + b_k).reshape(Bq, n, HEADS, HC)
        v = (xs @ w_v + b_v).reshape(Bq, n, HEADS, HC)
        qh = q.reshape(Bq, n, HEADS, HC)
        attn = jnp.einsum('bmhc,bnhc->bhmn', qh, k) * scale
        disp = (ref.reshape(1, n, 1, 2) - pos.reshape(Bq * G, 1, n, 2)) * 0.5
        rpe_g = rpe.reshape(2 * Hq - 1, 2 * Wq - 1, G, GH).transpose(2, 0, 1, 3)
        rpe_img = jnp.broadcast_to(rpe_g[None], (Bq, G, 2 * Hq - 1, 2 * Wq - 1, GH))
        rpe_img = rpe_img.reshape(Bq * G, 2 * Hq - 1, 2 * Wq - 1, GH)
        bias = _bilinear_sample(rpe_img, disp)
        bias = bias.reshape(Bq, G, n, n, GH).transpose(0, 1, 4, 2, 3).reshape(Bq, HEADS, n, n)
        attn = jax.nn.softmax(attn + bias, axis=-1)
        out = jnp.einsum('bhmn,bnhc->bmhc', attn, v).reshape(Bq, Hq, Wq, NC)
        return out @ w_out + b_out

    def _L0_ffn_ref(x, gate_w, gate_b, w1, b1, w2, b2):
        import jax, jax.numpy as jnp
        import numpy as np
        NUM_EXPERTS = 4
        TOP_K = 2
        DIM = 384
        HID = 4 * DIM
        scores = jnp.einsum('bsd,de->bse', x, gate_w) + gate_b
        probs = jax.nn.softmax(scores, axis=-1)
        topk_vals, topk_idx = jax.lax.top_k(probs, TOP_K)
        mask = jnp.sum(jax.nn.one_hot(topk_idx, NUM_EXPERTS, dtype=probs.dtype), axis=-2)
        masked = probs * mask
        masked = masked / (jnp.sum(masked, axis=-1, keepdims=True) + 1e-09)
        h = jax.nn.gelu(jnp.einsum('bsd,edh->ebsh', x, w1) + b1[:, None, None, :], approximate=False)
        y = jnp.einsum('ebsh,ehd->ebsd', h, w2) + b2[:, None, None, :]
        out = jnp.einsum('bse,ebsd->bsd', masked, y)
        return out

    def _gn(v, G=32, eps=1e-5):
        B_, H_, W_, C_ = v.shape
        g = v.reshape(B_, H_, W_, G, C_ // G)
        m = jnp.mean(g, axis=(1, 2, 4), keepdims=True)
        s = jnp.var(g, axis=(1, 2, 4), keepdims=True)
        return ((g - m) / jnp.sqrt(s + eps)).reshape(v.shape)

    def _ln_c(v, eps=1e-6):
        m = jnp.mean(v, axis=-1, keepdims=True)
        s = jnp.var(v, axis=-1, keepdims=True)
        return (v - m) / jnp.sqrt(s + eps)

    def _ln_t(v, eps=1e-5):
        m = jnp.mean(v, axis=-1, keepdims=True)
        s = jnp.var(v, axis=-1, keepdims=True)
        return (v - m) / jnp.sqrt(s + eps)

    def _to_tokens(v):
        B_, H_, W_, C_ = v.shape
        return v.reshape(B_, H_ * W_, C_)
    def _from_tokens(t, like):
        return t.reshape(like.shape)

    x = x + _L0_conv_ref(_ln_c(x), L0_conv_w_q, L0_conv_b_q, L0_conv_w_off0, L0_conv_b_off0, L0_conv_ln_g, L0_conv_ln_b, L0_conv_w_offp, L0_conv_w_k, L0_conv_b_k, L0_conv_w_v, L0_conv_b_v, L0_conv_w_out, L0_conv_b_out, L0_conv_rpe)
    t = _to_tokens(x)
    t = t + _L0_ffn_ref(_ln_t(t), L0_ffn_gate_w, L0_ffn_gate_b, L0_ffn_w1, L0_ffn_b1, L0_ffn_w2, L0_ffn_b2)
    x = _from_tokens(t, x)
    return x


_drawn_inputs = setup_inputs


def setup_inputs(seed=0):
    import zlib

    import numpy as np

    out = dict(_drawn_inputs(seed))
    spreads = {'L0_conv_b_q': (0.0, 0.528),
     'L0_conv_b_off0': (0.0, 0.519),
     'L0_conv_ln_g': (1.0, 0.6),
     'L0_conv_ln_b': (0.0, 0.8),
     'L0_conv_b_k': (0.0, 2.0),
     'L0_conv_b_v': (0.0, 0.1),
     'L0_conv_b_out': (0.0, 0.1),
     'L0_ffn_gate_b': (0.0, 0.1),
     'L0_ffn_b1': (0.0, 0.1),
     'L0_ffn_b2': (0.0, 0.1)}
    factors = {'L0_conv_w_q': 4.715,
     'L0_conv_w_off0': 5.11,
     'L0_conv_w_offp': 5.277,
     'L0_conv_w_k': 8.0,
     'L0_conv_w_v': 3.387,
     'L0_conv_rpe': 51.302}
    for name, (base, spread) in spreads.items():
        noise = np.random.default_rng([zlib.crc32(name.encode()), seed]).standard_normal(out[name].shape)
        drawn = base * np.exp(spread * noise) if base else spread * noise
        out[name] = jnp.asarray(drawn.astype(out[name].dtype))
    for name, factor in factors.items():
        out[name] = (out[name] * factor).astype(out[name].dtype)
    return out
```

```python
from contextlib import ExitStack

import numpy as np
import concourse.bass as bass
from concourse import mybir
from concourse.alu_op_type import AluOpType as ALU

ACT = mybir.ActivationFunctionType
AX = mybir.AxisListType
F32 = mybir.dt.float32
F32R = mybir.dt.float32r
I32 = mybir.dt.int32

P = 128
B, H, W, NC = 4, 32, 32, 384
CH = NC // P
G, GC = 6, 64
N = H * W
TI = N // P
HT = TI // 2
HN = N // 2
HROWS = H // 2
NT = B * TI
PAIRS = B * G // 2
E, HID = 4, 4 * NC
KH = HID // P
SCALE = GC ** -0.5
SLO, SN = 1 - (W - 1 + W // 2), W // 2 + 1 - (1 - (W - 1 + W // 2)) + 1
UN = SN + W
UW = W + 1
RY = (UN + SLO) // 2
QY, QX = H + 1, W + 2


def constants():
    up = np.zeros((RY, UN), np.float32)
    for y in range(1, RY + 1):
        for d, w in ((-1, 0.5), (0, 1.0), (1, 0.5)):
            if 2 * y + d - SLO < UN:
                up[y - 1, 2 * y + d - SLO] = w
    p = np.arange(P)
    cell = np.zeros((P, TI, 2), np.float32)
    for t in range(TI):
        cell[:, t, 0] = p % W
        cell[:, t, 1] = t * (P // W) + p // W
    base = np.zeros((P, 2, B * G), np.float32)
    base[:, 0] = np.arange(B * G) * (QY * QX * 2 * GC)
    base[:, 1] = (np.arange(B * G) % G) * (SN * UN * UW)
    return {"c_ident": np.eye(P, dtype=np.float32), "c_up": up, "c_cell": cell, "c_base": base}


def chunks(w):
    return w.rearrange("(c p) n -> p c n", p=P)


def rows(v, n):
    return bass.AP(tensor=v.tensor, offset=v.offset, ap=[[0, n], [1, v.shape[0]]])


def inner(ap, k):
    return bass.AP(tensor=ap.tensor, offset=ap.offset, ap=[*ap.ap, [0, k]])


class Count:

    def __init__(self):
        self.now = 0

    def up(self, by=1):
        self.now += by
        return by


def table(nc, sem, d):
    with ExitStack() as ctx:
        sb = lambda n, s, t=F32: ctx.enter_context(nc.sbuf_tensor(n, s, t))
        rpe = sb("tb_rpe", [RY, RY, G])
        up = sb("tb_up", [RY, UN])
        wide = sb("tb_wide", [RY, G, UN])
        full = sb("tb_full", [UN, G, UN])
        zero = sb("tb_zero", [P, 34 * 64])
        ps = ctx.enter_context(nc.psum_tensor("tb_ps", [UN, 2, 512], F32))
        loaded, cleared, halves, widened, product, copied, stored, zeroed = (
            sem("tb_" + x) for x in ("loaded", "cleared", "halves", "widened", "product", "copied", "stored", "zeroed"))
        block = ctx.enter_context(nc.Block())
        first = 2 - SLO

        @block.sync
        def _(sp):
            sp.dma_start(rpe[:, :, :], d["rpe"][0:RY, 0:RY, :]).then_inc(loaded, 16)
            sp.dma_start(up[:, :], d["c_up"]).then_inc(loaded, 16)
            quads = d["quads"].rearrange("n y x r c -> (n y) x (r c)")
            sp.wait_ge(zeroed, 1)
            nrow = B * G * QY
            z = zero[0:nrow // 8, 0:8 * 2 * GC].rearrange("p (a c) -> p a c", a=8)
            for x in (0, QX - 1):
                dst = bass.AP(tensor=quads.tensor, offset=x * 2 * GC,
                              ap=[[8 * QX * 2 * GC, nrow // 8], [QX * 2 * GC, 8], [1, 2 * GC]])
                sp.dma_start(dst, z).then_inc(stored, 16)
            z = zero[0:B * G, 0:W * GC].rearrange("p (a c) -> p a c", a=W)
            for off in (2 * GC, (QY - 1) * QX * 2 * GC + 2 * GC + GC):
                dst = bass.AP(tensor=quads.tensor, offset=off,
                              ap=[[QY * QX * 2 * GC, B * G], [2 * GC, W], [1, GC]])
                sp.dma_start(dst, z).then_inc(stored, 16)
            sp.wait_ge(copied, 1)
            for h in range(G):
                src = full[:, h, :]
                src = bass.AP(tensor=src.tensor, offset=src.offset, ap=[src.ap[0], [1, SN], [1, UW]])
                sp.dma_start(d["shifts"][h].rearrange("f u j -> u f j"), src).then_inc(stored, 16)
            sp.wait_ge(stored, 16 * (4 + G))

        @block.gpsimd
        def _(pool):
            pool.memset(zero[:, :], 0.0).then_inc(zeroed, 1)

        @block.vector
        def _(dve):
            dve.memset(wide[:, :, :], 0.0).then_inc(cleared, 1)
            dve.wait_ge(loaded, 32)
            dve.wait_ge(cleared, 1)
            r = rpe[:, :, :].rearrange("y x h -> y h x")
            dve.tensor_copy(wide[:, :, first::2], r[:, :, 0:RY - 1]).then_inc(widened, 1)
            dve.tensor_scalar(wide[:, :, first - 1:first], r[:, :, 0:1], 0.5, None, ALU.mult).then_inc(widened, 1)
            dve.tensor_tensor(wide[:, :, first + 1::2], r[:, :, 0:RY - 1], r[:, :, 1:RY], ALU.add).then_inc(halves, 1)
            dve.wait_ge(halves, 1)
            dve.tensor_scalar(wide[:, :, first + 1::2], wide[:, :, first + 1::2], 0.5, None, ALU.mult).then_inc(widened, 1)
            dve.wait_ge(product, 1)
            dve.tensor_copy(full[:, :, :].rearrange("p (a h) u -> p a (h u)", a=2), ps[:, :, 0:G // 2 * UN]).then_inc(copied, 1)

        @block.tensor
        def _(pe):
            pe.wait_ge(loaded, 32)
            pe.wait_ge(widened, 3)
            w = wide[:, :, :].rearrange("p (a h) u -> p a (h u)", a=2)
            for a in range(2):
                mm = pe.matmul(ps[:, a, 0:G // 2 * UN], up[:, :], w[:, a, :], start=True, stop=True)
            mm.then_inc(product, 1)


def mixer_q(nc, sem, d, keep):
    with ExitStack() as ctx:
        sb = lambda n, s, t=F32: ctx.enter_context(nc.sbuf_tensor(n, s, t))
        x_sb = sb("mq_x", [P, 2, HT, NC])
        stats = sb("mq_stats", [P, HT, 6])
        mv = sb("mq_mv", [P, HT, 2])
        var = sb("mq_var", [P, HT])
        half = sb("mq_half", [P, HT])
        rstd = sb("mq_rstd", [P, HT])
        xn = sb("mq_xn", [P, 2, HT, NC])
        wq = sb("mq_wq", [P, CH, NC])
        bq = sb("mq_bq", [P, CH])
        ident = sb("mq_ident", [P, P])
        xnT = sb("mq_xnT", [P, CH, HN])
        qT = sb("mq_qT", [P, 2, CH, HN])
        psT = ctx.enter_context(nc.psum_tensor("mq_psT", [P, CH, HN], F32))
        psQ = ctx.enter_context(nc.psum_tensor("mq_psQ", [P, CH, HN], F32))
        passed, half_set, var_ready, rstd_ready, weights, norm_steps, xn_ready, t_done, t_copied, q_done, q_copied, q_padded, pad_zero = (
            sem("mq_" + x) for x in ("passed", "half_set", "var_ready", "rstd_ready", "weights", "norm_steps", "xn_ready", "t_done", "t_copied", "q_done", "q_copied", "q_padded", "pad_zero"))
        x_in, quad_out, q_out = ([sem(f"mq_{x}{f}") for f in range(2)] for x in ("x_in", "quad_out", "q_out"))
        block = ctx.enter_context(nc.Block())
        x_v = d["x"].rearrange("b h w c -> (b h w) c").rearrange("(s t p) c -> s p t c", p=P, t=HT)
        q_v = d["q_scr"].rearrange("(b j) p (f n) -> b f p j n", j=CH, f=2)
        QD = 2 * HT * (P // W)

        @block.sync
        def _(sp):
            sp.dma_start(ident[:, :], d["c_ident"]).then_inc(weights, 16)
            sp.dma_start(wq[:, :, :], chunks(d["w_q"])).then_inc(weights, 16)
            sp.dma_start(bq[:, :], d["b_q"].rearrange("(c p) -> p c", p=P), allow_slow_non_contiguous=True).then_inc(weights, 16)
            sp.sem_inc(xn_ready, 2 * HT)
            with sp.Fori(0, B) as b:
                for f in range(2):
                    sp.wait_ge(xn_ready, b * 2 * HT + (f + 1) * HT)
                    sp.dma_start(x_sb[:, f], x_v[bass.ds(b * 2 + f, 1)].rearrange("s p t c -> (s p) t c")).then_inc(x_in[f], 16)
                for f in range(2):
                    for t in range(HT):
                        sp.wait_ge(xn_ready, b * 2 * HT + (2 + f) * HT + t + 1)
                        src = xn[:, f, t, :].rearrange("p (g c) -> p g c", g=G)
                        y = (f * HT + t) * (P // W)
                        for r in range(2):
                            for k in range(P // W):
                                dst = d["quads"][bass.ds(b * G, G), y + k + 1 - r:y + k + 2 - r, 1:W + 1, r, :]
                                sp.dma_start(dst.rearrange("g y x c -> (y x) g c"), src[k * W:k * W + W]).then_inc(quad_out[f], 16)
                    sp.wait_ge(q_copied, b * 2 * CH + f * CH + 2 * CH)
                    sp.dma_start(q_v[bass.ds(b, 1), f].rearrange("b p j n -> (b p) j n"), qT[:, f]).then_inc(q_out[f], 16)
            for f in range(2):
                sp.wait_ge(quad_out[f], (B + 1) * QD * 16)
                sp.wait_ge(q_out[f], (B + 1) * 16)

        @block.gpsimd
        def _(pool):
            pool.memset(keep["q_pad"][:, :, :, :, :], 0.0).then_inc(pad_zero, 1)
            pool.memset(half[:, :], -0.5).then_inc(half_set, 1)
            pool.wait_ge(half_set, 1)
            with pool.Fori(0, B) as b:
                for f in range(2):
                    pool.wait_ge(var_ready, b * 2 + f + 1)
                    pool.tensor_tensor(rstd[:, :], var[:, :], half[:, :], ALU.pow).then_inc(rstd_ready, 1)

        @block.vector
        def _(dve):
            K = 2 * 2 * HT
            dve.sem_inc(t_done, 2)
            for f in range(2):
                dve.sem_inc(quad_out[f], 16 * QD)
            dve.wait_ge(pad_zero, 1)

            def pad(b, f):
                for j in range(CH):
                    dve.wait_ge(q_copied, b * 2 * CH + f * CH + CH + j + 1)
                    dst = keep["q_pad"][:, j, bass.ds(b, 1), f * HROWS + 1:(f + 1) * HROWS + 1, 1:W + 1]
                    dve.tensor_copy(dst.rearrange("p b y x -> p (b y) x"), qT[:, f, j, :].rearrange("p (y x) -> p y x", x=W)).then_inc(q_padded, 1)

            with dve.Fori(0, B) as b:
                n = Count()
                for f in range(2):
                    dve.wait_ge(x_in[f], b * 16 + 16)
                    for t in range(HT):
                        dve.bn_stats(stats[:, t, :], x_sb[:, f, t, :]).then_inc(norm_steps, n.up())
                    dve.wait_ge(norm_steps, b * K + n.now)
                    dve.sem_inc(passed, 1)
                    for t in range(HT):
                        dve.bn_aggr(mv[:, t, :], stats[:, t, :]).then_inc(norm_steps, n.up())
                    dve.wait_ge(norm_steps, b * K + n.now)
                    dve.tensor_scalar(var[:, :], mv[:, :, 1], 1e-6, None, ALU.add).then_inc(var_ready, 1)
                    dve.wait_ge(rstd_ready, b * 2 + f + 1)
                    dve.wait_ge(quad_out[f], b * (16 * QD) + 16 * QD)
                    dve.wait_ge(t_done, b * 2 + f + 1)
                    for t in range(HT):
                        dve.tensor_scalar(xn[:, f, t, :], x_sb[:, f, t, :], mv[:, t, 0:1], rstd[:, t:t + 1],
                                          ALU.subtract, ALU.mult).then_inc(xn_ready, 1)
                    dve.wait_ge(xn_ready, b * 2 * HT + (3 + f) * HT)
                for f in range(2):
                    pad(b, f)
                assert n.now == K

        @block.tensor
        def _(pe):
            pe.wait_ge(weights, 48)
            pe.sem_inc(t_copied, 1)
            pe.sem_inc(q_copied, CH)
            with pe.Fori(0, B) as b:
                for f in range(2):
                    for t in range(HT):
                        pe.wait_ge(xn_ready, b * 2 * HT + (2 + f) * HT + t + 1)
                        if t == 0:
                            pe.wait_ge(t_copied, b * 2 + f + 1)
                        for j in range(CH):
                            mm = pe.transpose(psT[:, j, t * P:(t + 1) * P], xn[:, f, t, j * P:(j + 1) * P], ident[:, :])
                    mm.then_inc(t_done, 1)
                    pe.wait_ge(t_copied, b * 2 + f + 2)
                    for j in range(CH):
                        pe.wait_ge(q_copied, b * 2 * CH + f * CH + j + 1)
                        for c in range(CH):
                            mm = pe.matmul(psQ[:, j, :], wq[:, c, j * P:(j + 1) * P], xnT[:, c, :], start=c == 0, stop=c == CH - 1)
                        mm.then_inc(q_done, 1)

        @block.scalar
        def _(act):
            act.wait_ge(weights, 48)
            act.sem_inc(q_done, CH)
            act.sem_inc(q_padded, 2 * CH)
            for f in range(2):
                act.sem_inc(q_out[f], 16)
            with act.Fori(0, B) as b:
                for f in range(2):
                    act.wait_ge(t_done, b * 2 + f + 3)
                    act.wait_ge(q_done, b * 2 * CH + f * CH + CH)
                    act.activation(xnT[:, :, :], psT[:, :, :], ACT.Copy).then_inc(t_copied, 1)
                    act.wait_ge(q_out[f], b * 16 + 16)
                    act.wait_ge(q_padded, b * 2 * CH + f * CH + CH)
                    for j in range(CH):
                        act.wait_ge(q_done, b * 2 * CH + f * CH + CH + j + 1)
                        act.activation(qT[:, f, j, :], psQ[:, j, :], ACT.Identity, bias=bq[:, j:j + 1]).then_inc(q_copied, 1)


def offsets(nc, sem, d, keep):
    TAPS = 9
    with ExitStack() as ctx:
        sb = lambda n, s, t=F32: ctx.enter_context(nc.sbuf_tensor(n, s, t))
        wc = sb("of_wc", [P, TAPS, CH, P])
        bo = sb("of_bo", [P, CH])
        gain, shift = sb("of_gain", [P, NC]), sb("of_shift", [P, NC])
        woff = sb("of_woff", [P, GC, 2])
        ident = sb("of_ident", [P, P])
        cell, base = sb("of_cell", [P, TI, 2]), sb("of_base", [P, 2, B * G])
        oT = sb("of_oT", [P, CH, HN])
        on = sb("of_on", [P, 2, HT, NC])
        ge = sb("of_ge", [P, HT, NC])
        part = sb("of_part", [P, HT * G, GC])
        stats, mv = sb("of_stats", [P, HT, 6]), sb("of_mv", [P, HT, 2])
        var, half, rstd = sb("of_var", [P, HT]), sb("of_half", [P, HT]), sb("of_rstd", [P, HT])
        off, th = sb("of_off", [P, 2, G, HT]), sb("of_th", [P, 2, G, HT])
        pos = sb("of_pos", [P, 2, G, HT])
        v, fl, fr, co = (sb("of_" + x, [P, 2, 2, G, HT]) for x in ("v", "fl", "fr", "co"))
        whole = sb("of_whole", [P, 2, 2, G, HT], I32)
        flat = sb("of_flat", [P, 2, G, HT])
        ws, wb = sb("of_ws", [P, G, HT, 4]), sb("of_wb", [P, G, HT, 4])
        psC = ctx.enter_context(nc.psum_tensor("of_psC", [P, CH, HN], F32))
        psO = ctx.enter_context(nc.psum_tensor("of_psO", [P, HT, 512], F32))
        (weights, wc_zero, conv_done, oT_ready, back_done, steps, passed, half_set, var_ready, rstd_ready, normed, gelu_done,
         off_ready, tanh_done) = (sem("of_" + x) for x in (
             "weights", "wc_zero", "conv_done", "oT_ready", "back_done", "steps", "passed", "half_set", "var_ready", "rstd_ready",
             "normed", "gelu_done", "off_ready", "tanh_done"))
        block = ctx.enter_context(nc.Block())

        @block.sync
        def _(sp):
            sp.dma_start(ident[:, :], d["c_ident"]).then_inc(weights, 16)
            sp.dma_start(bo[:, :], d["b_off0"].rearrange("(c p) -> p c", p=P), allow_slow_non_contiguous=True).then_inc(weights, 16)
            sp.dma_start(gain[:, :], rows(d["ln_g"], P)).then_inc(weights, 16)
            sp.dma_start(shift[:, :], rows(d["ln_b"], P)).then_inc(weights, 16)
            sp.dma_start(woff[:, :, :].rearrange("p c k -> p (c k)"), rows(d["w_offp"].rearrange("c k -> (c k)"), P)).then_inc(weights, 16)
            sp.dma_start(cell[:, :, :], d["c_cell"]).then_inc(weights, 16)
            sp.dma_start(base[:, :, :], d["c_base"]).then_inc(weights, 16)
            sp.wait_ge(wc_zero, 1)
            w = d["w_off0"].rearrange("y x i (j g o) -> g i (y x) j o", g=2, o=GC)
            for g in range(2):
                for j in range(CH):
                    sp.dma_start(wc[g * GC:(g + 1) * GC, :, j, g * GC:(g + 1) * GC], w[g, :, :, j]).then_inc(weights, 16)
            sp.wait_ge(weights, 16 * (7 + 2 * CH))

        @block.gpsimd
        def _(pool):
            pool.memset(wc[:, :, :, :], 0.0).then_inc(wc_zero, 1)
            pool.memset(half[:, :], -0.5).then_inc(half_set, 1)
            pool.wait_ge(half_set, 1)
            with pool.Fori(0, B) as b:
                for f in range(2):
                    pool.wait_ge(var_ready, b * 2 + f + 1)
                    pool.tensor_tensor(rstd[:, :], var[:, :], half[:, :], ALU.pow).then_inc(rstd_ready, 1)

        @block.tensor
        def _(pe):
            pe.wait_ge(weights, 16 * (7 + 2 * CH))
            pe.sem_inc(oT_ready, CH)
            pe.sem_inc(normed, 1)
            with pe.Fori(0, B) as b:
                for f in range(2):
                    for j in range(CH):
                        pe.wait_ge(oT_ready, b * 2 * CH + f * CH + j + 1)
                        for tap in range(TAPS):
                            y, x = f * HROWS + tap // 3, tap % 3
                            q = keep["q_pad"][:, j, bass.ds(b, 1), y:y + HROWS, x:x + W].rearrange("p b y x -> p (b y) x")
                            mm = pe.matmul(psC[:, j, :].rearrange("p (y x) -> p y x", x=W), wc[:, tap, j, :], q,
                                           start=tap == 0, stop=tap == TAPS - 1)
                        mm.then_inc(conv_done, 1)
                    pe.wait_ge(normed, b * 2 + f + 1)
                    for j in range(CH):
                        pe.wait_ge(oT_ready, b * 2 * CH + f * CH + CH + j + 1)
                        for t in range(HT):
                            mm = pe.transpose(psO[:, t, j * P:(j + 1) * P], oT[:, j, t * P:(t + 1) * P], ident[:, :])
                    mm.then_inc(back_done, 1)

        @block.scalar
        def _(act):
            act.wait_ge(weights, 16 * (7 + 2 * CH))
            act.sem_inc(back_done, 1)
            act.sem_inc(off_ready, 2)
            with act.Fori(0, B) as b:
                for f in range(2):
                    act.wait_ge(back_done, b * 2 + f + 1)
                    for j in range(CH):
                        act.wait_ge(conv_done, b * 2 * CH + f * CH + j + 1)
                        act.activation(oT[:, j, :], psC[:, j, :], ACT.Identity, bias=bo[:, j:j + 1]).then_inc(oT_ready, 1)
                    act.wait_ge(steps, b * OFF_K + (f * OFF_K // 2 + OFF_GELU))
                    act.wait_ge(off_ready, b * 4 + f * 2 + 2)
                    act.activation(ge[:, :, :], on[:, f], ACT.Gelu).then_inc(gelu_done, 1)
                    act.wait_ge(off_ready, b * 4 + f * 2 + 4)
                    act.activation(th[:, :, :, :], off[:, :, :, :], ACT.Tanh).then_inc(tanh_done, 1)

        @block.vector
        def _(dve):
            dve.wait_ge(weights, 16 * (7 + 2 * CH))
            with dve.Fori(0, B) as b:
                n = Count()

                def after():
                    dve.wait_ge(steps, b * OFF_K + n.now)

                for f in range(2):
                    dve.wait_ge(back_done, b * 2 + f + 2)
                    for t in range(HT):
                        dve.bn_stats(stats[:, t, :], psO[:, t, 0:NC]).then_inc(steps, n.up())
                    after()
                    dve.sem_inc(passed, 1)
                    for t in range(HT):
                        dve.bn_aggr(mv[:, t, :], stats[:, t, :]).then_inc(steps, n.up())
                    after()
                    dve.tensor_scalar(var[:, :], mv[:, :, 1], 1e-3, None, ALU.add).then_inc(var_ready, 1)
                    dve.wait_ge(rstd_ready, b * 2 + f + 1)
                    for t in range(HT):
                        dve.tensor_scalar(on[:, f, t, :], psO[:, t, 0:NC], mv[:, t, 0:1], rstd[:, t:t + 1],
                                          ALU.subtract, ALU.mult).then_inc(steps, n.up())
                    after()
                    dve.sem_inc(normed, 1)
                    g3 = gain[:, :].rearrange("p (o c) -> p o c", o=1).broadcast_to([P, HT, NC])
                    s3 = shift[:, :].rearrange("p (o c) -> p o c", o=1).broadcast_to([P, HT, NC])
                    dve.tensor_tensor(on[:, f], on[:, f], g3, ALU.mult).then_inc(steps, n.up())
                    after()
                    dve.tensor_tensor(on[:, f], on[:, f], s3, ALU.add).then_inc(steps, n.up())
                    if f == 0:
                        assert n.now == OFF_GELU
                    dve.wait_ge(gelu_done, b * 2 + f + 1)
                    ge3 = ge[:, :, :].rearrange("p t (g c) -> p (t g) c", g=G)
                    for k in range(2):
                        w3 = woff[:, :, k].rearrange("p (o c) -> p o c", o=1).broadcast_to([P, HT * G, GC])
                        dve.tensor_tensor(part[:, :, :], ge3, w3, ALU.mult).then_inc(steps, n.up())
                        after()
                        dve.tensor_reduce(off[:, k].rearrange("p g t -> p t g"), part[:, :, :].rearrange("p (t g) c -> p t g c", g=G),
                                          AX.X, ALU.add).then_inc(off_ready, 1)
                        dve.wait_ge(off_ready, b * 4 + (f * 2 + k + 3))
                    dve.wait_ge(tanh_done, b * 2 + f + 1)
                    for k in range(2):
                        c3 = cell[:, f * HT:(f + 1) * HT, k].rearrange("p (o t) -> p o t", o=1).broadcast_to([P, G, HT])
                        dve.scalar_tensor_tensor(pos[:, k], th[:, k], float(W // 2), c3, ALU.mult, ALU.add).then_inc(steps, n.up())
                    after()
                    dve.tensor_scalar(v[:, 0], pos[:, :, :, :], 0.5, None, ALU.add).then_inc(steps, n.up())
                    dve.tensor_scalar(v[:, 1], pos[:, :, :, :], -1.0, float(1 - SLO), ALU.mult, ALU.add).then_inc(steps, n.up())
                    after()
                    dve.tensor_copy(whole[:, :, :, :, :], v[:, :, :, :, :]).then_inc(steps, n.up())
                    after()
                    dve.tensor_copy(fl[:, :, :, :, :], whole[:, :, :, :, :]).then_inc(steps, n.up())
                    after()
                    dve.tensor_tensor(co[:, :, :, :, :], fl[:, :, :, :, :], v[:, :, :, :, :], ALU.is_gt).then_inc(steps, n.up())
                    after()
                    dve.tensor_tensor(fl[:, :, :, :, :], fl[:, :, :, :, :], co[:, :, :, :, :], ALU.subtract).then_inc(steps, n.up())
                    after()
                    dve.tensor_scalar(fl[:, 0], fl[:, 0], 0.0, float(H), ALU.max, ALU.min).then_inc(steps, n.up())
                    dve.tensor_scalar(fl[:, 1], fl[:, 1], 0.0, float(SN - 1), ALU.max, ALU.min).then_inc(steps, n.up())
                    after()
                    dve.tensor_tensor(fr[:, :, :, :, :], v[:, :, :, :, :], fl[:, :, :, :, :], ALU.subtract).then_inc(steps, n.up())
                    dve.scalar_tensor_tensor(flat[:, 0], fl[:, 0, 1], float(QX), fl[:, 0, 0], ALU.mult, ALU.add).then_inc(steps, n.up())
                    dve.scalar_tensor_tensor(flat[:, 1], fl[:, 1, 0], float(UN), fl[:, 1, 1], ALU.mult, ALU.add).then_inc(steps, n.up())
                    after()
                    dve.tensor_scalar(fr[:, :, :, :, :], fr[:, :, :, :, :], 0.0, 1.0, ALU.max, ALU.min).then_inc(steps, n.up())
                    for k, pitch in ((0, 2 * GC), (1, UW)):
                        dve.tensor_scalar(flat[:, k], flat[:, k], float(pitch), None, ALU.mult).then_inc(steps, n.up())
                    after()
                    dve.tensor_scalar(co[:, :, :, :, :], fr[:, :, :, :, :], -1.0, 1.0, ALU.mult, ALU.add).then_inc(steps, n.up())
                    for k in range(2):
                        dst = (keep["quad_at"], keep["shift_at"])[k][:, bass.ds(b, 1), :, f * HT:(f + 1) * HT].rearrange("p b g t -> p (b g) t")
                        b3 = inner(base[:, k, bass.ds(b * G, G)], HT)
                        dve.tensor_tensor(dst, flat[:, k], b3, ALU.add).then_inc(steps, n.up())
                    after()
                    for q, (x, y) in enumerate(((co, co), (co, fr), (fr, co), (fr, fr))):
                        dve.tensor_tensor(ws[:, :, :, q], x[:, 0, 0], y[:, 0, 1], ALU.mult).then_inc(steps, n.up())
                    for q, x in enumerate((co[:, 1, 0], fr[:, 1, 0], co[:, 1, 1], fr[:, 1, 1])):
                        dve.tensor_copy(wb[:, :, :, q], x).then_inc(steps, n.up())
                    after()
                    for w, name in ((ws, "quad_w"), (wb, "shift_w")):
                        dst = keep[name][:, bass.ds(b, 1), :, f * HT:(f + 1) * HT, :].rearrange("p b g t k -> p (b g) (t k)")
                        dve.tensor_copy(dst, w[:, :, :, :].rearrange("p g t k -> p g (t k)")).then_inc(steps, n.up())
                    after()
                assert n.now == OFF_K, n.now


OFF_GELU = 3 * HT + 2
OFF_K = 2 * 45


def keys(nc, sem, d, keep):
    QUAD = 4 * GC
    with ExitStack() as ctx:
        sb = lambda n, s, t=F32: ctx.enter_context(nc.sbuf_tensor(n, s, t))
        at = sb("ke_at", [P, 2, G, HT], I32)
        quad = sb("ke_quad", [P, HT, G, QUAD])
        prod = sb("ke_prod", [P, G, 4, GC])
        side = sb("ke_side", [P, G, 2, GC])
        xs = sb("ke_xs", [P, HT, G, GC])
        xsT = sb("ke_xsT", [P, CH, HN])
        wk, wv = sb("ke_wk", [P, CH, NC]), sb("ke_wv", [P, CH, NC])
        bk, bks, bv = sb("ke_bk", [P, CH]), sb("ke_bks", [P, CH]), sb("ke_bv", [P, NC])
        ident = sb("ke_ident", [P, P])
        kT, vt = sb("ke_kT", [P, 2, CH, HN]), sb("ke_vt", [P, 2, HT, NC])
        psT = ctx.enter_context(nc.psum_tensor("ke_psT", [P, CH, HN], F32))
        psK = ctx.enter_context(nc.psum_tensor("ke_psK", [P, CH, HN], F32))
        psV = ctx.enter_context(nc.psum_tensor("ke_psV", [P, 2, 512], F32))
        (weights, bks_ready, passed, staged, prod_done, side_done, xs_ready, t_done, t_copied, k_done, k_ready, v_done, v_ready) = (
            sem("ke_" + x) for x in ("weights", "bks_ready", "passed", "staged", "prod_done", "side_done", "xs_ready", "t_done",
                                     "t_copied", "k_done", "k_ready", "v_done", "v_ready"))
        gathered = [sem(f"ke_gathered{t}") for t in range(HT)]
        k_out, v_out = ([sem(f"ke_{x}{f}") for f in range(2)] for x in ("k_out", "v_out"))
        block = ctx.enter_context(nc.Block())
        flat = d["quads"].rearrange("n y x r c -> (n y x r c)").rearrange("(n o) -> n o", o=1)
        k_v = d["k_scr"].rearrange("(b j) p (f n) -> b f p j n", j=CH, f=2)

        @block.sync
        def _(sp):
            sp.dma_start(ident[:, :], d["c_ident"]).then_inc(weights, 16)
            sp.dma_start(wk[:, :, :], chunks(d["w_k"])).then_inc(weights, 16)
            sp.dma_start(wv[:, :, :], chunks(d["w_v"])).then_inc(weights, 16)
            sp.dma_start(bk[:, :], d["b_k"].rearrange("(c p) -> p c", p=P), allow_slow_non_contiguous=True).then_inc(weights, 16)
            sp.dma_start(bv[:, :], rows(d["b_v"], P)).then_inc(weights, 16)
            with sp.Fori(0, B) as b:
                for f in range(2):
                    sp.wait_ge(k_ready, b * 2 * CH + f * CH + 2 * CH)
                    sp.dma_start(k_v[bass.ds(b, 1), f].rearrange("b p j n -> (b p) j n"), kT[:, f]).then_inc(k_out[f], 16)
                    for t in range(HT):
                        sp.wait_ge(v_ready, b * 2 * HT + f * HT + t + 3)
                        dst = d["v_scr"][bass.ds(b * CH, CH), f * HT + t].rearrange("j p c -> p j c")
                        sp.dma_start(dst, vt[:, f, t, :].rearrange("p (j c) -> p j c", j=CH)).then_inc(v_out[f], 16)
            for f in range(2):
                sp.wait_ge(k_out[f], (B + 1) * 16)
                sp.wait_ge(v_out[f], (B + 1) * 16 * HT)

        @block.gpsimd
        def _(pool):
            pool.sem_inc(xs_ready, 2 * HT)
            with pool.Fori(0, B) as b:
                for f in range(2):
                    pool.wait_ge(xs_ready, b * 2 * HT + (f + 1) * HT)
                    pool.sem_inc(passed, 1)
                    src = keep["quad_at"][:, bass.ds(b, 1), :, f * HT:(f + 1) * HT].rearrange("p b g t -> p (b g) t")
                    pool.tensor_copy(at[:, f], src).then_inc(staged, 1)
                    pool.wait_ge(staged, b * 2 + f + 1)
                    for t in range(HT):
                        pool.wait_ge(xs_ready, b * 2 * HT + (f + 1) * HT + t + 1)
                        pool.sem_inc(passed, 1)
                        for g in range(G):
                            pool.indirect_dma_start(out=quad[:, t, g, :], out_offset=None, in_=flat,
                                                    in_offset=bass.IndirectOffsetOnAxis(ap=at[:, f, g, t:t + 1], axis=0)
                                                    ).then_inc(gathered[t], 16)

        @block.vector
        def _(dve):
            dve.wait_ge(weights, 16 * 5)
            dve.sem_inc(t_done, 1)
            for f in range(2):
                dve.sem_inc(v_out[f], 16 * HT)
            with dve.Fori(0, B) as b:
                for f in range(2):
                    for t in range(HT):
                        s = b * 2 * HT + (f * HT + t)
                        dve.wait_ge(gathered[t], b * (2 * G * 16) + (f + 1) * G * 16)
                        w = keep["quad_w"][:, bass.ds(b, 1), :, f * HT + t, :].rearrange("p b g q -> p (b g) q")
                        dve.tensor_tensor(prod[:, :, :, :], quad[:, t].rearrange("p g (q c) -> p g q c", c=GC), inner(w, GC), ALU.mult).then_inc(prod_done, 1)
                        dve.wait_ge(prod_done, s + 1)
                        dve.tensor_tensor(side[:, :, :, :], prod[:, :, 0:2], prod[:, :, 2:4], ALU.add).then_inc(side_done, 1)
                        dve.wait_ge(side_done, s + 1)
                        if t == 0:
                            dve.wait_ge(t_done, b * 2 + f + 1)
                        dve.tensor_tensor(xs[:, t], side[:, :, 0], side[:, :, 1], ALU.add).then_inc(xs_ready, 1)
                        dve.wait_ge(xs_ready, s + (2 * HT + 1))
                    dve.wait_ge(v_out[f], b * (16 * HT) + 16 * HT)
                    for t in range(HT):
                        dve.wait_ge(v_done, b * 2 * HT + (f * HT + t + 1))
                        dve.tensor_tensor(vt[:, f, t, :], psV[:, t % 2, 0:NC], bv[:, :], ALU.add).then_inc(v_ready, 1)

        @block.tensor
        def _(pe):
            pe.wait_ge(weights, 16 * 5)
            pe.sem_inc(t_copied, 1)
            pe.sem_inc(k_ready, CH)
            pe.sem_inc(v_ready, 2)
            with pe.Fori(0, B) as b:
                for f in range(2):
                    for t in range(HT):
                        if t == 0:
                            pe.wait_ge(t_copied, b * 2 + f + 1)
                        pe.wait_ge(xs_ready, b * 2 * HT + (f * HT + t + 1 + 2 * HT))
                        for j in range(CH):
                            mm = pe.transpose(psT[:, j, t * P:(t + 1) * P], xs[:, t, 2 * j:2 * j + 2, :].rearrange("p g c -> p (g c)"), ident[:, :])
                    mm.then_inc(t_done, 1)
                    pe.wait_ge(t_copied, b * 2 + f + 2)
                    for t in range(HT):
                        pe.wait_ge(v_ready, b * 2 * HT + (f * HT + t + 1))
                        for c in range(CH):
                            mm = pe.matmul(psV[:, t % 2, 0:NC], xsT[:, c, t * P:(t + 1) * P], wv[:, c, :], start=c == 0, stop=c == CH - 1)
                        mm.then_inc(v_done, 1)
                    for j in range(CH):
                        pe.wait_ge(k_ready, b * 2 * CH + (f * CH + j + 1))
                        for c in range(CH):
                            mm = pe.matmul(psK[:, j, :], wk[:, c, j * P:(j + 1) * P], xsT[:, c, :], start=c == 0, stop=c == CH - 1)
                        mm.then_inc(k_done, 1)

        @block.scalar
        def _(act):
            act.wait_ge(weights, 16 * 5)
            act.activation(bks[:, :], bk[:, :], ACT.Copy, scale=SCALE).then_inc(bks_ready, 1)
            act.wait_ge(bks_ready, 1)
            act.sem_inc(k_done, CH)
            for f in range(2):
                act.sem_inc(k_out[f], 16)
            with act.Fori(0, B) as b:
                for f in range(2):
                    act.wait_ge(t_done, b * 2 + f + 2)
                    act.wait_ge(k_done, b * 2 * CH + (f + 1) * CH)
                    act.activation(xsT[:, :, :], psT[:, :, :], ACT.Copy).then_inc(t_copied, 1)
                    act.wait_ge(k_out[f], b * 16 + 16)
                    for j in range(CH):
                        act.wait_ge(k_done, b * 2 * CH + ((f + 1) * CH + j + 1))
                        act.activation(kT[:, f, j, :], psK[:, j, :], ACT.Identity, bias=bks[:, j:j + 1], scale=SCALE).then_inc(k_ready, 1)


def attend(nc, sem, d, keep):
    WB = 4
    ODD = GC + 1
    with ExitStack() as ctx:
        sb = lambda n, s, t=F32: ctx.enter_context(nc.sbuf_tensor(n, s, t))
        at = sb("at_at", [P, 2, TI], I32)
        wt = sb("at_wt", [P, 2, TI, 4])
        window = sb("at_window", [P, WB, UW, UW])
        rowx = sb("at_rowx", [P, 2, UW, W])
        logit = sb("at_logit", [P, 2, TI, N])
        most = sb("at_most", [P, 2, N])
        mx = sb("at_mx", [P, TI])
        diag = sb("at_diag", [P, TI, P])
        neg = sb("at_neg", [P, 2, N])
        ident, minus, ones = sb("at_ident", [P, P]), sb("at_minus", [P, P]), sb("at_ones", [P, P])
        qT, kT = sb("at_qT", [P, N]), sb("at_kT", [P, N])
        val = sb("at_val", [P, 2, TI, ODD])
        rcp = sb("at_rcp", [P, 2, TI // 2])
        psS = ctx.enter_context(nc.psum_tensor("at_psS", [P, 2, N], F32))
        psM = ctx.enter_context(nc.psum_tensor("at_psM", [P, N], F32))
        psO = ctx.enter_context(nc.psum_tensor("at_psO", [P, 2, 512], F32))
        (passed, consts, ones_set, minus_set, staged, x0_done, x_done, y0_done, logit_done, most_done, qk_done, turned, mx_ready,
         diag_ready, spread, neg_ready, sub_done, p_done, pv_done, rcp_ready, o_done, qk_in) = (sem("at_" + x) for x in (
             "passed", "consts", "ones_set", "minus_set", "staged", "x0_done", "x_done", "y0_done", "logit_done", "most_done",
             "qk_done", "turned", "mx_ready", "diag_ready", "spread", "neg_ready", "sub_done", "p_done", "pv_done", "rcp_ready",
             "o_done", "qk_in"))
        gathered = [sem(f"at_gathered{w}") for w in range(WB)]
        v_in = [sem(f"at_v_in{h}") for h in range(2)]
        block = ctx.enter_context(nc.Block())
        flat = d["shifts"].rearrange("h f u j -> (h f u j)").rearrange("(n o) -> n o", o=1)
        o_v = psO[:, :, 0:TI // 2 * ODD].rearrange("p a (m c) -> p a m c", c=ODD)

        def every_pair(eng, pair):
            pair(0, True)
            with eng.Fori(1, PAIRS) as i:
                pair(i, False)

        @block.sync
        def _(sp):
            sp.dma_start(ident[:, :], d["c_ident"]).then_inc(consts, 16)

            def pair(i, first):
                if not first:
                    sp.wait_ge(qk_done, i * 2 * TI)
                sp.dma_start(qT[:, :], d["q_scr"][bass.ds(i, 1)].rearrange("a p n -> (a p) n")).then_inc(qk_in, 16)
                sp.dma_start(kT[:, :], d["k_scr"][bass.ds(i, 1)].rearrange("a p n -> (a p) n")).then_inc(qk_in, 16)
                if first:
                    sp.wait_ge(ones_set, 2)
                for h in range(2):
                    if not first:
                        sp.wait_ge(pv_done, i * 2 * TI - (1 - h) * TI)
                    src = d["v_scr"][bass.ds(i, 1), :, :, h * GC:(h + 1) * GC].rearrange("a t p c -> (a p) t c")
                    sp.dma_start(val[:, h, :, 0:GC], src).then_inc(v_in[h], 16)

            every_pair(sp, pair)

        @block.gpsimd
        def _(pool):
            pool.memset(ones[:, :], 1.0).then_inc(ones_set, 1)
            pool.memset(val[:, :, :, GC:ODD], 1.0).then_inc(ones_set, 1)

            def subtract(s, h, k):
                if k == 0:
                    pool.wait_ge(neg_ready, s + 1)
                pool.tensor_tensor(logit[:, h, k, :], logit[:, h, k, :], neg[:, h, :], ALU.add).then_inc(sub_done, 1)

            def pair(i, first):
                for h in range(2):
                    s = i * 2 + h
                    if not first:
                        pool.wait_ge(logit_done, s * TI - TI)
                    pool.sem_inc(passed, 1)
                    pool.tensor_copy(at[:, h, :], keep["shift_at"][:, :, :, :].rearrange("p b g t -> p (b g) t")[:, bass.ds(s, 1), :].rearrange("p s t -> p (s t)")).then_inc(staged, 1)
                    pool.tensor_copy(wt[:, h].rearrange("p t k -> p (t k)"), keep["shift_w"][:, :, :, :, :].rearrange("p b g t k -> p (b g) (t k)")[:, bass.ds(s, 1), :].rearrange("p s t -> p (s t)")).then_inc(staged, 1)
                    pool.wait_ge(staged, s * 2 + 2)
                    pool.sem_inc(passed, 1)
                    for t in range(TI):
                        if not first or h or t >= WB:
                            pool.wait_ge(x_done, s * TI + (t - WB + 1))
                            pool.sem_inc(passed, 1)
                        pool.indirect_dma_start(out=window[:, t % WB].rearrange("p u j -> p (u j)"), out_offset=None, in_=flat,
                                                in_offset=bass.IndirectOffsetOnAxis(ap=at[:, h, t:t + 1], axis=0)
                                                ).then_inc(gathered[t % WB], 16)
                        if t < 5 and not first:
                            subtract(s - 2, h, t + 3)
                        if t >= 5 and (not first or h):
                            subtract(s - 1, 1 - h, t - 5)

            every_pair(pool, pair)
            last = 2 * PAIRS - 1
            for k in range(3, TI):
                subtract(last - 1, 0, k)
            for k in range(TI):
                subtract(last, 1, k)

        @block.scalar
        def _(act):
            def spread_max(s, h):
                act.wait_ge(spread, s + 1)
                act.activation(neg[:, h, :], psM[:, :], ACT.Copy).then_inc(neg_ready, 1)

            def exps(s, h, k):
                act.wait_ge(sub_done, s * TI + (k + 1))
                act.activation(logit[:, h, k, :], logit[:, h, k, :], ACT.Exp).then_inc(p_done, 1)

            def pair(i, first):
                for h in range(2):
                    s = i * 2 + h
                    act.wait_ge(staged, s * 2 + 2)
                    for t in range(TI):
                        act.wait_ge(gathered[t % WB], s * (TI // WB * 16) + (t // WB + 1) * 16)
                        if not first or h or t >= 2:
                            act.wait_ge(logit_done, s * TI + (t - 1))
                        act.activation(rowx[:, t % 2], window[:, t % WB, :, 0:W], ACT.Copy, scale=wt[:, h, t, 0:1]).then_inc(x0_done, 1)
                        if t == 2 and (not first or h):
                            spread_max(s - 1, 1 - h)
                        if t < 4 and not first:
                            exps(s - 2, h, t + 4)
                        if t >= 4 and (not first or h):
                            exps(s - 1, 1 - h, t - 4)

            every_pair(act, pair)
            last = 2 * PAIRS - 1
            spread_max(last, 1)
            for k in range(4, TI):
                exps(last - 1, 0, k)
            for k in range(TI):
                exps(last, 1, k)

        @block.tensor
        def _(pe):
            pe.wait_ge(consts, 16)
            pe.wait_ge(ones_set, 2)

            def turn_max(s, h, first):
                pe.wait_ge(most_done, s * (TI - 1) + (TI - 1))
                if not first:
                    pe.wait_ge(neg_ready, s)
                for k in range(TI):
                    mm = pe.transpose(psM[:, k * P:(k + 1) * P], most[:, h, k * P:(k + 1) * P], ident[:, :])
                mm.then_inc(turned, 1)

            def spread_max(s):
                pe.wait_ge(diag_ready, s + 1)
                dg = diag[:, :, :].rearrange("p t q -> p (t q)")
                for a in range(2):
                    mm = pe.matmul(psM[:, a * 512:(a + 1) * 512], ones[:, :], dg[:, a * 512:(a + 1) * 512], start=True, stop=True)
                mm.then_inc(spread, 1)

            def values(s, h, k, i, first):
                pe.wait_ge(p_done, s * TI + (k + 1))
                if k == 0:
                    pe.wait_ge(v_in[h], i * 16 + 16)
                    if not first:
                        pe.wait_ge(o_done, s)
                for m in range(TI):
                    mm = pe.matmul(o_v[:, m // 4, m % 4, :], logit[:, h, k, m * P:(m + 1) * P], val[:, h, k, :],
                                   start=k == 0 and m % 4 == 0, stop=k == TI - 1, skip_group_check=True)
                mm.then_inc(pv_done, 1)

            def pair(i, first):
                for h in range(2):
                    s = i * 2 + h
                    if h == 0:
                        pe.wait_ge(qk_in, i * 32 + 32)
                    for t in range(TI):
                        if not first or h or t >= 2:
                            pe.wait_ge(y0_done, s * TI + (t - 1))
                        for a in range(2):
                            mm = pe.matmul(psS[:, t % 2, a * 512:(a + 1) * 512], kT[h * GC:(h + 1) * GC, t * P:(t + 1) * P],
                                           qT[h * GC:(h + 1) * GC, a * 512:(a + 1) * 512], start=True, stop=True)
                        mm.then_inc(qk_done, 1)
                        if not first or h:
                            if t == 1:
                                turn_max(s - 1, 1 - h, first)
                            if t == 2:
                                spread_max(s - 1)
                        if t < 6 and not first:
                            values(s - 2, h, t + 2, i - 1, False)
                        if t >= 6 and (not first or h):
                            values(s - 1, 1 - h, t - 6, i if h else i - 1, first)

            every_pair(pe, pair)
            last = 2 * PAIRS - 1
            turn_max(last, 1, False)
            spread_max(last)
            for k in range(2, TI):
                values(last - 1, 0, k, PAIRS - 1, False)
            for k in range(TI):
                values(last, 1, k, PAIRS - 1, False)

        @block.vector
        def _(dve):
            dve.wait_ge(consts, 16)
            dve.tensor_scalar(minus[:, :], ident[:, :], -1.0, None, ALU.mult).then_inc(minus_set, 1)
            dve.wait_ge(minus_set, 1)

            def reduce_max(s):
                dve.wait_ge(turned, s + 1)
                dve.tensor_reduce(mx[:, :], psM[:, :].rearrange("p (t q) -> p t q", t=TI), AX.X, ALU.max).then_inc(mx_ready, 1)
                dve.wait_ge(mx_ready, s + 1)
                m3 = minus[:, :].rearrange("p (o q) -> p o q", o=1).broadcast_to([P, TI, P])
                dve.tensor_tensor(diag[:, :, :], m3, inner(mx[:, :], P), ALU.mult).then_inc(diag_ready, 1)

            def output(s, h, i):
                dve.wait_ge(pv_done, s * TI + TI)
                dve.reciprocal(rcp[:, :, :], o_v[:, :, :, GC]).then_inc(rcp_ready, 1)
                dve.wait_ge(rcp_ready, s + 1)
                dst = keep["o"][:, bass.ds(i, 1), :, h * GC:(h + 1) * GC].rearrange("p i (a m) c -> p (i a) m c", a=2)
                dve.tensor_tensor(dst, o_v[:, :, :, 0:GC], inner(rcp[:, :, :], GC), ALU.mult).then_inc(o_done, 1)

            def pair(i, first):
                for h in range(2):
                    s = i * 2 + h
                    for t in range(TI):
                        n = s * TI + t
                        dve.wait_ge(x0_done, n + 1)
                        dve.scalar_tensor_tensor(rowx[:, t % 2], window[:, t % WB, :, 1:UW], wt[:, h, t, 1:2], rowx[:, t % 2],
                                                 ALU.mult, ALU.add).then_inc(x_done, 1)
                        dve.wait_ge(x_done, n + 1)
                        dve.wait_ge(qk_done, n + 1)
                        if not first:
                            dve.wait_ge(pv_done, n - (2 * TI - 1))
                        flat_row = rowx[:, t % 2].rearrange("p u j -> p (u j)")
                        lt = logit[:, h, t, :]
                        dve.scalar_tensor_tensor(lt, flat_row[:, 0:N], wt[:, h, t, 2:3], psS[:, t % 2, :],
                                                 ALU.mult, ALU.add).then_inc(y0_done, 1)
                        dve.wait_ge(y0_done, n + 1)
                        dve.scalar_tensor_tensor(lt, flat_row[:, W:W + N], wt[:, h, t, 3:4], lt, ALU.mult, ALU.add).then_inc(logit_done, 1)
                        dve.wait_ge(logit_done, n + 1)
                        if t >= 1:
                            if t >= 2:
                                dve.wait_ge(most_done, s * (TI - 1) + (t - 1))
                            so_far = logit[:, h, 0, :] if t == 1 else most[:, h, :]
                            dve.tensor_tensor(most[:, h, :], so_far, lt, ALU.max).then_inc(most_done, 1)
                        if t == 0 and (not first or h):
                            reduce_max(s - 1)
                        if t == 5 and not first:
                            output(s - 2, h, i - 1)

            every_pair(dve, pair)
            last = 2 * PAIRS - 1
            reduce_max(last)
            output(last - 1, 0, PAIRS - 1)
            output(last, 1, PAIRS - 1)


def join(nc, sem, d, keep):
    with ExitStack() as ctx:
        sb = lambda n, s, t=F32: ctx.enter_context(nc.sbuf_tensor(n, s, t))
        ident, wo, wg = sb("jo_ident", [P, P]), sb("jo_wo", [P, CH, NC]), sb("jo_wg", [P, CH, E])
        bo, bg = sb("jo_bo", [P, NC]), sb("jo_bg", [P, E])
        x = sb("jo_x", [P, 2, HT, NC])
        o = sb("jo_o", [P, CH, HT, P])
        oT = sb("jo_oT", [P, CH, HN])
        stats, mv = sb("jo_stats", [P, HT, 6]), sb("jo_mv", [P, HT, 2])
        var, half, rstd = sb("jo_var", [P, HT]), sb("jo_half", [P, HT]), sb("jo_rstd", [P, HT])
        tn = sb("jo_tn", [P, HT, NC])
        tnT = sb("jo_tnT", [P, CH, HN])
        parts = sb("jo_parts", [P, 2, 2, CH, HN], F32R)
        score, prob, top = sb("jo_score", [P, HT, E]), sb("jo_prob", [P, HT, E]), sb("jo_top", [P, HT, E])
        one = sb("jo_one", [P, HT])
        above = sb("jo_above", [P, HT, E, E])
        psT = ctx.enter_context(nc.psum_tensor("jo_psT", [P, CH, HN], F32))
        psY = ctx.enter_context(nc.psum_tensor("jo_psY", [P, 2, 512], F32))
        psG = ctx.enter_context(nc.psum_tensor("jo_psG", [P, HT, E], F32))
        (weights, passed, copying, half_set, above_set, o_ready, o_turned, oT_ready, y_done, t_ready, steps, var_ready, rstd_ready, tn_ready,
         tn_turned, tnT_ready, parts_ready, gate_done, score_ready, exp_done) = (sem("jo_" + n) for n in (
             "weights", "passed", "copying", "half_set", "above_set", "o_ready", "o_turned", "oT_ready", "y_done", "t_ready", "steps", "var_ready",
             "rstd_ready", "tn_ready", "tn_turned", "tnT_ready", "parts_ready", "gate_done", "score_ready", "exp_done"))
        x_in, parts_out = ([sem(f"jo_{n}{f}") for f in range(2)] for n in ("x_in", "parts_out"))
        block = ctx.enter_context(nc.Block())
        x_v = d["x"].rearrange("b h w c -> (b h w) c").rearrange("(s t p) c -> s p t c", p=P, t=HT)
        LOADS = 5 * 16

        @block.sync
        def _(sp):
            sp.dma_start(ident[:, :], d["c_ident"]).then_inc(weights, 16)
            sp.dma_start(wo[:, :, :], chunks(d["w_out"])).then_inc(weights, 16)
            sp.dma_start(wg[:, :, :], chunks(d["gate_w"])).then_inc(weights, 16)
            sp.dma_start(bo[:, :], rows(d["b_out"], P)).then_inc(weights, 16)
            sp.dma_start(bg[:, :], rows(d["gate_b"], P)).then_inc(weights, 16)
            sp.sem_inc(t_ready, 2 * HT)
            with sp.Fori(0, B) as b:
                for f in range(2):
                    sp.wait_ge(t_ready, b * 2 * HT + ((f + 1) * HT + 2))
                    sp.dma_start(x[:, f], x_v[bass.ds(b * 2 + f, 1)].rearrange("s p t c -> (s p) t c")).then_inc(x_in[f], 16)
                for f in range(2):
                    sp.wait_ge(parts_ready, b * 4 + 2 * f + 4)
                    sp.dma_start(d["t_scr"][bass.ds(b * 2 + f, 1)].rearrange("s p k c n -> (s p) k c n"), parts[:, f].bitcast(F32)).then_inc(parts_out[f], 16)
            for f in range(2):
                sp.wait_ge(parts_out[f], (B + 1) * 16)

        @block.gpsimd
        def _(pool):
            pool.memset(half[:, :], -0.5).then_inc(half_set, 1)
            pool.memset(above[:, :, :, :], 0.0).then_inc(above_set, 1)
            pool.wait_ge(half_set, 1)
            with pool.Fori(0, B) as b:
                for f in range(2):
                    pool.wait_ge(var_ready, b * 2 + f + 1)
                    pool.tensor_tensor(rstd[:, :], var[:, :], half[:, :], ALU.pow).then_inc(rstd_ready, 1)

        @block.scalar
        def _(act):
            act.wait_ge(weights, LOADS)
            act.sem_inc(o_turned, 1)
            act.sem_inc(y_done, HT)
            act.sem_inc(parts_ready, 2)
            act.sem_inc(gate_done, HT)
            with act.Fori(0, B) as b:
                for f in range(2):
                    s = b * 2 + f
                    act.wait_ge(o_turned, s + 1)
                    act.sem_inc(copying, 1)
                    act.activation(o[:, :, :, :], keep["o"][:, bass.ds(b * CH, CH), f * HT:(f + 1) * HT, :], ACT.Copy).then_inc(o_ready, 1)
                    act.wait_ge(o_turned, s + 2)
                    act.wait_ge(y_done, s * HT + HT)
                    act.activation(oT[:, :, :], psT[:, :, :], ACT.Copy).then_inc(oT_ready, 1)
                    act.wait_ge(tn_turned, s + 1)
                    act.wait_ge(parts_ready, s * 2 + 2)
                    act.wait_ge(gate_done, s * HT + HT)
                    act.activation(tnT[:, :, :], psT[:, :, :], ACT.Copy).then_inc(tnT_ready, 1)
                    act.wait_ge(score_ready, s + 2)
                    act.activation(prob[:, :, :], score[:, :, :], ACT.Exp).then_inc(exp_done, 1)

        @block.tensor
        def _(pe):
            pe.wait_ge(weights, LOADS)
            pe.sem_inc(tnT_ready, 1)
            pe.sem_inc(t_ready, 2)
            pe.sem_inc(score_ready, 1)
            with pe.Fori(0, B) as b:
                for f in range(2):
                    s = b * 2 + f
                    pe.wait_ge(o_ready, s + 1)
                    pe.wait_ge(tnT_ready, s + 1)
                    for j in range(CH):
                        for t in range(HT):
                            mm = pe.transpose(psT[:, j, t * P:(t + 1) * P], o[:, j, t, :], ident[:, :])
                    mm.then_inc(o_turned, 1)
                    pe.wait_ge(oT_ready, s + 1)
                    for t in range(HT):
                        pe.wait_ge(t_ready, s * HT + (2 * HT + 1 + t))
                        for c in range(CH):
                            mm = pe.matmul(psY[:, t % 2, 0:NC], oT[:, c, t * P:(t + 1) * P], wo[:, c, :], start=c == 0, stop=c == CH - 1)
                        mm.then_inc(y_done, 1)
                    for t in range(HT):
                        pe.wait_ge(tn_ready, s * HT + (t + 1))
                        for j in range(CH):
                            mm = pe.transpose(psT[:, j, t * P:(t + 1) * P], tn[:, t, j * P:(j + 1) * P], ident[:, :])
                    mm.then_inc(tn_turned, 1)
                    pe.wait_ge(tnT_ready, s + 2)
                    pe.wait_ge(score_ready, s + 1)
                    for t in range(HT):
                        for c in range(CH):
                            mm = pe.matmul(psG[:, t, :], tnT[:, c, t * P:(t + 1) * P], wg[:, c, :], start=c == 0, stop=c == CH - 1)
                        mm.then_inc(gate_done, 1)

        @block.vector
        def _(dve):
            dve.wait_ge(weights, LOADS)
            dve.wait_ge(above_set, 1)
            for f in range(2):
                dve.sem_inc(parts_out[f], 16)
            with dve.Fori(0, B) as b:
                n = Count()

                def after():
                    dve.wait_ge(steps, b * JOIN_K + n.now)

                for f in range(2):
                    s = b * 2 + f
                    tile = lambda t: keep["acc"][:, bass.ds(b * TI + (f * HT + t), 1), :].rearrange("p o c -> p (o c)")
                    dve.wait_ge(x_in[f], b * 16 + 16)
                    b3 = bo[:, :].rearrange("p (o c) -> p o c", o=1).broadcast_to([P, HT, NC])
                    dve.tensor_tensor(x[:, f], x[:, f], b3, ALU.add).then_inc(steps, n.up())
                    after()
                    for t in range(HT):
                        dve.wait_ge(y_done, s * HT + (HT + t + 1))
                        dve.tensor_tensor(tile(t), psY[:, t % 2, 0:NC], x[:, f, t, :], ALU.add).then_inc(t_ready, 1)
                    dve.wait_ge(t_ready, s * HT + (3 * HT + 2))
                    dve.sem_inc(passed, 1)
                    for t in range(HT):
                        dve.bn_stats(stats[:, t, :], tile(t)).then_inc(steps, n.up())
                    after()
                    dve.sem_inc(passed, 1)
                    for t in range(HT):
                        dve.bn_aggr(mv[:, t, :], stats[:, t, :]).then_inc(steps, n.up())
                    after()
                    dve.tensor_scalar(var[:, :], mv[:, :, 1], 1e-5, None, ALU.add).then_inc(var_ready, 1)
                    dve.wait_ge(rstd_ready, s + 1)
                    for t in range(HT):
                        dve.tensor_scalar(tn[:, t, :], tile(t), mv[:, t, 0:1], rstd[:, t:t + 1], ALU.subtract, ALU.mult).then_inc(tn_ready, 1)
                    dve.wait_ge(tn_ready, s * HT + HT)
                    dve.wait_ge(tnT_ready, s + 2)
                    dve.wait_ge(parts_out[f], b * 16 + 16)
                    dve.tensor_copy(parts[:, f, 0], tnT[:, :, :]).then_inc(parts_ready, 1)
                    dve.wait_ge(parts_ready, s * 2 + 3)
                    dve.tensor_tensor(parts[:, f, 1], tnT[:, :, :], parts[:, f, 0].bitcast(F32), ALU.subtract).then_inc(parts_ready, 1)
                    dve.wait_ge(gate_done, s * HT + 2 * HT)
                    g3 = bg[:, :].rearrange("p (o e) -> p o e", o=1).broadcast_to([P, HT, E])
                    dve.tensor_tensor(score[:, :, :], psG[:, :, :], g3, ALU.add).then_inc(steps, n.up())
                    after()
                    dve.tensor_reduce(one[:, :], score[:, :, :], AX.X, ALU.max).then_inc(steps, n.up())
                    after()
                    dve.tensor_tensor(score[:, :, :], score[:, :, :], inner(one[:, :], E), ALU.subtract).then_inc(score_ready, 1)
                    dve.wait_ge(exp_done, s + 1)
                    dve.tensor_reduce(one[:, :], prob[:, :, :], AX.X, ALU.add).then_inc(steps, n.up())
                    after()
                    dve.reciprocal(one[:, :], one[:, :]).then_inc(steps, n.up())
                    after()
                    dve.tensor_tensor(prob[:, :, :], prob[:, :, :], inner(one[:, :], E), ALU.mult).then_inc(steps, n.up())
                    after()
                    for e in range(E):
                        for lo, hi, op in ((0, e, ALU.is_ge), (e + 1, E, ALU.is_gt)):
                            if lo < hi:
                                dve.tensor_tensor(above[:, :, e, lo:hi], prob[:, :, lo:hi], prob[:, :, e:e + 1].broadcast_to([P, HT, hi - lo]), op
                                                  ).then_inc(steps, n.up())
                    after()
                    dve.tensor_reduce(top[:, :, :], above[:, :, :, :], AX.X, ALU.add).then_inc(steps, n.up())
                    after()
                    dve.scalar_tensor_tensor(top[:, :, :], top[:, :, :], 1.5, prob[:, :, :], ALU.is_lt, ALU.mult).then_inc(steps, n.up())
                    after()
                    dve.tensor_reduce(one[:, :], top[:, :, :], AX.X, ALU.add).then_inc(steps, n.up())
                    after()
                    dve.tensor_scalar(one[:, :], one[:, :], 1e-9, None, ALU.add).then_inc(steps, n.up())
                    after()
                    dve.reciprocal(one[:, :], one[:, :]).then_inc(steps, n.up())
                    after()
                    dst = keep["gates"][:, bass.ds(b * TI + f * HT, HT), :]
                    dve.tensor_tensor(dst, top[:, :, :], inner(one[:, :], E), ALU.mult).then_inc(steps, n.up())
                    after()
                assert n.now == JOIN_K, n.now


JOIN_K = 2 * 26


def experts(nc, sem, d, keep):
    TILES = E * B * 2
    R = 4
    with ExitStack() as ctx:
        sb = lambda n, s, t=F32: ctx.enter_context(nc.sbuf_tensor(n, s, t))
        raw1, raw2 = sb("ex_raw1", [P, R, CH, P]), sb("ex_raw2", [P, R, NC])
        w1, w2 = sb("ex_w1", [P, R, 2, CH, P], F32R), sb("ex_w2", [P, R, 2, NC], F32R)
        xT = sb("ex_xT", [P, 2, 2, CH, HN], F32R)
        h, hp = sb("ex_h", [P, R, HN]), sb("ex_hp", [P, R, 2, HN], F32R)
        b1, b2 = sb("ex_b1", [P, E, KH]), sb("ex_b2", [P, E, NC])
        bias = sb("ex_bias", [P, 2, KH])
        y = sb("ex_y", [P, 2, NC])
        psH = ctx.enter_context(nc.psum_tensor("ex_psH", [P, R, HN], F32))
        psY = ctx.enter_context(nc.psum_tensor("ex_psY", [P, HT, 512], F32))
        (weights, passed, bias_ready, split_done, h_done, gelu_done, hp_ready, y_done, y_read, added, out_done) = (sem("ex_" + n) for n in (
            "weights", "passed", "bias_ready", "split_done", "h_done", "gelu_done", "hp_ready", "y_done", "y_read", "added", "out_done"))
        raw_in = [sem(f"ex_raw_in{r}") for r in range(R)]
        x_in = [sem(f"ex_x_in{u}") for u in range(2)]
        block = ctx.enter_context(nc.Block())
        LOADS = 2 * 16
        PASSES = ((0, 0), (0, 1), (1, 0))

        def every_two(eng, two):
            two(0, True)
            with eng.Fori(1, TILES // 2) as i:
                two(i, False)

        @block.sync
        def _(sp):
            sp.dma_start(b1[:, :, :], d["b1"].rearrange("e (k p) -> p e k", p=P), allow_slow_non_contiguous=True).then_inc(weights, 16)
            sp.dma_start(b2[:, :, :].rearrange("p e c -> p (e c)"), rows(d["b2"].rearrange("e c -> (e c)"), P)).then_inc(weights, 16)
            w1_v = d["w1"].rearrange("e (c p) (k n) -> k e p c n", p=P, n=P)
            w2_v = d["w2"].rearrange("e (k p) c -> (e k) p c", p=P)

            def two(i, first):
                for u in range(2):
                    n = i * 2 + u
                    e = i // (B)
                    if not first:
                        sp.wait_ge(h_done, n * KH - KH)
                    sp.dma_start(xT[:, u].bitcast(F32), d["t_scr"][bass.ds((i % B) * 2 + u, 1)].rearrange("s p k c n -> (s p) k c n")).then_inc(x_in[u], 16)
                    for k in range(KH):
                        if not first or u or k >= R:
                            sp.wait_ge(split_done, n * 4 * KH + 4 * (k - R + 1))
                        sp.dma_start(raw1[:, k % R], w1_v[k, bass.ds(e, 1)].rearrange("e p c n -> (e p) c n")).then_inc(raw_in[k % R], 16)
                        sp.dma_start(raw2[:, k % R], w2_v[bass.ds(e * KH + k, 1)].rearrange("e p c -> (e p) c")).then_inc(raw_in[k % R], 16)

            every_two(sp, two)
            sp.wait_ge(added, TILES * HT)
            sp.dma_start(d["out"].rearrange("b h w c -> (b h w) c").rearrange("(t p) c -> p t c", p=P), keep["acc"][:, :, :]).then_inc(out_done, 16)
            sp.wait_ge(out_done, 16)

        @block.scalar
        def _(act):
            act.wait_ge(weights, LOADS)

            def two(i, first):
                for u in range(2):
                    n = i * 2 + u
                    if not first:
                        act.wait_ge(hp_ready, n * 2 * KH - 2 * KH)
                    act.sem_inc(passed, 1)
                    act.activation(bias[:, u, :], b1[:, bass.ds(i // B, 1), :].rearrange("p e k -> p (e k)"), ACT.Copy).then_inc(bias_ready, 1)
                    act.wait_ge(bias_ready, n + 1)
                    for k in range(KH):
                        act.wait_ge(h_done, n * KH + (k + 1))
                        if not first or u or k >= R:
                            act.wait_ge(hp_ready, n * 2 * KH + 2 * (k - R + 1))
                        act.activation(h[:, k % R, :], psH[:, k % R, :], ACT.Gelu, bias=bias[:, u, k:k + 1]).then_inc(gelu_done, 1)

            every_two(act, two)

        @block.tensor
        def _(pe):
            def down(n, k, first):
                pe.wait_ge(hp_ready, n * 2 * KH + 2 * (k + 1))
                if k == 0 and not first:
                    pe.wait_ge(y_read, n * HT)
                for m in range(HT):
                    for a, c in PASSES:
                        mm = pe.matmul(psY[:, m, 0:NC], hp[:, k % R, a, m * P:(m + 1) * P], w2[:, k % R, c, :],
                                       start=k == 0 and (a, c) == (0, 0), stop=k == KH - 1 and a == 1)
                mm.then_inc(y_done, 1)

            def two(i, first):
                for u in range(2):
                    n = i * 2 + u
                    pe.wait_ge(x_in[u], i * 16 + 16)
                    for k in range(KH):
                        pe.wait_ge(split_done, n * 4 * KH + 4 * (k + 1))
                        if not first or u or k >= R:
                            pe.wait_ge(gelu_done, n * KH + (k - R + 1))
                        for c in range(CH):
                            for a, z in PASSES:
                                mm = pe.matmul(psH[:, k % R, :], w1[:, k % R, a, c, :], xT[:, u, z, c, :],
                                               start=c == 0 and (a, z) == (0, 0), stop=c == CH - 1 and a == 1)
                        mm.then_inc(h_done, 1)
                        if k >= 2:
                            down(n, k - 2, first and not u)
                        elif not first or u:
                            down(n - 1, KH - 2 + k, False)

            every_two(pe, two)
            for k in (KH - 2, KH - 1):
                down(TILES - 1, k, False)

        @block.vector
        def _(dve):
            dve.wait_ge(weights, LOADS)

            def split(n, k, early):
                dve.wait_ge(raw_in[k % R], n * (KH // R * 32) + (k // R + 1) * 32)
                if not early:
                    dve.wait_ge(y_done, n * KH + (k - R + 1))
                s = n * 4 * KH + 4 * k
                dve.tensor_copy(w1[:, k % R, 0], raw1[:, k % R]).then_inc(split_done, 1)
                dve.tensor_copy(w2[:, k % R, 0], raw2[:, k % R]).then_inc(split_done, 1)
                dve.wait_ge(split_done, s + 1)
                dve.tensor_tensor(w1[:, k % R, 1], raw1[:, k % R], w1[:, k % R, 0].bitcast(F32), ALU.subtract).then_inc(split_done, 1)
                dve.wait_ge(split_done, s + 2)
                dve.tensor_tensor(w2[:, k % R, 1], raw2[:, k % R], w2[:, k % R, 0].bitcast(F32), ALU.subtract).then_inc(split_done, 1)

            def hidden(n, k, early):
                dve.wait_ge(gelu_done, n * KH + (k + 1))
                if not early:
                    dve.wait_ge(y_done, n * KH + (k - R + 1))
                dve.tensor_copy(hp[:, k % R, 0, :], h[:, k % R, :]).then_inc(hp_ready, 1)
                dve.wait_ge(hp_ready, n * 2 * KH + (2 * k + 1))
                dve.tensor_tensor(hp[:, k % R, 1, :], h[:, k % R, :], hp[:, k % R, 0, :].bitcast(F32), ALU.subtract).then_inc(hp_ready, 1)

            def add(n, i, u):
                dve.wait_ge(y_done, n * KH + KH)
                for m in range(HT):
                    if m >= 2:
                        dve.wait_ge(added, n * HT + (m - 1))
                    b_e = b2[:, bass.ds(i // B, 1), :].rearrange("p e c -> p (e c)")
                    dve.tensor_tensor(y[:, m % 2, :], psY[:, m, 0:NC], b_e, ALU.add).then_inc(y_read, 1)
                    dve.wait_ge(y_read, n * HT + (m + 1))
                    row = (i % B) * 2 * HT + (u * HT + m)
                    acc = keep["acc"][:, bass.ds(row, 1), :].rearrange("p o c -> p (o c)")
                    gate = keep["gates"][:, :, :].rearrange("p t e -> p (t e)")[:, bass.ds(row * E + i // B, 1)]
                    dve.scalar_tensor_tensor(acc, y[:, m % 2, :], gate, acc, ALU.mult, ALU.add).then_inc(added, 1)
                dve.wait_ge(added, n * HT + HT)

            def two(i, first):
                for u in range(2):
                    n = i * 2 + u
                    for k in range(KH):
                        early = first and not u and k < R
                        split(n, k, early)
                        if k >= 2:
                            hidden(n, k - 2, first and not u and k - 2 < R)
                        elif not first or u:
                            hidden(n - 1, KH - 2 + k, False)
                        if k == 3 and (not first or u):
                            add(n - 1, i if u else i - 1, 1 - u)

            every_two(dve, two)
            for k in (KH - 2, KH - 1):
                hidden(TILES - 1, k, False)
            add(TILES - 1, TILES // 2 - 1, 1)


NAMES = {"x": "x", "w_q": "L0_conv_w_q", "b_q": "L0_conv_b_q", "w_off0": "L0_conv_w_off0", "b_off0": "L0_conv_b_off0",
         "ln_g": "L0_conv_ln_g", "ln_b": "L0_conv_ln_b", "w_offp": "L0_conv_w_offp", "w_k": "L0_conv_w_k",
         "b_k": "L0_conv_b_k", "w_v": "L0_conv_w_v", "b_v": "L0_conv_b_v", "w_out": "L0_conv_w_out",
         "b_out": "L0_conv_b_out", "rpe": "L0_conv_rpe", "gate_w": "L0_ffn_gate_w", "gate_b": "L0_ffn_gate_b",
         "w1": "L0_ffn_w1", "b1": "L0_ffn_b1", "w2": "L0_ffn_w2", "b2": "L0_ffn_b2"}


def build(nc, d, out):
    def scratch(name, shape, dt=F32):
        d[name] = nc.dram_tensor("s_" + name, shape, dt, kind="Internal").ap()
    scratch("shifts", (G, SN, UN, UW))
    scratch("quads", (B * G, QY, QX, 2, GC))
    scratch("q_scr", (PAIRS, P, N))
    scratch("k_scr", (PAIRS, P, N))
    scratch("v_scr", (PAIRS, TI, P, P))
    scratch("t_scr", (B * 2, P, 2, CH, HN))
    d["out"] = out
    with ExitStack() as ctx:
        sem = lambda name: ctx.enter_context(nc.semaphore(name))
        table(nc, sem, d)
        keep = {}
        with ExitStack() as held:
            for name, shape, dt in (("quad_at", [P, B, G, TI], I32), ("shift_at", [P, B, G, TI], I32),
                                    ("quad_w", [P, B, G, TI, 4], F32), ("shift_w", [P, B, G, TI, 4], F32)):
                keep[name] = held.enter_context(nc.sbuf_tensor(name, shape, dt))
            with nc.sbuf_tensor("q_pad", [P, CH, B, H + 2, W + 2], F32) as keep["q_pad"]:
                mixer_q(nc, sem, d, keep)
                offsets(nc, sem, d, keep)
            keys(nc, sem, d, keep)
            keep["o"] = held.enter_context(nc.sbuf_tensor("o_all", [P, PAIRS, TI, P], F32))
            attend(nc, sem, d, keep)
            keep["acc"] = held.enter_context(nc.sbuf_tensor("acc", [P, NT, NC], F32))
            keep["gates"] = held.enter_context(nc.sbuf_tensor("gates", [P, NT, E], F32))
            join(nc, sem, d, keep)
            experts(nc, sem, d, keep)


def kernel(**inputs):
    import concourse.bacc as bacc
    from concourse.bass_utils import run_bass_kernel_spmd

    nc = bacc.Bacc("TRN2", target_bir_lowering=False, num_devices=1)
    arrays = {"in_" + n: np.ascontiguousarray(inputs[long]) for n, long in NAMES.items()}
    arrays |= {"in_" + n: a for n, a in constants().items()}
    d = {n[3:]: nc.dram_tensor(n, a.shape, mybir.dt.from_np(a.dtype), kind="ExternalInput").ap() for n, a in arrays.items()}
    out = nc.dram_tensor("out_0", (B, H, W, NC), F32, kind="ExternalOutput").ap()
    build(nc, d, out)
    r = run_bass_kernel_spmd(nc, [arrays], core_ids=[0])
    return r.results[0]["out_0"]
```

```python
from contextlib import ExitStack

import numpy as np
import concourse.bass as bass
from concourse import mybir
from concourse.alu_op_type import AluOpType as ALU

ACT = mybir.ActivationFunctionType
AX = mybir.AxisListType
F32 = mybir.dt.float32
F32R = mybir.dt.float32r
I32 = mybir.dt.int32

P = 128
B, H, W, NC = 4, 32, 32, 384
CH = NC // P
G, GC = 6, 64
N = H * W
TI = N // P
HT = TI // 2
HN = N // 2
HROWS = H // 2
NT = B * TI
PAIRS = B * G // 2
E, HID = 4, 4 * NC
KH = HID // P
SCALE = GC ** -0.5
SLO, SN = 1 - (W - 1 + W // 2), W // 2 + 1 - (1 - (W - 1 + W // 2)) + 1
UN = SN + W
UW = W + 1
RY = (UN + SLO) // 2
TN = 512
QUEUE = NT * P + TN
TILES = (2 * NT * P + E * (TN - 1)) // TN
SLOTS_T = TILES
QY, QX = H + 1, W + 2


def constants():
    up = np.zeros((RY, UN), np.float32)
    for y in range(1, RY + 1):
        for d, w in ((-1, 0.5), (0, 1.0), (1, 0.5)):
            if 2 * y + d - SLO < UN:
                up[y - 1, 2 * y + d - SLO] = w
    p = np.arange(P)
    cell = np.zeros((P, TI, 2), np.float32)
    for t in range(TI):
        cell[:, t, 0] = p % W
        cell[:, t, 1] = t * (P // W) + p // W
    base = np.zeros((P, 2, B * G), np.float32)
    base[:, 0] = np.arange(B * G) * (QY * QX * 2 * GC)
    base[:, 1] = (np.arange(B * G) % G) * (SN * UN * UW)
    earlier = np.triu(np.ones((P, P), np.float32), 1)
    region = np.broadcast_to(np.arange(E, dtype=np.float32) * QUEUE, (P, E))
    tile = np.broadcast_to(np.arange(SLOTS_T, dtype=np.float32), (P, SLOTS_T))
    return {"c_earlier": earlier, "c_region": np.ascontiguousarray(region), "c_tile": np.ascontiguousarray(tile),
            "c_ident": np.eye(P, dtype=np.float32), "c_up": up, "c_cell": cell, "c_base": base}


def chunks(w):
    return w.rearrange("(c p) n -> p c n", p=P)


def rows(v, n):
    return bass.AP(tensor=v.tensor, offset=v.offset, ap=[[0, n], [1, v.shape[0]]])


def inner(ap, k):
    return bass.AP(tensor=ap.tensor, offset=ap.offset, ap=[*ap.ap, [0, k]])



class Count:

    def __init__(self):
        self.now = 0

    def up(self, by=1):
        self.now += by
        return by


def table(nc, sem, d):
    with ExitStack() as ctx:
        sb = lambda n, s, t=F32: ctx.enter_context(nc.sbuf_tensor(n, s, t))
        rpe = sb("tb_rpe", [RY, RY, G])
        up = sb("tb_up", [RY, UN])
        wide = sb("tb_wide", [RY, G, UN])
        full = sb("tb_full", [UN, G, UN])
        zero = sb("tb_zero", [P, 34 * 64])
        ps = ctx.enter_context(nc.psum_tensor("tb_ps", [UN, 2, 512], F32))
        loaded, cleared, halves, widened, product, copied, stored, zeroed = (
            sem("tb_" + x) for x in ("loaded", "cleared", "halves", "widened", "product", "copied", "stored", "zeroed"))
        block = ctx.enter_context(nc.Block())
        first = 2 - SLO

        @block.sync
        def _(sp):
            sp.dma_start(rpe[:, :, :], d["rpe"][0:RY, 0:RY, :]).then_inc(loaded, 16)
            sp.dma_start(up[:, :], d["c_up"]).then_inc(loaded, 16)
            quads = d["quads"].rearrange("n y x r c -> (n y) x (r c)")
            sp.wait_ge(zeroed, 1)
            nrow = B * G * QY
            z = zero[0:nrow // 8, 0:8 * 2 * GC].rearrange("p (a c) -> p a c", a=8)
            for x in (0, QX - 1):
                dst = bass.AP(tensor=quads.tensor, offset=x * 2 * GC,
                              ap=[[8 * QX * 2 * GC, nrow // 8], [QX * 2 * GC, 8], [1, 2 * GC]])
                sp.dma_start(dst, z).then_inc(stored, 16)
            z = zero[0:B * G, 0:W * GC].rearrange("p (a c) -> p a c", a=W)
            for off in (2 * GC, (QY - 1) * QX * 2 * GC + 2 * GC + GC):
                dst = bass.AP(tensor=quads.tensor, offset=off,
                              ap=[[QY * QX * 2 * GC, B * G], [2 * GC, W], [1, GC]])
                sp.dma_start(dst, z).then_inc(stored, 16)
            sp.wait_ge(copied, 1)
            for h in range(G):
                src = full[:, h, :]
                src = bass.AP(tensor=src.tensor, offset=src.offset, ap=[src.ap[0], [1, SN], [1, UW]])
                sp.dma_start(d["shifts"][h].rearrange("f u j -> u f j"), src).then_inc(stored, 16)
            sp.wait_ge(stored, 16 * (4 + G))

        @block.gpsimd
        def _(pool):
            pool.memset(zero[:, :], 0.0).then_inc(zeroed, 1)

        @block.vector
        def _(dve):
            dve.memset(wide[:, :, :], 0.0).then_inc(cleared, 1)
            dve.wait_ge(loaded, 32)
            dve.wait_ge(cleared, 1)
            r = rpe[:, :, :].rearrange("y x h -> y h x")
            dve.tensor_copy(wide[:, :, first::2], r[:, :, 0:RY - 1]).then_inc(widened, 1)
            dve.tensor_scalar(wide[:, :, first - 1:first], r[:, :, 0:1], 0.5, None, ALU.mult).then_inc(widened, 1)
            dve.tensor_tensor(wide[:, :, first + 1::2], r[:, :, 0:RY - 1], r[:, :, 1:RY], ALU.add).then_inc(halves, 1)
            dve.wait_ge(halves, 1)
            dve.tensor_scalar(wide[:, :, first + 1::2], wide[:, :, first + 1::2], 0.5, None, ALU.mult).then_inc(widened, 1)
            dve.wait_ge(product, 1)
            dve.tensor_copy(full[:, :, :].rearrange("p (a h) u -> p a (h u)", a=2), ps[:, :, 0:G // 2 * UN]).then_inc(copied, 1)

        @block.tensor
        def _(pe):
            pe.wait_ge(loaded, 32)
            pe.wait_ge(widened, 3)
            w = wide[:, :, :].rearrange("p (a h) u -> p a (h u)", a=2)
            for a in range(2):
                mm = pe.matmul(ps[:, a, 0:G // 2 * UN], up[:, :], w[:, a, :], start=True, stop=True)
            mm.then_inc(product, 1)


def mixer_q(nc, sem, d, keep):
    with ExitStack() as ctx:
        sb = lambda n, s, t=F32: ctx.enter_context(nc.sbuf_tensor(n, s, t))
        x_sb = sb("mq_x", [P, 2, HT, NC])
        stats = sb("mq_stats", [P, HT, 6])
        mv = sb("mq_mv", [P, HT, 2])
        var = sb("mq_var", [P, HT])
        half = sb("mq_half", [P, HT])
        rstd = sb("mq_rstd", [P, HT])
        xn = sb("mq_xn", [P, 2, HT, NC])
        wq = sb("mq_wq", [P, CH, NC])
        bq = sb("mq_bq", [P, CH])
        ident = sb("mq_ident", [P, P])
        xnT = sb("mq_xnT", [P, CH, HN])
        qT = sb("mq_qT", [P, 2, CH, HN])
        qparts = sb("mq_qparts", [P, 2, 2, CH, HN], F32R)
        psT = ctx.enter_context(nc.psum_tensor("mq_psT", [P, CH, HN], F32))
        psQ = ctx.enter_context(nc.psum_tensor("mq_psQ", [P, CH, HN], F32))
        half_set, var_ready, rstd_ready, weights, norm_steps, xn_ready, t_done, t_copied, q_done, q_copied, q_high, q_low, q_padded, pad_zero = (
            sem("mq_" + x) for x in ("half_set", "var_ready", "rstd_ready", "weights", "norm_steps", "xn_ready", "t_done", "t_copied", "q_done", "q_copied", "q_high", "q_low", "q_padded", "pad_zero"))
        x_in, quad_out, q_out = ([sem(f"mq_{x}{f}") for f in range(2)] for x in ("x_in", "quad_out", "q_out"))
        passed = keep["passed"]
        block = ctx.enter_context(nc.Block())
        x_v = d["x"].rearrange("b h w c -> (b h w) c").rearrange("(s t p) c -> s p t c", p=P, t=HT)
        q_v = d["q_scr"].rearrange("(b j) z p (f n) -> b f z p j n", j=CH, f=2)
        QD = 2 * HT * (P // W)

        @block.sync
        def _(sp):
            sp.dma_start(ident[:, :], d["c_ident"]).then_inc(weights, 16)
            sp.dma_start(wq[:, :, :], chunks(d["w_q"])).then_inc(weights, 16)
            sp.dma_start(bq[:, :], d["b_q"].rearrange("(c p) -> p c", p=P), allow_slow_non_contiguous=True).then_inc(weights, 16)
            sp.sem_inc(xn_ready, 2 * HT)
            with sp.Fori(0, B) as b:
                for f in range(2):
                    sp.wait_ge(xn_ready, b * 2 * HT + (f + 1) * HT)
                    sp.dma_start(x_sb[:, f], x_v[bass.ds(b * 2 + f, 1)].rearrange("s p t c -> (s p) t c")).then_inc(x_in[f], 16)
                for f in range(2):
                    for t in range(HT):
                        sp.wait_ge(xn_ready, b * 2 * HT + (2 + f) * HT + t + 1)
                        src = xn[:, f, t, :].rearrange("p (g c) -> p g c", g=G)
                        y = (f * HT + t) * (P // W)
                        for r in range(2):
                            for k in range(P // W):
                                dst = d["quads"][bass.ds(b * G, G), y + k + 1 - r:y + k + 2 - r, 1:W + 1, r, :]
                                sp.dma_start(dst.rearrange("g y x c -> (y x) g c"), src[k * W:k * W + W]).then_inc(quad_out[f], 16)
                    sp.wait_ge(q_high, b * 2 * CH + f * CH + CH)
                    sp.sem_inc(passed, 1)
                    sp.wait_ge(q_low, b * 2 * CH + f * CH + 3 * CH)
                    for z in range(2):
                        sp.dma_start(q_v[bass.ds(b, 1), f, z].rearrange("b p j n -> (b p) j n"), qparts[:, f, z].bitcast(F32)).then_inc(q_out[f], 16)
            for f in range(2):
                sp.wait_ge(quad_out[f], (B + 1) * QD * 16)
                sp.wait_ge(q_out[f], (B + 1) * 32)

        @block.gpsimd
        def _(pool):
            pool.memset(keep["q_pad"][:, :, :, :, :], 0.0).then_inc(pad_zero, 1)
            pool.memset(half[:, :], -0.5).then_inc(half_set, 1)
            pool.wait_ge(half_set, 1)
            with pool.Fori(0, B) as b:
                for f in range(2):
                    pool.wait_ge(var_ready, b * 2 + f + 1)
                    pool.tensor_tensor(rstd[:, :], var[:, :], half[:, :], ALU.pow).then_inc(rstd_ready, 1)

        @block.vector
        def _(dve):
            K = 2 * 2 * HT
            dve.sem_inc(t_done, 2)
            for f in range(2):
                dve.sem_inc(quad_out[f], 16 * QD)
            dve.wait_ge(pad_zero, 1)

            def pad(b, f):
                for j in range(CH):
                    dve.wait_ge(q_copied, b * 2 * CH + f * CH + CH + j + 1)
                    dst = keep["q_pad"][:, j, bass.ds(b, 1), f * HROWS + 1:(f + 1) * HROWS + 1, 1:W + 1]
                    dve.tensor_copy(dst.rearrange("p b y x -> p (b y) x"), qT[:, f, j, :].rearrange("p (y x) -> p y x", x=W)).then_inc(q_padded, 1)
                    dve.wait_ge(q_high, b * 2 * CH + f * CH + j + 1)
                    dve.tensor_tensor(qparts[:, f, 1, j, :], qT[:, f, j, :], qparts[:, f, 0, j, :].bitcast(F32), ALU.subtract).then_inc(q_low, 1)

            with dve.Fori(0, B) as b:
                n = Count()
                for f in range(2):
                    dve.wait_ge(x_in[f], b * 16 + 16)
                    for t in range(HT):
                        dve.bn_stats(stats[:, t, :], x_sb[:, f, t, :]).then_inc(norm_steps, n.up())
                    dve.wait_ge(norm_steps, b * K + n.now)
                    dve.sem_inc(passed, 1)
                    for t in range(HT):
                        dve.bn_aggr(mv[:, t, :], stats[:, t, :]).then_inc(norm_steps, n.up())
                    dve.wait_ge(norm_steps, b * K + n.now)
                    dve.tensor_scalar(var[:, :], mv[:, :, 1], 1e-6, None, ALU.add).then_inc(var_ready, 1)
                    dve.wait_ge(rstd_ready, b * 2 + f + 1)
                    dve.wait_ge(quad_out[f], b * (16 * QD) + 16 * QD)
                    dve.wait_ge(t_done, b * 2 + f + 1)
                    for t in range(HT):
                        dve.tensor_scalar(xn[:, f, t, :], x_sb[:, f, t, :], mv[:, t, 0:1], rstd[:, t:t + 1],
                                          ALU.subtract, ALU.mult).then_inc(xn_ready, 1)
                    dve.wait_ge(xn_ready, b * 2 * HT + (3 + f) * HT)
                for f in range(2):
                    pad(b, f)
                assert n.now == K

        @block.tensor
        def _(pe):
            pe.wait_ge(weights, 48)
            pe.sem_inc(t_copied, 1)
            pe.sem_inc(q_copied, CH)
            with pe.Fori(0, B) as b:
                for f in range(2):
                    for t in range(HT):
                        pe.wait_ge(xn_ready, b * 2 * HT + (2 + f) * HT + t + 1)
                        if t == 0:
                            pe.wait_ge(t_copied, b * 2 + f + 1)
                        for j in range(CH):
                            mm = pe.transpose(psT[:, j, t * P:(t + 1) * P], xn[:, f, t, j * P:(j + 1) * P], ident[:, :])
                    mm.then_inc(t_done, 1)
                    pe.wait_ge(t_copied, b * 2 + f + 2)
                    for j in range(CH):
                        pe.wait_ge(q_copied, b * 2 * CH + f * CH + j + 1)
                        for c in range(CH):
                            mm = pe.matmul(psQ[:, j, :], wq[:, c, j * P:(j + 1) * P], xnT[:, c, :], start=c == 0, stop=c == CH - 1)
                        mm.then_inc(q_done, 1)

        @block.scalar
        def _(act):
            act.wait_ge(weights, 48)
            act.sem_inc(q_done, CH)
            act.sem_inc(q_padded, 2 * CH)
            act.sem_inc(q_low, 2 * CH)
            for f in range(2):
                act.sem_inc(q_out[f], 32)
            with act.Fori(0, B) as b:
                for f in range(2):
                    act.wait_ge(t_done, b * 2 + f + 3)
                    act.wait_ge(q_done, b * 2 * CH + f * CH + CH)
                    act.activation(xnT[:, :, :], psT[:, :, :], ACT.Copy).then_inc(t_copied, 1)
                    act.wait_ge(q_out[f], b * 32 + 32)
                    act.wait_ge(q_padded, b * 2 * CH + f * CH + CH)
                    act.wait_ge(q_low, b * 2 * CH + f * CH + CH)
                    for j in range(CH):
                        act.wait_ge(q_done, b * 2 * CH + f * CH + CH + j + 1)
                        act.activation(qT[:, f, j, :], psQ[:, j, :], ACT.Identity, bias=bq[:, j:j + 1]).then_inc(q_copied, 1)
                        act.wait_ge(q_copied, b * 2 * CH + f * CH + CH + j + 1)
                        act.activation(qparts[:, f, 0, j, :], qT[:, f, j, :], ACT.Copy).then_inc(q_high, 1)


def offsets(nc, sem, d, keep):
    TAPS = 9
    with ExitStack() as ctx:
        sb = lambda n, s, t=F32: ctx.enter_context(nc.sbuf_tensor(n, s, t))
        wc = sb("of_wc", [P, TAPS, CH, P])
        bo = sb("of_bo", [P, CH])
        gain, shift = sb("of_gain", [P, NC]), sb("of_shift", [P, NC])
        woff = sb("of_woff", [P, GC, 2])
        ident = sb("of_ident", [P, P])
        cell, base = sb("of_cell", [P, TI, 2]), sb("of_base", [P, 2, B * G])
        oT = sb("of_oT", [P, CH, HN])
        on = sb("of_on", [P, 2, HT, NC])
        ge = sb("of_ge", [P, HT, NC])
        part = sb("of_part", [P, HT * G, GC])
        stats, mv = sb("of_stats", [P, HT, 6]), sb("of_mv", [P, HT, 2])
        var, half, rstd = sb("of_var", [P, HT]), sb("of_half", [P, HT]), sb("of_rstd", [P, HT])
        off, th = sb("of_off", [P, 2, G, HT]), sb("of_th", [P, 2, G, HT])
        pos = sb("of_pos", [P, 2, G, HT])
        v, fl, fr, co = (sb("of_" + x, [P, 2, 2, G, HT]) for x in ("v", "fl", "fr", "co"))
        whole = sb("of_whole", [P, 2, 2, G, HT], I32)
        flat = sb("of_flat", [P, 2, G, HT])
        ws, wb = sb("of_ws", [P, G, HT, 4]), sb("of_wb", [P, G, HT, 4])
        psC = ctx.enter_context(nc.psum_tensor("of_psC", [P, CH, HN], F32))
        psO = ctx.enter_context(nc.psum_tensor("of_psO", [P, HT, 512], F32))
        (weights, wc_zero, conv_done, oT_ready, back_done, steps, half_set, var_ready, rstd_ready, normed, gelu_done,
         off_ready, tanh_done) = (sem("of_" + x) for x in (
             "weights", "wc_zero", "conv_done", "oT_ready", "back_done", "steps", "half_set", "var_ready", "rstd_ready",
             "normed", "gelu_done", "off_ready", "tanh_done"))
        passed = keep["passed"]
        block = ctx.enter_context(nc.Block())

        @block.sync
        def _(sp):
            sp.dma_start(ident[:, :], d["c_ident"]).then_inc(weights, 16)
            sp.dma_start(bo[:, :], d["b_off0"].rearrange("(c p) -> p c", p=P), allow_slow_non_contiguous=True).then_inc(weights, 16)
            sp.dma_start(gain[:, :], rows(d["ln_g"], P)).then_inc(weights, 16)
            sp.dma_start(shift[:, :], rows(d["ln_b"], P)).then_inc(weights, 16)
            sp.dma_start(woff[:, :, :].rearrange("p c k -> p (c k)"), rows(d["w_offp"].rearrange("c k -> (c k)"), P)).then_inc(weights, 16)
            sp.dma_start(cell[:, :, :], d["c_cell"]).then_inc(weights, 16)
            sp.dma_start(base[:, :, :], d["c_base"]).then_inc(weights, 16)
            sp.wait_ge(wc_zero, 1)
            w = d["w_off0"].rearrange("y x i (j g o) -> g i (y x) j o", g=2, o=GC)
            for g in range(2):
                for j in range(CH):
                    sp.dma_start(wc[g * GC:(g + 1) * GC, :, j, g * GC:(g + 1) * GC], w[g, :, :, j]).then_inc(weights, 16)
            sp.wait_ge(weights, 16 * (7 + 2 * CH))

        @block.gpsimd
        def _(pool):
            pool.memset(wc[:, :, :, :], 0.0).then_inc(wc_zero, 1)
            pool.memset(half[:, :], -0.5).then_inc(half_set, 1)
            pool.wait_ge(half_set, 1)
            with pool.Fori(0, B) as b:
                for f in range(2):
                    pool.wait_ge(var_ready, b * 2 + f + 1)
                    pool.tensor_tensor(rstd[:, :], var[:, :], half[:, :], ALU.pow).then_inc(rstd_ready, 1)

        @block.tensor
        def _(pe):
            pe.wait_ge(weights, 16 * (7 + 2 * CH))
            pe.sem_inc(oT_ready, CH)
            pe.sem_inc(normed, 1)
            with pe.Fori(0, B) as b:
                for f in range(2):
                    for j in range(CH):
                        pe.wait_ge(oT_ready, b * 2 * CH + f * CH + j + 1)
                        for tap in range(TAPS):
                            y, x = f * HROWS + tap // 3, tap % 3
                            q = keep["q_pad"][:, j, bass.ds(b, 1), y:y + HROWS, x:x + W].rearrange("p b y x -> p (b y) x")
                            mm = pe.matmul(psC[:, j, :].rearrange("p (y x) -> p y x", x=W), wc[:, tap, j, :], q,
                                           start=tap == 0, stop=tap == TAPS - 1)
                        mm.then_inc(conv_done, 1)
                    pe.wait_ge(normed, b * 2 + f + 1)
                    for j in range(CH):
                        pe.wait_ge(oT_ready, b * 2 * CH + f * CH + CH + j + 1)
                        for t in range(HT):
                            mm = pe.transpose(psO[:, t, j * P:(j + 1) * P], oT[:, j, t * P:(t + 1) * P], ident[:, :])
                    mm.then_inc(back_done, 1)

        @block.scalar
        def _(act):
            act.wait_ge(weights, 16 * (7 + 2 * CH))
            act.sem_inc(back_done, 1)
            act.sem_inc(off_ready, 2)
            with act.Fori(0, B) as b:
                for f in range(2):
                    act.wait_ge(back_done, b * 2 + f + 1)
                    for j in range(CH):
                        act.wait_ge(conv_done, b * 2 * CH + f * CH + j + 1)
                        act.activation(oT[:, j, :], psC[:, j, :], ACT.Identity, bias=bo[:, j:j + 1]).then_inc(oT_ready, 1)
                    act.wait_ge(steps, b * OFF_K + (f * OFF_K // 2 + OFF_GELU))
                    act.wait_ge(off_ready, b * 4 + f * 2 + 2)
                    act.activation(ge[:, :, :], on[:, f], ACT.Gelu).then_inc(gelu_done, 1)
                    act.wait_ge(off_ready, b * 4 + f * 2 + 4)
                    act.activation(th[:, :, :, :], off[:, :, :, :], ACT.Tanh).then_inc(tanh_done, 1)

        @block.vector
        def _(dve):
            dve.wait_ge(weights, 16 * (7 + 2 * CH))
            with dve.Fori(0, B) as b:
                n = Count()

                def after():
                    dve.wait_ge(steps, b * OFF_K + n.now)

                for f in range(2):
                    dve.wait_ge(back_done, b * 2 + f + 2)
                    for t in range(HT):
                        dve.bn_stats(stats[:, t, :], psO[:, t, 0:NC]).then_inc(steps, n.up())
                    after()
                    dve.sem_inc(passed, 1)
                    for t in range(HT):
                        dve.bn_aggr(mv[:, t, :], stats[:, t, :]).then_inc(steps, n.up())
                    after()
                    dve.tensor_scalar(var[:, :], mv[:, :, 1], 1e-3, None, ALU.add).then_inc(var_ready, 1)
                    dve.wait_ge(rstd_ready, b * 2 + f + 1)
                    for t in range(HT):
                        dve.tensor_scalar(on[:, f, t, :], psO[:, t, 0:NC], mv[:, t, 0:1], rstd[:, t:t + 1],
                                          ALU.subtract, ALU.mult).then_inc(steps, n.up())
                    after()
                    dve.sem_inc(normed, 1)
                    g3 = gain[:, :].rearrange("p (o c) -> p o c", o=1).broadcast_to([P, HT, NC])
                    s3 = shift[:, :].rearrange("p (o c) -> p o c", o=1).broadcast_to([P, HT, NC])
                    dve.tensor_tensor(on[:, f], on[:, f], g3, ALU.mult).then_inc(steps, n.up())
                    after()
                    dve.tensor_tensor(on[:, f], on[:, f], s3, ALU.add).then_inc(steps, n.up())
                    if f == 0:
                        assert n.now == OFF_GELU
                    dve.wait_ge(gelu_done, b * 2 + f + 1)
                    ge3 = ge[:, :, :].rearrange("p t (g c) -> p (t g) c", g=G)
                    for k in range(2):
                        w3 = woff[:, :, k].rearrange("p (o c) -> p o c", o=1).broadcast_to([P, HT * G, GC])
                        dve.tensor_tensor(part[:, :, :], ge3, w3, ALU.mult).then_inc(steps, n.up())
                        after()
                        dve.tensor_reduce(off[:, k].rearrange("p g t -> p t g"), part[:, :, :].rearrange("p (t g) c -> p t g c", g=G),
                                          AX.X, ALU.add).then_inc(off_ready, 1)
                        dve.wait_ge(off_ready, b * 4 + (f * 2 + k + 3))
                    dve.wait_ge(tanh_done, b * 2 + f + 1)
                    for k in range(2):
                        c3 = cell[:, f * HT:(f + 1) * HT, k].rearrange("p (o t) -> p o t", o=1).broadcast_to([P, G, HT])
                        dve.scalar_tensor_tensor(pos[:, k], th[:, k], float(W // 2), c3, ALU.mult, ALU.add).then_inc(steps, n.up())
                    after()
                    dve.tensor_scalar(v[:, 0], pos[:, :, :, :], 0.5, None, ALU.add).then_inc(steps, n.up())
                    dve.tensor_scalar(v[:, 1], pos[:, :, :, :], -1.0, float(1 - SLO), ALU.mult, ALU.add).then_inc(steps, n.up())
                    after()
                    dve.tensor_copy(whole[:, :, :, :, :], v[:, :, :, :, :]).then_inc(steps, n.up())
                    after()
                    dve.tensor_copy(fl[:, :, :, :, :], whole[:, :, :, :, :]).then_inc(steps, n.up())
                    after()
                    dve.tensor_tensor(co[:, :, :, :, :], fl[:, :, :, :, :], v[:, :, :, :, :], ALU.is_gt).then_inc(steps, n.up())
                    after()
                    dve.tensor_tensor(fl[:, :, :, :, :], fl[:, :, :, :, :], co[:, :, :, :, :], ALU.subtract).then_inc(steps, n.up())
                    after()
                    dve.tensor_scalar(fl[:, 0], fl[:, 0], 0.0, float(H), ALU.max, ALU.min).then_inc(steps, n.up())
                    dve.tensor_scalar(fl[:, 1], fl[:, 1], 0.0, float(SN - 1), ALU.max, ALU.min).then_inc(steps, n.up())
                    after()
                    dve.tensor_tensor(fr[:, :, :, :, :], v[:, :, :, :, :], fl[:, :, :, :, :], ALU.subtract).then_inc(steps, n.up())
                    dve.scalar_tensor_tensor(flat[:, 0], fl[:, 0, 1], float(QX), fl[:, 0, 0], ALU.mult, ALU.add).then_inc(steps, n.up())
                    dve.scalar_tensor_tensor(flat[:, 1], fl[:, 1, 0], float(UN), fl[:, 1, 1], ALU.mult, ALU.add).then_inc(steps, n.up())
                    after()
                    dve.tensor_scalar(fr[:, :, :, :, :], fr[:, :, :, :, :], 0.0, 1.0, ALU.max, ALU.min).then_inc(steps, n.up())
                    for k, pitch in ((0, 2 * GC), (1, UW)):
                        dve.tensor_scalar(flat[:, k], flat[:, k], float(pitch), None, ALU.mult).then_inc(steps, n.up())
                    after()
                    dve.tensor_scalar(co[:, :, :, :, :], fr[:, :, :, :, :], -1.0, 1.0, ALU.mult, ALU.add).then_inc(steps, n.up())
                    for k in range(2):
                        dst = (keep["quad_at"], keep["shift_at"])[k][:, bass.ds(b, 1), :, f * HT:(f + 1) * HT].rearrange("p b g t -> p (b g) t")
                        b3 = inner(base[:, k, bass.ds(b * G, G)], HT)
                        dve.tensor_tensor(dst, flat[:, k], b3, ALU.add).then_inc(steps, n.up())
                    after()
                    for q, (x, y) in enumerate(((co, co), (co, fr), (fr, co), (fr, fr))):
                        dve.tensor_tensor(ws[:, :, :, q], x[:, 0, 0], y[:, 0, 1], ALU.mult).then_inc(steps, n.up())
                    for q, x in enumerate((co[:, 1, 0], fr[:, 1, 0], co[:, 1, 1], fr[:, 1, 1])):
                        dve.tensor_copy(wb[:, :, :, q], x).then_inc(steps, n.up())
                    after()
                    for w, name in ((ws, "quad_w"), (wb, "shift_w")):
                        dst = keep[name][:, bass.ds(b, 1), :, f * HT:(f + 1) * HT, :].rearrange("p b g t k -> p (b g) (t k)")
                        dve.tensor_copy(dst, w[:, :, :, :].rearrange("p g t k -> p g (t k)")).then_inc(steps, n.up())
                    after()
                assert n.now == OFF_K, n.now


OFF_GELU = 3 * HT + 2
OFF_K = 2 * 45


def keys(nc, sem, d, keep):
    QUAD = 4 * GC
    with ExitStack() as ctx:
        sb = lambda n, s, t=F32: ctx.enter_context(nc.sbuf_tensor(n, s, t))
        at = sb("ke_at", [P, 2, G, HT], I32)
        quad = sb("ke_quad", [P, HT, G, QUAD])
        prod = sb("ke_prod", [P, G, 4, GC])
        side = sb("ke_side", [P, G, 2, GC])
        xs = sb("ke_xs", [P, HT, G, GC])
        xsT = sb("ke_xsT", [P, CH, HN])
        wk, wv = sb("ke_wk", [P, CH, NC]), sb("ke_wv", [P, CH, NC])
        bk, bks, bv = sb("ke_bk", [P, CH]), sb("ke_bks", [P, CH]), sb("ke_bv", [P, NC])
        ident = sb("ke_ident", [P, P])
        kT, kparts = sb("ke_kT", [P, CH, HN]), sb("ke_kparts", [P, 2, 2, CH, HN], F32R)
        vt = sb("ke_vt", [P, 2, HT, NC])
        psT = ctx.enter_context(nc.psum_tensor("ke_psT", [P, CH, HN], F32))
        psK = ctx.enter_context(nc.psum_tensor("ke_psK", [P, CH, HN], F32))
        psV = ctx.enter_context(nc.psum_tensor("ke_psV", [P, 2, 512], F32))
        (weights, bks_ready, staged, prod_done, side_done, xs_ready, t_done, t_copied, k_done, k_ready, k_high, k_low, v_done, v_ready) = (
            sem("ke_" + x) for x in ("weights", "bks_ready", "staged", "prod_done", "side_done", "xs_ready", "t_done",
                                     "t_copied", "k_done", "k_ready", "k_high", "k_low", "v_done", "v_ready"))
        gathered = [sem(f"ke_gathered{t}") for t in range(HT)]
        k_out, v_out = ([sem(f"ke_{x}{f}") for f in range(2)] for x in ("k_out", "v_out"))
        passed = keep["passed"]
        block = ctx.enter_context(nc.Block())
        flat = d["quads"].rearrange("n y x r c -> (n y x r c)").rearrange("(n o) -> n o", o=1)
        k_v = d["k_scr"].rearrange("(b j) z p (f n) -> b f z p j n", j=CH, f=2)

        @block.sync
        def _(sp):
            sp.dma_start(ident[:, :], d["c_ident"]).then_inc(weights, 16)
            sp.dma_start(wk[:, :, :], chunks(d["w_k"])).then_inc(weights, 16)
            sp.dma_start(wv[:, :, :], chunks(d["w_v"])).then_inc(weights, 16)
            sp.dma_start(bk[:, :], d["b_k"].rearrange("(c p) -> p c", p=P), allow_slow_non_contiguous=True).then_inc(weights, 16)
            sp.dma_start(bv[:, :], rows(d["b_v"], P)).then_inc(weights, 16)
            with sp.Fori(0, B) as b:
                for f in range(2):
                    sp.wait_ge(k_high, b * 2 * CH + (f + 1) * CH)
                    sp.sem_inc(passed, 1)
                    sp.wait_ge(k_low, b * 2 * CH + (f + 2) * CH)
                    for z in range(2):
                        sp.dma_start(k_v[bass.ds(b, 1), f, z].rearrange("b p j n -> (b p) j n"), kparts[:, f, z].bitcast(F32)).then_inc(k_out[f], 16)
                    for t in range(HT):
                        sp.wait_ge(v_ready, b * 2 * HT + f * HT + t + 3)
                        dst = d["v_scr"][bass.ds(b * CH, CH), f * HT + t].rearrange("j p c -> p j c")
                        sp.dma_start(dst, vt[:, f, t, :].rearrange("p (j c) -> p j c", j=CH)).then_inc(v_out[f], 16)
            for f in range(2):
                sp.wait_ge(k_out[f], (B + 1) * 32)
                sp.wait_ge(v_out[f], (B + 1) * 16 * HT)

        @block.gpsimd
        def _(pool):
            pool.sem_inc(xs_ready, 2 * HT)
            with pool.Fori(0, B) as b:
                for f in range(2):
                    pool.wait_ge(xs_ready, b * 2 * HT + (f + 1) * HT)
                    pool.sem_inc(passed, 1)
                    src = keep["quad_at"][:, bass.ds(b, 1), :, f * HT:(f + 1) * HT].rearrange("p b g t -> p (b g) t")
                    pool.tensor_copy(at[:, f], src).then_inc(staged, 1)
                    pool.wait_ge(staged, b * 2 + f + 1)
                    for t in range(HT):
                        pool.wait_ge(xs_ready, b * 2 * HT + (f + 1) * HT + t + 1)
                        pool.sem_inc(passed, 1)
                        for g in range(G):
                            pool.indirect_dma_start(out=quad[:, t, g, :], out_offset=None, in_=flat,
                                                    in_offset=bass.IndirectOffsetOnAxis(ap=at[:, f, g, t:t + 1], axis=0)
                                                    ).then_inc(gathered[t], 16)

        @block.vector
        def _(dve):
            dve.wait_ge(weights, 16 * 5)
            dve.sem_inc(t_done, 1)
            dve.sem_inc(k_low, CH)
            for f in range(2):
                dve.sem_inc(v_out[f], 16 * HT)

            def samples(b, f):
                for t in range(HT):
                    s = b * 2 * HT + (f * HT + t)
                    dve.wait_ge(gathered[t], b * (2 * G * 16) + (f + 1) * G * 16)
                    w = keep["quad_w"][:, bass.ds(b, 1), :, f * HT + t, :].rearrange("p b g q -> p (b g) q")
                    dve.tensor_tensor(prod[:, :, :, :], quad[:, t].rearrange("p g (q c) -> p g q c", c=GC), inner(w, GC), ALU.mult).then_inc(prod_done, 1)
                    dve.wait_ge(prod_done, s + 1)
                    dve.tensor_tensor(side[:, :, :, :], prod[:, :, 0:2], prod[:, :, 2:4], ALU.add).then_inc(side_done, 1)
                    dve.wait_ge(side_done, s + 1)
                    if t == 0:
                        dve.wait_ge(t_done, b * 2 + f + 1)
                    dve.tensor_tensor(xs[:, t], side[:, :, 0], side[:, :, 1], ALU.add).then_inc(xs_ready, 1)
                    dve.wait_ge(xs_ready, s + (2 * HT + 1))

            def results(b, f):
                dve.wait_ge(v_out[f], b * (16 * HT) + 16 * HT)
                for t in range(HT):
                    dve.wait_ge(v_done, b * 2 * HT + (f * HT + t + 1))
                    dve.tensor_tensor(vt[:, f, t, :], psV[:, t % 2, 0:NC], bv[:, :], ALU.add).then_inc(v_ready, 1)
                for j in range(CH):
                    dve.wait_ge(k_high, b * 2 * CH + (f * CH + j + 1))
                    dve.tensor_tensor(kparts[:, f, 1, j, :], kT[:, j, :], kparts[:, f, 0, j, :].bitcast(F32), ALU.subtract).then_inc(k_low, 1)

            samples(0, 0)
            samples(0, 1)
            results(0, 0)
            with dve.Fori(1, B) as b:
                samples(b, 0)
                results(b - 1, 1)
                samples(b, 1)
                results(b, 0)
            results(B - 1, 1)

        @block.tensor
        def _(pe):
            pe.wait_ge(weights, 16 * 5)
            pe.sem_inc(t_copied, 1)
            pe.sem_inc(k_ready, CH)
            pe.sem_inc(v_ready, 2)
            with pe.Fori(0, B) as b:
                for f in range(2):
                    for t in range(HT):
                        if t == 0:
                            pe.wait_ge(t_copied, b * 2 + f + 1)
                        pe.wait_ge(xs_ready, b * 2 * HT + (f * HT + t + 1 + 2 * HT))
                        for j in range(CH):
                            mm = pe.transpose(psT[:, j, t * P:(t + 1) * P], xs[:, t, 2 * j:2 * j + 2, :].rearrange("p g c -> p (g c)"), ident[:, :])
                    mm.then_inc(t_done, 1)
                    pe.wait_ge(t_copied, b * 2 + f + 2)
                    for t in range(HT):
                        pe.wait_ge(v_ready, b * 2 * HT + (f * HT + t + 1))
                        for c in range(CH):
                            mm = pe.matmul(psV[:, t % 2, 0:NC], xsT[:, c, t * P:(t + 1) * P], wv[:, c, :], start=c == 0, stop=c == CH - 1)
                        mm.then_inc(v_done, 1)
                    for j in range(CH):
                        pe.wait_ge(k_ready, b * 2 * CH + (f * CH + j + 1))
                        for c in range(CH):
                            mm = pe.matmul(psK[:, j, :], wk[:, c, j * P:(j + 1) * P], xsT[:, c, :], start=c == 0, stop=c == CH - 1)
                        mm.then_inc(k_done, 1)

        @block.scalar
        def _(act):
            act.wait_ge(weights, 16 * 5)
            act.activation(bks[:, :], bk[:, :], ACT.Copy, scale=SCALE).then_inc(bks_ready, 1)
            act.wait_ge(bks_ready, 1)
            act.sem_inc(k_done, CH)
            for f in range(2):
                act.sem_inc(k_out[f], 32)
            with act.Fori(0, B) as b:
                for f in range(2):
                    act.wait_ge(t_done, b * 2 + f + 2)
                    act.wait_ge(k_done, b * 2 * CH + (f + 1) * CH)
                    act.activation(xsT[:, :, :], psT[:, :, :], ACT.Copy).then_inc(t_copied, 1)
                    act.wait_ge(k_out[f], b * 32 + 32)
                    for j in range(CH):
                        act.wait_ge(k_done, b * 2 * CH + ((f + 1) * CH + j + 1))
                        act.wait_ge(k_low, b * 2 * CH + (f * CH + j + 1))
                        act.activation(kT[:, j, :], psK[:, j, :], ACT.Identity, bias=bks[:, j:j + 1], scale=SCALE).then_inc(k_ready, 1)
                        act.wait_ge(k_ready, b * 2 * CH + ((f + 1) * CH + j + 1))
                        act.activation(kparts[:, f, 0, j, :], kT[:, j, :], ACT.Copy).then_inc(k_high, 1)


def attend(nc, sem, d, keep):
    WB = 4
    ON_PE = ATTEND_ON_PE
    ON_DVE = [t for t in range(TI) if t not in ON_PE]
    LAG = 6
    ISSUE = [[t] if t < LAG else list(range(LAG, TI)) if t == LAG else [] for t in range(TI)]
    MAX_AT, SPREAD_AT = 2, 4
    with ExitStack() as ctx:
        sb = lambda n, s, t=F32: ctx.enter_context(nc.sbuf_tensor(n, s, t))
        at = sb("at_at", [P, 2, TI], I32)
        wt = sb("at_wt", [P, 2, TI, 4])
        window = sb("at_window", [P, WB, UW, UW])
        rowx = sb("at_rowx", [P, WB, UW, W])
        below = sb("at_below", [P, WB, P])
        logit = sb("at_logit", [P, 2, TI, N])
        most = sb("at_most", [P, 2, N])
        mx = sb("at_mx", [P, TI])
        diag = sb("at_diag", [P, TI, P])
        neg = sb("at_neg", [P, N])
        ident, minus, ones = sb("at_ident", [P, P]), sb("at_minus", [P, P]), sb("at_ones", [P, P])
        qs, ks = sb("at_qs", [P, 2, 2, N], F32R), sb("at_ks", [P, 2, N], F32R)
        val = sb("at_val", [P, 2, TI, P])
        raw = sb("at_raw", [P, N])
        inverse = diag[:, :, :].rearrange("p t q -> p (t q)")
        psS = ctx.enter_context(nc.psum_tensor("at_psS", [P, 2, N], F32))
        psM = ctx.enter_context(nc.psum_tensor("at_psM", [P, N], F32))
        psO = ctx.enter_context(nc.psum_tensor("at_psO", [P, N], F32))
        (consts, ones_set, minus_set, staged, x0_done, below_ready, x_done, y0_done, logit_done, most_done, sum_ready, turned, mx_ready,
         diag_ready, spread, neg_ready, sub_done, p_done, pv_done, raw_ready, inverse_ready, o_done) = (sem("at_" + x) for x in (
             "consts", "ones_set", "minus_set", "staged", "x0_done", "below_ready", "x_done", "y0_done", "logit_done", "most_done",
             "sum_ready", "turned", "mx_ready", "diag_ready", "spread", "neg_ready", "sub_done", "p_done", "pv_done", "raw_ready",
             "inverse_ready", "o_done"))
        gathered = [sem(f"at_gathered{w}") for w in range(WB)]
        qk_in, v_in = ([sem(f"at_{n}{h}") for h in range(2)] for n in ("qk_in", "v_in"))
        passed = keep["passed"]
        block = ctx.enter_context(nc.Block())
        flat = d["shifts"].rearrange("h f u j -> (h f u j)").rearrange("(n o) -> n o", o=1)
        half = lambda h: slice(h * GC, (h + 1) * GC)

        def every_pair(eng, pair):
            pair(0, True)
            with eng.Fori(1, PAIRS) as i:
                pair(i, False)

        @block.sync
        def _(sp):
            sp.dma_start(ident[:, :], d["c_ident"]).then_inc(consts, 16)

            def pair(i, first):
                for h in range(2):
                    s = i * 2 + h
                    if not first:
                        sp.wait_ge(sum_ready, s * TI - TI)
                        sp.sem_inc(passed, 1)
                    k = d["k_scr"][bass.ds(i, 1), :, half(h), :].rearrange("a z c n -> (a z) c n")
                    sp.dma_start(ks[:, h, :].bitcast(F32), k).then_inc(qk_in[h], 16)
                    for z in range(2):
                        q = d["q_scr"][bass.ds(i, 1), z, half(h), :].rearrange("a c n -> (a c) n")
                        for a in range(2):
                            sp.dma_start(qs[half(a), h, z, :].bitcast(F32), q).then_inc(qk_in[h], 16)
                if first:
                    sp.wait_ge(ones_set, 3)
                for h in range(2):
                    if not first:
                        sp.wait_ge(pv_done, (i * 2 + h) * TI - TI)
                        sp.sem_inc(passed, 1)
                    src = d["v_scr"][bass.ds(i, 1), :, :, half(h)].rearrange("a t p c -> (a p) t c")
                    sp.dma_start(val[:, h, :, half(h)], src).then_inc(v_in[h], 16)

            every_pair(sp, pair)

        @block.gpsimd
        def _(pool):
            pool.memset(ones[:, :], 1.0).then_inc(ones_set, 1)
            for h in range(2):
                pool.memset(val[:, h, :, half(1 - h)], 1.0).then_inc(ones_set, 1)

            def subtract(s, h, k):
                if k == 0:
                    pool.wait_ge(neg_ready, s + 1)
                pool.tensor_tensor(logit[:, h, k, :], logit[:, h, k, :], neg[:, :], ALU.add).then_inc(sub_done, 1)

            def pair(i, first):
                for h in range(2):
                    s = i * 2 + h
                    if not first:
                        pool.wait_ge(logit_done, s * TI - TI)
                    pool.sem_inc(passed, 1)
                    pool.tensor_copy(at[:, h, :], keep["shift_at"][:, :, :, :].rearrange("p b g t -> p (b g) t")[:, bass.ds(s, 1), :].rearrange("p s t -> p (s t)")).then_inc(staged, 1)
                    pool.tensor_copy(wt[:, h].rearrange("p t k -> p (t k)"), keep["shift_w"][:, :, :, :, :].rearrange("p b g t k -> p (b g) (t k)")[:, bass.ds(s, 1), :].rearrange("p s t -> p (s t)")).then_inc(staged, 1)
                    pool.wait_ge(staged, s * 2 + 2)
                    pool.sem_inc(passed, 1)

                    def gather(t):
                        if not first or h or t >= WB:
                            pool.wait_ge(x_done, s * TI + (t - WB + 1))
                            pool.sem_inc(passed, 1)
                        pool.indirect_dma_start(out=window[:, t % WB].rearrange("p u j -> p (u j)"), out_offset=None, in_=flat,
                                                in_offset=bass.IndirectOffsetOnAxis(ap=at[:, h, t:t + 1], axis=0)
                                                ).then_inc(gathered[t % WB], 16)

                    for t in range(TI):
                        for ahead in ISSUE[t]:
                            gather(ahead)
                        if t < LAG and not first:
                            subtract(s - 2, h, t + TI - LAG)
                        if t >= LAG and (not first or h):
                            subtract(s - 1, 1 - h, t - LAG)

            every_pair(pool, pair)
            last = 2 * PAIRS - 1
            for k in range(TI - LAG, TI):
                subtract(last - 1, 0, k)
            for k in range(TI):
                subtract(last, 1, k)

        @block.scalar
        def _(act):
            act.wait_ge(consts, 16)

            def spread_max(s):
                act.wait_ge(spread, s + 1)
                act.wait_ge(sub_done, s * TI)
                act.activation(neg[:, :], psM[:, :], ACT.Copy).then_inc(neg_ready, 1)

            def exps(s, h, k):
                act.wait_ge(sub_done, s * TI + (k + 1))
                act.activation(logit[:, h, k, :], logit[:, h, k, :], ACT.Exp).then_inc(p_done, 1)

            def take(s, h):
                act.wait_ge(pv_done, s * TI + TI)
                act.activation(raw[half(h), :], psO[half(h), :], ACT.Copy).then_inc(raw_ready, 1)
                act.activation(inverse[half(h), :], psO[half(1 - h), :], ACT.Ln).then_inc(raw_ready, 1)
                act.wait_ge(raw_ready, s * 2 + 2)
                act.activation(inverse[half(h), :], inverse[half(h), :], ACT.Exp, scale=-1.0).then_inc(inverse_ready, 1)

            def pair(i, first):
                for h in range(2):
                    s = i * 2 + h
                    act.wait_ge(staged, s * 2 + 2)

                    def across_left(t):
                        act.wait_ge(gathered[t % WB], s * (TI // WB * 16) + (t // WB + 1) * 16)
                        if not first or h or t >= WB:
                            act.wait_ge(logit_done, s * TI + (t - WB + 1))
                        act.activation(rowx[:, t % WB], window[:, t % WB, :, 0:W], ACT.Copy, scale=wt[:, h, t, 0:1]).then_inc(x0_done, 1)
                        if t in ON_PE:
                            act.activation(below[:, t % WB], ident[:, :], ACT.Copy, scale=wt[:, h, t, 3:4]).then_inc(below_ready, 1)

                    for t in range(TI):
                        for ahead in ISSUE[t]:
                            across_left(ahead)
                        if t == LAG and (not first or h):
                            if first:
                                act.wait_ge(spread, 1)
                                act.activation(neg[:, :], psM[:, :], ACT.Copy).then_inc(neg_ready, 1)
                            else:
                                spread_max(s - 1)
                        if t == LAG + 1 and not first:
                            take(s - 2, h)
                        if t < LAG and not first:
                            exps(s - 2, h, t + TI - LAG)
                        if t >= LAG and (not first or h):
                            exps(s - 1, 1 - h, t - LAG)

            every_pair(act, pair)
            last = 2 * PAIRS - 1
            for k in range(TI - LAG, TI):
                exps(last - 1, 0, k)
            spread_max(last)
            act.wait_ge(o_done, last - 1)
            take(last - 1, 0)
            for k in range(TI):
                exps(last, 1, k)
            act.wait_ge(o_done, last)
            take(last, 1)

        @block.tensor
        def _(pe):
            pe.wait_ge(consts, 16)
            pe.wait_ge(ones_set, 3)

            def turn_max(s, h, first):
                pe.wait_ge(most_done, s * (TI - 1) + (TI - 1))
                if not first:
                    pe.wait_ge(neg_ready, s)
                for k in range(TI):
                    mm = pe.transpose(psM[:, k * P:(k + 1) * P], most[:, h, k * P:(k + 1) * P], ident[:, :])
                mm.then_inc(turned, 1)

            def spread_max(s):
                pe.wait_ge(diag_ready, s + 1)
                dg = diag[:, :, :].rearrange("p t q -> p (t q)")
                for a in range(2):
                    mm = pe.matmul(psM[:, a * 512:(a + 1) * 512], ones[:, :], dg[:, a * 512:(a + 1) * 512], start=True, stop=True)
                mm.then_inc(spread, 1)

            def values(s, h, k, i, first):
                pe.wait_ge(p_done, s * TI + (k + 1))
                if k == 0:
                    pe.wait_ge(v_in[h], i * 16 + 16)
                    if not first:
                        pe.wait_ge(raw_ready, s * 2)
                for a in range(2):
                    mm = pe.matmul(psO[:, a * 512:(a + 1) * 512], val[:, h, k, :], logit[:, h, k, a * 512:(a + 1) * 512],
                                   start=k == 0, stop=k == TI - 1)
                mm.then_inc(pv_done, 1)

            def product(s, h, t, first):
                if not first or h or t >= 2:
                    pe.wait_ge(logit_done, s * TI + (t - 1))
                for a in range(2):
                    for z in range(2):
                        mm = pe.matmul(psS[:, t % 2, a * 512:(a + 1) * 512], ks[:, h, t * P:(t + 1) * P], qs[:, h, z, a * 512:(a + 1) * 512],
                                       start=z == 0, stop=z == 1 and t not in ON_PE, skip_group_check=True)
                if t not in ON_PE:
                    mm.then_inc(sum_ready, 1)

            def lower_row(s, t):
                pe.wait_ge(below_ready, s * len(ON_PE) + ON_PE.index(t) + 1)
                pe.wait_ge(x_done, s * TI + (t + 1))
                flat_row = rowx[:, t % WB].rearrange("p u j -> p (u j)")
                for a in range(2):
                    mm = pe.matmul(psS[:, t % 2, a * 512:(a + 1) * 512], below[:, t % WB, :], flat_row[:, W + a * 512:W + (a + 1) * 512],
                                   start=False, stop=True, skip_group_check=True)
                mm.then_inc(sum_ready, 1)

            def pair(i, first):
                for h in range(2):
                    s = i * 2 + h
                    pe.wait_ge(qk_in[h], i * 80 + 80)
                    for t in range(TI):
                        product(s, h, t, first)
                        if t < LAG and not first:
                            values(s - 2, h, t + TI - LAG, i - 1, False)
                        if not first or h:
                            if t == MAX_AT:
                                turn_max(s - 1, 1 - h, first)
                            if t == SPREAD_AT:
                                spread_max(s - 1)
                        if t in ON_PE:
                            lower_row(s, t)
                        if t >= LAG and (not first or h):
                            values(s - 1, 1 - h, t - LAG, i if h else i - 1, first)

            every_pair(pe, pair)
            last = 2 * PAIRS - 1
            for k in range(TI - LAG, TI):
                values(last - 1, 0, k, PAIRS - 1, False)
            turn_max(last, 1, False)
            spread_max(last)
            for k in range(TI):
                values(last, 1, k, PAIRS - 1, False)

        @block.vector
        def _(dve):
            dve.wait_ge(consts, 16)
            dve.tensor_scalar(minus[:, :], ident[:, :], -1.0, None, ALU.mult).then_inc(minus_set, 1)
            dve.wait_ge(minus_set, 1)

            def reduce_max(s):
                dve.wait_ge(turned, s + 1)
                dve.tensor_reduce(mx[:, :], psM[:, :].rearrange("p (t q) -> p t q", t=TI), AX.X, ALU.max).then_inc(mx_ready, 1)

            def diagonals(s):
                dve.wait_ge(mx_ready, s + 1)
                m3 = minus[:, :].rearrange("p (o q) -> p o q", o=1).broadcast_to([P, TI, P])
                dve.tensor_tensor(diag[:, :, :], m3, inner(mx[:, :], P), ALU.mult).then_inc(diag_ready, 1)

            def output(s, h, i):
                dve.wait_ge(inverse_ready, s + 1)
                dst = keep["o"][half(h), bass.ds(i // CH, 1), :, bass.ds(i % CH, 1), :, :].rearrange("p b f j t c -> p (b f j) (t c)")
                dve.tensor_tensor(dst, raw[half(h), :].rearrange("p (f n) -> p f n", f=2), inverse[half(h), :].rearrange("p (f n) -> p f n", f=2),
                                  ALU.mult).then_inc(o_done, 1)

            def across(s, h, t):
                dve.wait_ge(x0_done, s * TI + (t + 1))
                dve.scalar_tensor_tensor(rowx[:, t % WB], window[:, t % WB, :, 1:UW], wt[:, h, t, 1:2], rowx[:, t % WB],
                                         ALU.mult, ALU.add).then_inc(x_done, 1)

            def logits(s, h, t, fresh):
                n = s * TI + t
                dve.wait_ge(x_done, n + 1)
                dve.wait_ge(sum_ready, n + 1)
                if not fresh:
                    dve.wait_ge(pv_done, n - (2 * TI - 1))
                flat_row = rowx[:, t % WB].rearrange("p u j -> p (u j)")
                lt = logit[:, h, t, :]
                dve.scalar_tensor_tensor(lt, flat_row[:, 0:N], wt[:, h, t, 2:3], psS[:, t % 2, :],
                                         ALU.mult, ALU.add).then_inc(logit_done if t in ON_PE else y0_done, 1)
                if t in ON_DVE:
                    dve.wait_ge(y0_done, s * len(ON_DVE) + ON_DVE.index(t) + 1)
                    dve.scalar_tensor_tensor(lt, flat_row[:, W:W + N], wt[:, h, t, 3:4], lt, ALU.mult, ALU.add).then_inc(logit_done, 1)

            def running_max(s, h, t):
                dve.wait_ge(logit_done, s * TI + (t + 1))
                if t >= 2:
                    dve.wait_ge(most_done, s * (TI - 1) + (t - 1))
                so_far = logit[:, h, 0, :] if t == 1 else most[:, h, :]
                dve.tensor_tensor(most[:, h, :], so_far, logit[:, h, t, :], ALU.max).then_inc(most_done, 1)

            def pair(i, first):
                for h in range(2):
                    s = i * 2 + h
                    for t in range(TI):
                        across(s, h, t)
                        if t == MAX_AT + 1 and (not first or h):
                            reduce_max(s - 1)
                        if t >= 3:
                            running_max(s, h, t - 2)
                        elif t < 2 and (not first or h):
                            running_max(s - 1, 1 - h, t + TI - 2)
                        if t >= 1:
                            logits(s, h, t - 1, first)
                        elif not first or h:
                            logits(s - 1, 1 - h, TI - 1, True)
                        if t == MAX_AT + 1 and (not first or h):
                            diagonals(s - 1)
                        if t == LAG + 1 and not first:
                            output(s - 2, h, i - 1)

            every_pair(dve, pair)
            last = 2 * PAIRS - 1
            running_max(last, 1, TI - 2)
            logits(last, 1, TI - 1, False)
            running_max(last, 1, TI - 1)
            reduce_max(last)
            diagonals(last)
            output(last - 1, 0, PAIRS - 1)
            output(last, 1, PAIRS - 1)


ATTEND_ON_PE = (0, 1, 3, 5, 6, 7)


def join(nc, sem, d, keep):
    with ExitStack() as ctx:
        sb = lambda n, s, t=F32: ctx.enter_context(nc.sbuf_tensor(n, s, t))
        ident, wo, wg = sb("jo_ident", [P, P]), sb("jo_wo", [P, CH, NC]), sb("jo_wg", [P, CH, E])
        bo, bg = sb("jo_bo", [P, NC]), sb("jo_bg", [P, E])
        x = sb("jo_x", [P, 2, HT, NC])
        oT = sb("jo_oT", [P, CH, HN])
        stats, mv = sb("jo_stats", [P, HT, 6]), sb("jo_mv", [P, HT, 2])
        var, half, rstd = sb("jo_var", [P, HT]), sb("jo_half", [P, HT]), sb("jo_rstd", [P, HT])
        tn = sb("jo_tn", [P, 2, HT, NC])
        tnT = sb("jo_tnT", [P, CH, HN])
        earlier, ones, region = sb("jo_earlier", [P, P]), sb("jo_ones", [P, P]), sb("jo_region", [P, E])
        chosen, before, place = sb("jo_chosen", [P, HT, E]), sb("jo_before", [P, HT, E]), sb("jo_place", [P, HT, E])
        run = sb("jo_run", [P, HT + 1, E])
        pick, picked = sb("jo_pick", [P, HT, 2, E]), sb("jo_picked", [P, HT, 2, E])
        slot = sb("jo_slot", [P, HT, 2])
        at = sb("jo_at", [P, 2, HT, 2], I32)
        score, prob, top = sb("jo_score", [P, HT, E]), sb("jo_prob", [P, HT, E]), sb("jo_top", [P, HT, E])
        one = sb("jo_one", [P, HT])
        above = sb("jo_above", [P, HT, E, E])
        psT = ctx.enter_context(nc.psum_tensor("jo_psT", [P, CH, HN], F32))
        psY = ctx.enter_context(nc.psum_tensor("jo_psY", [P, 2, 512], F32))
        psG = ctx.enter_context(nc.psum_tensor("jo_psG", [P, HT, E], F32))
        psR = ctx.enter_context(nc.psum_tensor("jo_psR", [P, 2, HT, E], F32))
        (weights, rows_free, counted, half_set, above_set, oT_ready, y_done, t_ready, steps, var_ready, rstd_ready, tn_ready,
         tn_turned, tnT_ready, gate_done, score_ready, exp_done, chosen_ready, ranked, at_ready) = (sem("jo_" + n) for n in (
             "weights", "rows_free", "counted", "half_set", "above_set", "oT_ready", "y_done", "t_ready", "steps", "var_ready",
             "rstd_ready", "tn_ready", "tn_turned", "tnT_ready", "gate_done", "score_ready", "exp_done", "chosen_ready", "ranked", "at_ready"))
        x_in, rows_out = ([sem(f"jo_{n}{f}") for f in range(2)] for n in ("x_in", "rows_out"))
        passed = keep["passed"]
        block = ctx.enter_context(nc.Block())
        x_v = d["x"].rearrange("b h w c -> (b h w) c").rearrange("(s t p) c -> s p t c", p=P, t=HT)
        LOADS = 7 * 16

        @block.sync
        def _(sp):
            sp.dma_start(ident[:, :], d["c_ident"]).then_inc(weights, 16)
            sp.dma_start(wo[:, :, :], chunks(d["w_out"])).then_inc(weights, 16)
            sp.dma_start(wg[:, :, :], chunks(d["gate_w"])).then_inc(weights, 16)
            sp.dma_start(bo[:, :], rows(d["b_out"], P)).then_inc(weights, 16)
            sp.dma_start(bg[:, :], rows(d["gate_b"], P)).then_inc(weights, 16)
            sp.dma_start(earlier[:, :], d["c_earlier"]).then_inc(weights, 16)
            sp.dma_start(region[:, :], d["c_region"]).then_inc(weights, 16)
            sp.sem_inc(t_ready, 2 * HT)
            with sp.Fori(0, B) as b:
                for f in range(2):
                    sp.wait_ge(t_ready, b * 2 * HT + ((f + 1) * HT + 2))
                    sp.dma_start(x[:, f], x_v[bass.ds(b * 2 + f, 1)].rearrange("s p t c -> (s p) t c")).then_inc(x_in[f], 16)

        @block.gpsimd
        def _(pool):
            pool.memset(half[:, :], -0.5).then_inc(half_set, 1)
            pool.memset(above[:, :, :, :], 0.0).then_inc(above_set, 1)
            pool.memset(before[:, :, :], 0.0).then_inc(above_set, 1)
            pool.memset(run[:, :, :], 0.0).then_inc(above_set, 1)
            pool.memset(ones[:, :], 1.0).then_inc(above_set, 1)
            pool.sem_inc(rows_free, 2)
            pool.wait_ge(half_set, 1)
            with pool.Fori(0, B) as b:
                for f in range(2):
                    pool.wait_ge(var_ready, b * 2 + f + 1)
                    pool.tensor_tensor(rstd[:, :], var[:, :], half[:, :], ALU.pow).then_inc(rstd_ready, 1)
                    pool.wait_ge(at_ready, b * 2 + f + 1)
                    pool.sem_inc(passed, 1)
                    for t in range(HT):
                        for k in range(2):
                            pool.indirect_dma_start(out=d["rows"], out_offset=bass.IndirectOffsetOnAxis(ap=at[:, f, t, k:k + 1], axis=0),
                                                    in_=tn[:, f, t, :], in_offset=None).then_inc(rows_out[f], 16)
                for f in range(2):
                    pool.wait_ge(rows_out[f], b * (2 * HT * 16) + 2 * HT * 16)
                    pool.sem_inc(rows_free, 1)

        @block.scalar
        def _(act):
            act.wait_ge(weights, LOADS)
            act.sem_inc(y_done, HT)
            act.sem_inc(gate_done, HT)
            with act.Fori(0, B) as b:
                for f in range(2):
                    s = b * 2 + f
                    act.wait_ge(y_done, s * HT + HT)
                    act.sem_inc(passed, 1)
                    act.activation(oT[:, :, :], keep["o"][:, bass.ds(b, 1), f].rearrange("p b j t c -> p (b j) (t c)"), ACT.Copy).then_inc(oT_ready, 1)
                    act.wait_ge(tn_turned, s + 1)
                    act.wait_ge(gate_done, s * HT + HT)
                    act.activation(tnT[:, :, :], psT[:, :, :], ACT.Copy).then_inc(tnT_ready, 1)
                    act.wait_ge(score_ready, s + 2)
                    act.activation(prob[:, :, :], score[:, :, :], ACT.Exp).then_inc(exp_done, 1)

        @block.tensor
        def _(pe):
            pe.wait_ge(weights, LOADS)
            pe.sem_inc(tnT_ready, 1)
            pe.sem_inc(t_ready, 2)
            pe.sem_inc(score_ready, 1)
            pe.wait_ge(above_set, 4)
            with pe.Fori(0, B) as b:
                for f in range(2):
                    s = b * 2 + f
                    pe.wait_ge(oT_ready, s + 1)
                    for t in range(HT):
                        pe.wait_ge(t_ready, s * HT + (2 * HT + 1 + t))
                        for c in range(CH):
                            mm = pe.matmul(psY[:, t % 2, 0:NC], oT[:, c, t * P:(t + 1) * P], wo[:, c, :], start=c == 0, stop=c == CH - 1)
                        mm.then_inc(y_done, 1)
                    pe.wait_ge(tnT_ready, s + 1)
                    for t in range(HT):
                        pe.wait_ge(tn_ready, s * HT + (t + 1))
                        for j in range(CH):
                            mm = pe.transpose(psT[:, j, t * P:(t + 1) * P], tn[:, f, t, j * P:(j + 1) * P], ident[:, :])
                    mm.then_inc(tn_turned, 1)
                    pe.wait_ge(tnT_ready, s + 2)
                    pe.wait_ge(score_ready, s + 1)
                    for t in range(HT):
                        for c in range(CH):
                            mm = pe.matmul(psG[:, t, :], tnT[:, c, t * P:(t + 1) * P], wg[:, c, :], start=c == 0, stop=c == CH - 1)
                        mm.then_inc(gate_done, 1)
                    pe.wait_ge(chosen_ready, s + 1)
                    c2 = chosen[:, :, :].rearrange("p t e -> p (t e)")
                    pe.matmul(psR[:, 0].rearrange("p t e -> p (t e)"), earlier[:, :], c2, start=True, stop=True)
                    pe.matmul(psR[:, 1].rearrange("p t e -> p (t e)"), ones[:, :], c2, start=True, stop=True).then_inc(ranked, 1)

        @block.vector
        def _(dve):
            dve.wait_ge(weights, LOADS)
            dve.wait_ge(above_set, 4)
            with dve.Fori(0, B) as b:
                n = Count()

                def after():
                    dve.wait_ge(steps, b * JOIN_K + n.now)

                for f in range(2):
                    s = b * 2 + f
                    tile = lambda t: keep["acc"][:, bass.ds(b * TI + (f * HT + t), 1), :].rearrange("p o c -> p (o c)")
                    dve.wait_ge(x_in[f], b * 16 + 16)
                    b3 = bo[:, :].rearrange("p (o c) -> p o c", o=1).broadcast_to([P, HT, NC])
                    dve.tensor_tensor(x[:, f], x[:, f], b3, ALU.add).then_inc(steps, n.up())
                    after()
                    for t in range(HT):
                        dve.wait_ge(y_done, s * HT + (HT + t + 1))
                        dve.tensor_tensor(tile(t), psY[:, t % 2, 0:NC], x[:, f, t, :], ALU.add).then_inc(t_ready, 1)
                    dve.wait_ge(t_ready, s * HT + (3 * HT + 2))
                    dve.sem_inc(passed, 1)
                    for t in range(HT):
                        dve.bn_stats(stats[:, t, :], tile(t)).then_inc(steps, n.up())
                    after()
                    dve.sem_inc(passed, 1)
                    for t in range(HT):
                        dve.bn_aggr(mv[:, t, :], stats[:, t, :]).then_inc(steps, n.up())
                    after()
                    dve.tensor_scalar(var[:, :], mv[:, :, 1], 1e-5, None, ALU.add).then_inc(var_ready, 1)
                    dve.wait_ge(rstd_ready, s + 1)
                    dve.wait_ge(rows_free, s + 1)
                    for t in range(HT):
                        dve.tensor_scalar(tn[:, f, t, :], tile(t), mv[:, t, 0:1], rstd[:, t:t + 1], ALU.subtract, ALU.mult).then_inc(tn_ready, 1)
                    dve.wait_ge(gate_done, s * HT + 2 * HT)
                    g3 = bg[:, :].rearrange("p (o e) -> p o e", o=1).broadcast_to([P, HT, E])
                    dve.tensor_tensor(score[:, :, :], psG[:, :, :], g3, ALU.add).then_inc(steps, n.up())
                    after()
                    dve.tensor_reduce(one[:, :], score[:, :, :], AX.X, ALU.max).then_inc(steps, n.up())
                    after()
                    dve.tensor_tensor(score[:, :, :], score[:, :, :], inner(one[:, :], E), ALU.subtract).then_inc(score_ready, 1)
                    dve.wait_ge(exp_done, s + 1)
                    dve.tensor_reduce(one[:, :], prob[:, :, :], AX.X, ALU.add).then_inc(steps, n.up())
                    after()
                    dve.reciprocal(one[:, :], one[:, :]).then_inc(steps, n.up())
                    after()
                    dve.tensor_tensor(prob[:, :, :], prob[:, :, :], inner(one[:, :], E), ALU.mult).then_inc(steps, n.up())
                    after()
                    for e in range(E):
                        for lo, hi, op in ((0, e, ALU.is_ge), (e + 1, E, ALU.is_gt)):
                            if lo < hi:
                                dve.tensor_tensor(above[:, :, e, lo:hi], prob[:, :, lo:hi], prob[:, :, e:e + 1].broadcast_to([P, HT, hi - lo]), op
                                                  ).then_inc(steps, n.up())
                    after()
                    dve.tensor_reduce(top[:, :, :], above[:, :, :, :], AX.X, ALU.add).then_inc(steps, n.up())
                    after()
                    dve.tensor_scalar(chosen[:, :, :], top[:, :, :], 1.5, None, ALU.is_lt).then_inc(chosen_ready, 1)
                    dve.wait_ge(chosen_ready, s + 1)
                    dve.tensor_copy(before[:, :, 1:2], chosen[:, :, 0:1]).then_inc(steps, n.up())
                    dve.tensor_tensor(before[:, :, 2], chosen[:, :, 0], chosen[:, :, 1], ALU.add).then_inc(steps, n.up())
                    after()
                    dve.tensor_tensor(before[:, :, 3], before[:, :, 2], chosen[:, :, 2], ALU.add).then_inc(steps, n.up())
                    dve.tensor_tensor(top[:, :, :], chosen[:, :, :], prob[:, :, :], ALU.mult).then_inc(steps, n.up())
                    after()
                    dve.scalar_tensor_tensor(pick[:, :, 0, :], before[:, :, :], 0.5, chosen[:, :, :], ALU.is_lt, ALU.mult).then_inc(steps, n.up())
                    dve.tensor_reduce(one[:, :], top[:, :, :], AX.X, ALU.add).then_inc(steps, n.up())
                    after()
                    dve.tensor_tensor(pick[:, :, 1, :], chosen[:, :, :], pick[:, :, 0, :], ALU.subtract).then_inc(steps, n.up())
                    dve.tensor_scalar(one[:, :], one[:, :], 1e-9, None, ALU.add).then_inc(steps, n.up())
                    after()
                    dve.reciprocal(one[:, :], one[:, :]).then_inc(steps, n.up())
                    after()
                    dve.tensor_tensor(top[:, :, :], top[:, :, :], inner(one[:, :], E), ALU.mult).then_inc(steps, n.up())
                    after()
                    two = lambda v: bass.AP(tensor=v.tensor, offset=v.offset, ap=[v.ap[0], v.ap[1], [0, 2], v.ap[2]])
                    dve.tensor_tensor(picked[:, :, :, :], pick[:, :, :, :], two(top[:, :, :]), ALU.mult).then_inc(steps, n.up())
                    after()
                    dst = keep["gates"][:, bass.ds(b * TI + f * HT, HT), :]
                    dve.tensor_reduce(dst, picked[:, :, :, :], AX.X, ALU.add).then_inc(steps, n.up())
                    after()
                    dve.wait_ge(ranked, s + 1)
                    for t in range(HT):
                        dve.tensor_tensor(run[:, t + 1], run[:, t], psR[:, 1, t], ALU.add).then_inc(steps, n.up())
                        after()
                    dve.tensor_tensor(place[:, :, :], psR[:, 0], run[:, 0:HT], ALU.add).then_inc(steps, n.up())
                    after()
                    r3 = region[:, :].rearrange("p (o e) -> p o e", o=1).broadcast_to([P, HT, E])
                    dve.tensor_tensor(place[:, :, :], place[:, :, :], r3, ALU.add).then_inc(steps, n.up())
                    dve.tensor_copy(run[:, 0], run[:, HT]).then_inc(steps, n.up())
                    after()
                    dve.tensor_tensor(picked[:, :, :, :], pick[:, :, :, :], two(place[:, :, :]), ALU.mult).then_inc(steps, n.up())
                    after()
                    dve.tensor_reduce(slot[:, :, :], picked[:, :, :, :], AX.X, ALU.add).then_inc(steps, n.up())
                    after()
                    dve.tensor_scalar(slot[:, :, :], slot[:, :, :], float(E * QUEUE - 1), None, ALU.min).then_inc(steps, n.up())
                    after()
                    dve.tensor_copy(keep["slots"][:, bass.ds(b * TI + f * HT, HT), :], slot[:, :, :]).then_inc(steps, n.up())
                    dve.tensor_copy(at[:, f], slot[:, :, :]).then_inc(at_ready, 1)
                    dve.wait_ge(at_ready, s + 1)
                    after()
                assert n.now == JOIN_K, n.now
            dve.tensor_copy(keep["counts"][:, :], run[:, 0]).then_inc(counted, 1)


JOIN_K = 2 * 44


def plan(nc, sem, d, keep):
    with ExitStack() as ctx:
        sb = lambda n, s, t=F32: ctx.enter_context(nc.sbuf_tensor(n, s, t))
        v, fl, up = sb("pl_v", [P, E]), sb("pl_fl", [P, E]), sb("pl_up", [P, E])
        whole = sb("pl_whole", [P, E], I32)
        ends = sb("pl_ends", [P, E + 1])
        last = sb("pl_last", [P, 1])
        tile, past, skip, expert = (sb("pl_" + x, [P, SLOTS_T]) for x in ("tile", "past", "skip", "expert"))
        region = sb("pl_region", [P, E])
        tails = sb("pl_tails", [P, E], I32)
        jump, step = sb("pl_jump", [P, E]), sb("pl_step", [P, E - 1])
        beyond, row = sb("pl_beyond", [P, NT, 2]), sb("pl_row", [P, NT, 2])
        zero = sb("pl_zero", [P, TN // P, NC])
        loaded, steps, zeroed, tails_ready, tails_out = (sem("pl_" + n) for n in ("loaded", "steps", "zeroed", "tails_ready", "tails_out"))
        block = ctx.enter_context(nc.Block())

        @block.gpsimd
        def _(pool):
            pool.memset(zero[:, :, :], 0.0).then_inc(zeroed, 1)

        @block.sync
        def _(sp):
            sp.dma_start(tile[:, :], d["c_tile"]).then_inc(loaded, 16)
            sp.dma_start(region[:, :], d["c_region"]).then_inc(loaded, 16)
            sp.wait_ge(zeroed, 1)
            sp.wait_ge(tails_ready, 1)
            for e in range(E):
                tail = sp.value_load(tails[0:1, e:e + 1], min_val=e * QUEUE, max_val=e * QUEUE + QUEUE - TN)
                sp.dma_start(d["rows"][bass.ds(tail, TN), :].rearrange("(m p) c -> p m c", p=P), zero[:, :, :]).then_inc(tails_out, 16)
            sp.wait_ge(tails_out, 16 * E)

        @block.vector
        def _(dve):
            n = Count()

            def after():
                dve.wait_ge(steps, n.now)

            dve.wait_ge(loaded, 32)
            dve.tensor_scalar(v[:, :], keep["counts"][:, :], 1.0 / TN, float(TN - 1) / TN, ALU.mult, ALU.add).then_inc(steps, n.up())
            dve.tensor_tensor(up[:, :], keep["counts"][:, :], region[:, :], ALU.add).then_inc(steps, n.up())
            dve.memset(ends[:, 0:1], 0.0).then_inc(steps, n.up())
            after()
            dve.tensor_copy(tails[:, :], up[:, :]).then_inc(tails_ready, 1)
            dve.tensor_copy(whole[:, :], v[:, :]).then_inc(steps, n.up())
            after()
            dve.tensor_copy(fl[:, :], whole[:, :]).then_inc(steps, n.up())
            after()
            dve.wait_ge(tails_ready, 1)
            dve.tensor_tensor(up[:, :], fl[:, :], v[:, :], ALU.is_gt).then_inc(steps, n.up())
            after()
            dve.tensor_tensor(fl[:, :], fl[:, :], up[:, :], ALU.subtract).then_inc(steps, n.up())
            after()
            for e in range(E):
                dve.tensor_tensor(ends[:, e + 1:e + 2], ends[:, e:e + 1], fl[:, e:e + 1], ALU.add).then_inc(steps, n.up())
                after()
            dve.tensor_scalar(last[:, :], ends[:, E:E + 1], -1.0, None, ALU.add).then_inc(steps, n.up())
            after()
            dve.tensor_scalar(tile[:, :], tile[:, :], last[:, 0:1], None, ALU.min).then_inc(steps, n.up())
            dve.memset(expert[:, :], 0.0).then_inc(steps, n.up())
            dve.memset(skip[:, :], 0.0).then_inc(steps, n.up())
            after()
            for e in range(E - 1):
                dve.tensor_scalar(past[:, :], tile[:, :], ends[:, e + 1:e + 2], None, ALU.is_ge).then_inc(steps, n.up())
                after()
                dve.tensor_tensor(expert[:, :], expert[:, :], past[:, :], ALU.add).then_inc(steps, n.up())
                dve.scalar_tensor_tensor(skip[:, :], past[:, :], fl[:, e:e + 1], skip[:, :], ALU.mult, ALU.add).then_inc(steps, n.up())
                after()
            dve.tensor_tensor(skip[:, :], tile[:, :], skip[:, :], ALU.subtract).then_inc(steps, n.up())
            dve.tensor_copy(keep["expert"][:, :], expert[:, :]).then_inc(steps, n.up())
            after()
            dve.tensor_scalar(skip[:, :], skip[:, :], float(TN), None, ALU.mult).then_inc(steps, n.up())
            after()
            dve.scalar_tensor_tensor(skip[:, :], expert[:, :], float(QUEUE), skip[:, :], ALU.mult, ALU.add).then_inc(steps, n.up())
            after()
            dve.tensor_copy(keep["start"][:, :], skip[:, :]).then_inc(steps, n.up())
            dve.scalar_tensor_tensor(jump[:, :], ends[:, 0:E], float(TN), region[:, :], ALU.mult, ALU.subtract).then_inc(steps, n.up())
            dve.tensor_copy(row[:, :, :], keep["slots"][:, :, :]).then_inc(steps, n.up())
            after()
            dve.tensor_tensor(step[:, :], jump[:, 1:E], jump[:, 0:E - 1], ALU.subtract).then_inc(steps, n.up())
            after()
            for e in range(1, E):
                dve.tensor_scalar(beyond[:, :, :], keep["slots"][:, :, :], float(e * QUEUE), None, ALU.is_ge).then_inc(steps, n.up())
                after()
                dve.scalar_tensor_tensor(row[:, :, :], beyond[:, :, :], step[:, e - 1:e], row[:, :, :], ALU.mult, ALU.add).then_inc(steps, n.up())
                after()
            dve.tensor_copy(keep["result_at"][:, :, :], row[:, :, :]).then_inc(steps, n.up())
            after()


def experts(nc, sem, d, keep):
    TM = TN // P
    R = 4
    HB = 2
    YAT = 3 + R
    XAT = 6
    with ExitStack() as ctx:
        sb = lambda n, s, t=F32: ctx.enter_context(nc.sbuf_tensor(n, s, t))
        raw1, raw2 = sb("ex_raw1", [P, R, CH, P]), sb("ex_raw2", [P, R, NC])
        w1, w2 = sb("ex_w1", [P, R, 2, CH, P], F32R), sb("ex_w2", [P, R, 2, NC], F32R)
        xr = sb("ex_xr", [P, 2, TM, NC])
        xT = sb("ex_xT", [P, 2, 2, CH, TN], F32R)
        h, hp = sb("ex_h", [P, R, TN]), sb("ex_hp", [P, R, 2, TN], F32R)
        b1, b2 = sb("ex_b1", [P, E, KH]), sb("ex_b2", [P, E, NC])
        bias1, bias2 = sb("ex_bias1", [P, 2, KH]), sb("ex_bias2", [P, 2, NC])
        y = sb("ex_y", [P, 2, TM, NC])
        ident = sb("ex_ident", [P, P])
        psX = ctx.enter_context(nc.psum_tensor("ex_psX", [P, 2, 512], F32))
        psH = ctx.enter_context(nc.psum_tensor("ex_psH", [P, HB, 512], F32))
        psY = ctx.enter_context(nc.psum_tensor("ex_psY", [P, TM, 512], F32))
        (weights, split_done, h_done, gelu_done, hp_ready, y_done, y_ready, x_turned, x_high, x_low) = (sem("ex_" + n) for n in (
            "weights", "split_done", "h_done", "gelu_done", "hp_ready", "y_done", "y_ready", "x_turned", "x_high", "x_low"))
        raw_in = [sem(f"ex_raw_in{r}") for r in range(R)]
        x_in, b_in, y_out = ([sem(f"ex_{n}{u}") for u in range(2)] for n in ("x_in", "b_in", "y_out"))
        passed = keep["passed"]
        block = ctx.enter_context(nc.Block())
        LOADS = 3 * 16
        PASSES = ((0, 0), (0, 1), (1, 0))

        def every_two(eng, two):
            assert TILES % 2 == 1
            two(0, True)
            with eng.Fori(1, TILES // 2) as i:
                two(i, False)
            two(TILES // 2, False, True)

        def load_value(eng, name, n, most):
            return eng.value_load(keep[name][0:1, bass.ds(n, 1)], min_val=0, max_val=most)

        @block.sync
        def _(sp):
            sp.dma_start(b1[:, :, :], d["b1"].rearrange("e (k p) -> p e k", p=P), allow_slow_non_contiguous=True).then_inc(weights, 16)
            sp.dma_start(b2[:, :, :].rearrange("p e c -> p (e c)"), rows(d["b2"].rearrange("e c -> (e c)"), P)).then_inc(weights, 16)
            sp.dma_start(ident[:, :], d["c_ident"]).then_inc(weights, 16)
            w1_v = d["w1"].rearrange("e (c p) (k n) -> k e p c n", p=P, n=P)
            w2_v = d["w2"].rearrange("e (k p) c -> k e p c", p=P)
            results = d["results"].rearrange("(n m p) c -> n m p c", m=TM, p=P)

            def store(n, u):
                sp.wait_ge(y_ready, n * TM + TM)
                sp.dma_start(results[bass.ds(n, 1)].rearrange("n m p c -> p (n m) c"), y[:, u]).then_inc(y_out[u], 16)

            def two(i, first, last=False):
                for u in range(1 if last else 2):
                    n = i * 2 + u
                    e = load_value(sp, "expert", n, E - 1)
                    for k in range(KH):
                        if k == YAT and (not first or u):
                            store(n - 1, 1 - u)
                        if not first or u or k >= R:
                            sp.wait_ge(split_done, n * 4 * KH + 4 * (k - R + 1))
                        sp.dma_start(raw1[:, k % R], w1_v[k, bass.ds(e, 1)].rearrange("e p c n -> (e p) c n")).then_inc(raw_in[k % R], 16)
                        sp.dma_start(raw2[:, k % R], w2_v[k, bass.ds(e, 1)].rearrange("e p c -> (e p) c")).then_inc(raw_in[k % R], 16)

            every_two(sp, two)
            store(TILES - 1, 0)
            sp.wait_ge(y_out[0], (TILES // 2 + 2) * 16)
            sp.wait_ge(y_out[1], (TILES // 2 + 1) * 16)

        @block.gpsimd
        def _(pool):
            pool.wait_ge(weights, LOADS)

            def load(n, u):
                e = load_value(pool, "expert", n, E - 1)
                start = load_value(pool, "start", n, E * QUEUE - TN)
                pool.dma_start(xr[:, u], d["rows"][bass.ds(start, TN), :].rearrange("(m p) c -> p m c", p=P)).then_inc(x_in[u], 16)
                pool.dma_start(bias1[:, u, :], b1[:, bass.ds(e, 1), :].rearrange("p e k -> p (e k)")).then_inc(b_in[u], 16)
                pool.dma_start(bias2[:, u, :], b2[:, bass.ds(e, 1), :].rearrange("p e c -> p (e c)")).then_inc(b_in[u], 16)

            def two(i, first, last=False):
                for u in range(0 if last else 2):
                    n = i * 2 + u
                    if not first or u:
                        pool.wait_ge(x_turned, n * CH)
                        pool.wait_ge(y_ready, n * TM)
                        pool.wait_ge(gelu_done, n * KH)
                        pool.sem_inc(passed, 1)
                    load(n + 1, 1 - u)

            load(0, 0)
            every_two(pool, two)

        @block.scalar
        def _(act):
            def high(n, u, c, fresh):
                act.wait_ge(x_turned, n * CH + (c + 1))
                if not fresh:
                    act.wait_ge(h_done, n * KH - KH)
                act.activation(xT[:, u, 0, c, :], psX[:, (u + c) % 2, 0:TN], ACT.Copy).then_inc(x_high, 1)

            def two(i, first, last=False):
                for u in range(1 if last else 2):
                    n = i * 2 + u
                    act.wait_ge(b_in[u], i * 32 + 32)
                    for k in range(KH):
                        act.wait_ge(h_done, n * KH + (k + 1))
                        if not first or u or k >= R:
                            act.wait_ge(hp_ready, n * 2 * KH + 2 * (k - R + 1))
                        act.activation(h[:, k % R, :], psH[:, k % HB, 0:TN], ACT.Gelu, bias=bias1[:, u, k:k + 1]).then_inc(gelu_done, 1)
                        if XAT <= k < XAT + CH and not last:
                            high(n + 1, 1 - u, k - XAT, first and not u)

            for c in range(CH):
                high(0, 0, c, True)
            every_two(act, two)

        @block.tensor
        def _(pe):
            pe.wait_ge(weights, LOADS)

            def turn(n, u, c, seen, early):
                if c == 0:
                    pe.wait_ge(x_in[u], seen)
                if not early:
                    pe.wait_ge(x_low, n * CH + (c - 1))
                for m in range(TM):
                    mm = pe.transpose(psX[:, (u + c) % 2, m * P:(m + 1) * P], xr[:, u, m, c * P:(c + 1) * P], ident[:, :])
                mm.then_inc(x_turned, 1)

            def down(n, k, first):
                pe.wait_ge(hp_ready, n * 2 * KH + 2 * (k + 1))
                if k == 0 and not first:
                    pe.wait_ge(y_ready, n * TM)
                for m in range(TM):
                    for a, c in PASSES:
                        mm = pe.matmul(psY[:, m, 0:NC], hp[:, k % R, a, m * P:(m + 1) * P], w2[:, k % R, c, :],
                                       start=k == 0 and (a, c) == (0, 0), stop=k == KH - 1 and a == 1)
                mm.then_inc(y_done, 1)

            def two(i, first, last=False):
                for u in range(1 if last else 2):
                    n = i * 2 + u
                    pe.wait_ge(x_low, n * CH + CH)
                    for k in range(KH):
                        pe.wait_ge(split_done, n * 4 * KH + 4 * (k + 1))
                        if not first or u or k >= HB:
                            pe.wait_ge(gelu_done, n * KH + (k - HB + 1))
                        for c in range(CH):
                            for a, z in PASSES:
                                mm = pe.matmul(psH[:, k % HB, 0:TN], w1[:, k % R, a, c, :], xT[:, u, z, c, :],
                                               start=c == 0 and (a, z) == (0, 0), stop=c == CH - 1 and a == 1)
                        mm.then_inc(h_done, 1)
                        if k >= 2:
                            down(n, k - 2, first and not u)
                        elif not first or u:
                            down(n - 1, KH - 2 + k, False)
                        if XAT <= k < XAT + CH and not last:
                            turn(n + 1, 1 - u, k - XAT, i * 16 + u * 16 + 16, False)

            for c in range(CH):
                turn(0, 0, c, 16, c < 2)
            every_two(pe, two)
            for k in (KH - 2, KH - 1):
                down(TILES - 1, k, False)

        @block.vector
        def _(dve):
            for u in range(2):
                dve.sem_inc(y_out[u], 16)

            def low(n, u, c):
                dve.wait_ge(x_high, n * CH + (c + 1))
                dve.tensor_tensor(xT[:, u, 1, c, :], psX[:, (u + c) % 2, 0:TN], xT[:, u, 0, c, :].bitcast(F32), ALU.subtract).then_inc(x_low, 1)

            def split(n, k, early):
                dve.wait_ge(raw_in[k % R], n * (KH // R * 32) + (k // R + 1) * 32)
                if not early:
                    dve.wait_ge(y_done, n * KH + (k - R + 1))
                s = n * 4 * KH + 4 * k
                dve.tensor_copy(w1[:, k % R, 0], raw1[:, k % R]).then_inc(split_done, 1)
                dve.tensor_copy(w2[:, k % R, 0], raw2[:, k % R]).then_inc(split_done, 1)
                dve.wait_ge(split_done, s + 1)
                dve.tensor_tensor(w1[:, k % R, 1], raw1[:, k % R], w1[:, k % R, 0].bitcast(F32), ALU.subtract).then_inc(split_done, 1)
                dve.wait_ge(split_done, s + 2)
                dve.tensor_tensor(w2[:, k % R, 1], raw2[:, k % R], w2[:, k % R, 0].bitcast(F32), ALU.subtract).then_inc(split_done, 1)

            def hidden(n, k, early):
                dve.wait_ge(gelu_done, n * KH + (k + 1))
                if not early:
                    dve.wait_ge(y_done, n * KH + (k - R + 1))
                dve.tensor_copy(hp[:, k % R, 0, :], h[:, k % R, :]).then_inc(hp_ready, 1)
                dve.wait_ge(hp_ready, n * 2 * KH + (2 * k + 1))
                dve.tensor_tensor(hp[:, k % R, 1, :], h[:, k % R, :], hp[:, k % R, 0, :].bitcast(F32), ALU.subtract).then_inc(hp_ready, 1)

            def result(n, u, count):
                dve.wait_ge(y_done, n * KH + KH)
                dve.wait_ge(y_out[u], count)
                for m in range(TM):
                    dve.tensor_tensor(y[:, u, m, :], psY[:, m, 0:NC], bias2[:, u, :], ALU.add).then_inc(y_ready, 1)

            def two(i, first, last=False):
                for u in range(1 if last else 2):
                    n = i * 2 + u
                    dve.wait_ge(b_in[u], i * 32 + 32)
                    for k in range(KH):
                        early = first and not u and k < R
                        split(n, k, early)
                        if k == 2 and (not first or u):
                            result(n - 1, 1 - u, (i * 16 + 16) if u else i * 16)
                        if k >= 2:
                            hidden(n, k - 2, first and not u and k - 2 < R)
                        elif not first or u:
                            hidden(n - 1, KH - 2 + k, False)
                        if XAT < k <= XAT + CH and not last:
                            low(n + 1, 1 - u, k - XAT - 1)

            for c in range(CH):
                low(0, 0, c)
            every_two(dve, two)
            for k in (KH - 2, KH - 1):
                hidden(TILES - 1, k, False)
            result(TILES - 1, 0, TILES // 2 * 16 + 16)


def combine(nc, sem, d, keep):
    with ExitStack() as ctx:
        sb = lambda n, s, t=F32: ctx.enter_context(nc.sbuf_tensor(n, s, t))
        at = sb("co_at", [P, 2, HT, 2], I32)
        gate = sb("co_gate", [P, 2, HT, 2])
        r = sb("co_r", [P, 2, HT, 2, NC])
        part = sb("co_part", [P, 2, HT, NC])
        staged, part_done, sum_done = (sem("co_" + n) for n in ("staged", "part_done", "sum_done"))
        taken = [[sem(f"co_taken{f}{t}") for t in range(HT)] for f in range(2)]
        written = [sem(f"co_written{f}") for f in range(2)]
        passed = keep["passed"]
        block = ctx.enter_context(nc.Block())
        out_v = d["out"].rearrange("b h w c -> (b h w) c").rearrange("(t p) c -> t p c", p=P)

        @block.gpsimd
        def _(pool):
            pool.sem_inc(sum_done, 2 * HT)
            with pool.Fori(0, B) as b:
                for f in range(2):
                    pool.wait_ge(sum_done, b * 2 * HT + (f + 1) * HT)
                    pool.sem_inc(passed, 1)
                    pool.tensor_copy(at[:, f], keep["result_at"][:, bass.ds(b * TI + f * HT, HT), :]).then_inc(staged, 1)
                    pool.tensor_copy(gate[:, f], keep["gates"][:, bass.ds(b * TI + f * HT, HT), :]).then_inc(staged, 1)
                    pool.wait_ge(staged, b * 4 + 2 * f + 2)
                    pool.sem_inc(passed, 1)
                    for t in range(HT):
                        for k in range(2):
                            pool.indirect_dma_start(out=r[:, f, t, k, :], out_offset=None, in_=d["results"],
                                                    in_offset=bass.IndirectOffsetOnAxis(ap=at[:, f, t, k:k + 1], axis=0)
                                                    ).then_inc(taken[f][t], 16)

        @block.vector
        def _(dve):
            for f in range(2):
                dve.sem_inc(written[f], 16 * HT)
            with dve.Fori(0, B) as b:
                for f in range(2):
                    for t in range(HT):
                        s = b * 2 * HT + f * HT + t
                        dve.wait_ge(taken[f][t], b * 32 + 32)
                        if t == 0:
                            dve.wait_ge(written[f], b * (16 * HT) + 16 * HT)
                        acc = keep["acc"][:, bass.ds(s, 1), :].rearrange("p o c -> p (o c)")
                        dve.scalar_tensor_tensor(part[:, f, t, :], r[:, f, t, 0, :], gate[:, f, t, 0:1], acc, ALU.mult, ALU.add).then_inc(part_done, 1)
                        dve.wait_ge(part_done, s + 1)
                        dve.scalar_tensor_tensor(part[:, f, t, :], r[:, f, t, 1, :], gate[:, f, t, 1:2], part[:, f, t, :], ALU.mult, ALU.add).then_inc(sum_done, 1)

        @block.sync
        def _(sp):
            with sp.Fori(0, B) as b:
                for f in range(2):
                    for t in range(HT):
                        s = b * 2 * HT + f * HT + t
                        sp.wait_ge(sum_done, s + (2 * HT + 1))
                        sp.dma_start(out_v[bass.ds(s, 1)].rearrange("o p c -> (o p) c"), part[:, f, t, :]).then_inc(written[f], 16)
            for f in range(2):
                sp.wait_ge(written[f], (B + 1) * HT * 16)


NAMES = {"x": "x", "w_q": "L0_conv_w_q", "b_q": "L0_conv_b_q", "w_off0": "L0_conv_w_off0", "b_off0": "L0_conv_b_off0",
         "ln_g": "L0_conv_ln_g", "ln_b": "L0_conv_ln_b", "w_offp": "L0_conv_w_offp", "w_k": "L0_conv_w_k",
         "b_k": "L0_conv_b_k", "w_v": "L0_conv_w_v", "b_v": "L0_conv_b_v", "w_out": "L0_conv_w_out",
         "b_out": "L0_conv_b_out", "rpe": "L0_conv_rpe", "gate_w": "L0_ffn_gate_w", "gate_b": "L0_ffn_gate_b",
         "w1": "L0_ffn_w1", "b1": "L0_ffn_b1", "w2": "L0_ffn_w2", "b2": "L0_ffn_b2"}


def build(nc, d, out):
    def scratch(name, shape, dt=F32):
        d[name] = nc.dram_tensor("s_" + name, shape, dt, kind="Internal").ap()
    scratch("shifts", (G, SN, UN, UW))
    scratch("quads", (B * G, QY, QX, 2, GC))
    scratch("q_scr", (PAIRS, 2, P, N))
    scratch("k_scr", (PAIRS, 2, P, N))
    scratch("v_scr", (PAIRS, TI, P, P))
    scratch("rows", (E * QUEUE, NC))
    scratch("results", (TILES * TN, NC))
    d["out"] = out
    with ExitStack() as ctx:
        sem = lambda name: ctx.enter_context(nc.semaphore(name))
        table(nc, sem, d)
        keep = {"passed": sem("passed")}
        with ExitStack() as held:
            for name, shape, dt in (("shift_at", [P, B, G, TI], I32), ("shift_w", [P, B, G, TI, 4], F32)):
                keep[name] = held.enter_context(nc.sbuf_tensor(name, shape, dt))
            with nc.sbuf_tensor("quad_at", [P, B, G, TI], I32) as keep["quad_at"], nc.sbuf_tensor("quad_w", [P, B, G, TI, 4], F32) as keep["quad_w"]:
                with nc.sbuf_tensor("q_pad", [P, CH, B, H + 2, W + 2], F32) as keep["q_pad"]:
                    mixer_q(nc, sem, d, keep)
                    offsets(nc, sem, d, keep)
                keys(nc, sem, d, keep)
            o_all = held.enter_context(nc.sbuf_tensor("o_all", [P, B, 2, CH, HT, P], F32))
            keep["o"] = o_all
            keep["acc"] = o_all[:, :, :, :, :, :].rearrange("p b f j t c -> p (b f j t c)").rearrange("p (t c) -> p t c", c=NC)
            attend(nc, sem, d, keep)
            keep["gates"] = held.enter_context(nc.sbuf_tensor("gates", [P, NT, 2], F32))
            keep["slots"] = held.enter_context(nc.sbuf_tensor("slots", [P, NT, 2], F32))
            keep["counts"] = held.enter_context(nc.sbuf_tensor("counts", [P, E], F32))
            join(nc, sem, d, keep)
            for name, shape, dt in (("expert", [P, SLOTS_T], I32), ("start", [P, SLOTS_T], I32),
                                    ("result_at", [P, NT, 2], I32)):
                keep[name] = held.enter_context(nc.sbuf_tensor(name, shape, dt))
            plan(nc, sem, d, keep)
            experts(nc, sem, d, keep)
            combine(nc, sem, d, keep)


def kernel(**inputs):
    import concourse.bacc as bacc
    from concourse.bass_utils import run_bass_kernel_spmd

    nc = bacc.Bacc("TRN2", target_bir_lowering=False, num_devices=1)
    arrays = {"in_" + n: np.ascontiguousarray(inputs[long]) for n, long in NAMES.items()}
    arrays |= {"in_" + n: a for n, a in constants().items()}
    d = {n[3:]: nc.dram_tensor(n, a.shape, mybir.dt.from_np(a.dtype), kind="ExternalInput").ap() for n, a in arrays.items()}
    out = nc.dram_tensor("out_0", (B, H, W, NC), F32, kind="ExternalOutput").ap()
    build(nc, d, out)
    r = run_bass_kernel_spmd(nc, [arrays], core_ids=[0])
    return r.results[0]["out_0"]
```

```python
from contextlib import ExitStack

import numpy as np
import concourse.bass as bass
from concourse import mybir
from concourse.alu_op_type import AluOpType as ALU

ACT = mybir.ActivationFunctionType
AX = mybir.AxisListType
F32 = mybir.dt.float32
F32R = mybir.dt.float32r
I32 = mybir.dt.int32

P = 128
B, H, W, NC = 4, 32, 32, 384
CH = NC // P
G, GC = 6, 64
N = H * W
TI = N // P
HT = TI // 2
HN = N // 2
HROWS = H // 2
NT = B * TI
PAIRS = B * G // 2
E, HID = 4, 4 * NC
KH = HID // P
SCALE = GC ** -0.5
SLO, SN = 1 - (W - 1 + W // 2), W // 2 + 1 - (1 - (W - 1 + W // 2)) + 1
UN = SN + W
UW = W + 1
RY = (UN + SLO) // 2
TN = 512
QUEUE = NT * P + TN
TILES = (2 * NT * P + E * (TN - 1)) // TN
SLOTS_T = TILES
QY, QX = H + 1, W + 2

PASSES = ((0, 0), (0, 1), (1, 0))


def constants():
    up = np.zeros((RY, UN), np.float32)
    for y in range(1, RY + 1):
        for d, w in ((-1, 0.5), (0, 1.0), (1, 0.5)):
            if 2 * y + d - SLO < UN:
                up[y - 1, 2 * y + d - SLO] = w
    p = np.arange(P)
    cell = np.zeros((P, TI, 2), np.float32)
    for t in range(TI):
        cell[:, t, 0] = p % W
        cell[:, t, 1] = t * (P // W) + p // W
    base = np.zeros((P, 2, B * G), np.float32)
    base[:, 0] = np.arange(B * G) * (QY * QX * 2 * GC)
    base[:, 1] = (np.arange(B * G) % G) * (SN * UN * UW)
    earlier = np.triu(np.ones((P, P), np.float32), 1)
    region = np.broadcast_to(np.arange(E, dtype=np.float32) * QUEUE, (P, E))
    tile = np.broadcast_to(np.arange(SLOTS_T, dtype=np.float32), (P, SLOTS_T))
    return {"c_earlier": earlier, "c_region": np.ascontiguousarray(region), "c_tile": np.ascontiguousarray(tile),
            "c_ident": np.eye(P, dtype=np.float32), "c_up": up, "c_cell": cell, "c_base": base}


def chunks(w):
    return w.rearrange("(c p) n -> p c n", p=P)


def rows(v, n):
    return bass.AP(tensor=v.tensor, offset=v.offset, ap=[[0, n], [1, v.shape[0]]])


def inner(ap, k):
    return bass.AP(tensor=ap.tensor, offset=ap.offset, ap=[*ap.ap, [0, k]])



class Count:

    def __init__(self):
        self.now = 0

    def up(self, by=1):
        self.now += by
        return by


def every_half(eng, ahead, behind):
    ahead(0, 0)
    ahead(0, 1)
    behind(0, 0)
    with eng.Fori(1, B) as b:
        ahead(b, 0)
        behind(b - 1, 1)
        ahead(b, 1)
        behind(b, 0)
    behind(B - 1, 1)


def table(nc, sem, d, keep):
    with ExitStack() as ctx:
        sb = lambda n, s, t=F32: ctx.enter_context(nc.sbuf_tensor(n, s, t))
        rpe = sb("tb_rpe", [RY, RY, G])
        up = sb("tb_up", [RY, UN])
        wide = sb("tb_wide", [RY, G, UN])
        full, zero = keep["table"], keep["zero"]
        ps = ctx.enter_context(nc.psum_tensor("tb_ps", [UN, 2, 512], F32))
        loaded, cleared, halves, widened, product, copied, zeroed = (
            sem("tb_" + x) for x in ("loaded", "cleared", "halves", "widened", "product", "copied", "zeroed"))
        stored = keep["table_out"]
        block = ctx.enter_context(nc.Block())
        first = 2 - SLO

        @block.sync
        def _(sp):
            sp.dma_start(rpe[:, :, :], d["rpe"][0:RY, 0:RY, :]).then_inc(loaded, 16)
            sp.dma_start(up[:, :], d["c_up"]).then_inc(loaded, 16)
            quads = d["quads"].rearrange("n y x r c -> (n y) x (r c)")
            sp.wait_ge(zeroed, 1)
            nrow = B * G * QY
            z = zero[0:nrow // 8, 0:8 * 2 * GC].rearrange("p (a c) -> p a c", a=8)
            for x in (0, QX - 1):
                dst = bass.AP(tensor=quads.tensor, offset=x * 2 * GC,
                              ap=[[8 * QX * 2 * GC, nrow // 8], [QX * 2 * GC, 8], [1, 2 * GC]])
                sp.dma_start(dst, z).then_inc(stored, 16)
            half_row = W // 2
            z = zero[0:B * G, 0:half_row * GC].rearrange("p (a c) -> p a c", a=half_row)
            for off in (2 * GC, (QY - 1) * QX * 2 * GC + 2 * GC + GC):
                for f in range(2):
                    dst = bass.AP(tensor=quads.tensor, offset=off + f * half_row * 2 * GC,
                                  ap=[[QY * QX * 2 * GC, B * G], [2 * GC, half_row], [1, GC]])
                    sp.dma_start(dst, z).then_inc(stored, 16)
            sp.wait_ge(copied, 1)
            for h in range(G):
                src = full[:, h, :]
                src = bass.AP(tensor=src.tensor, offset=src.offset, ap=[src.ap[0], [1, SN], [1, UW]])
                sp.dma_start(d["shifts"][h].rearrange("f u j -> u f j"), src).then_inc(stored, 16)

        @block.gpsimd
        def _(pool):
            pool.memset(zero[:, :], 0.0).then_inc(zeroed, 1)

        @block.vector
        def _(dve):
            dve.memset(wide[:, :, :], 0.0).then_inc(cleared, 1)
            dve.wait_ge(loaded, 32)
            dve.wait_ge(cleared, 1)
            r = rpe[:, :, :].rearrange("y x h -> y h x")
            dve.tensor_copy(wide[:, :, first::2], r[:, :, 0:RY - 1]).then_inc(widened, 1)
            dve.tensor_scalar(wide[:, :, first - 1:first], r[:, :, 0:1], 0.5, None, ALU.mult).then_inc(widened, 1)
            dve.tensor_tensor(wide[:, :, first + 1::2], r[:, :, 0:RY - 1], r[:, :, 1:RY], ALU.add).then_inc(halves, 1)
            dve.wait_ge(halves, 1)
            dve.tensor_scalar(wide[:, :, first + 1::2], wide[:, :, first + 1::2], 0.5, None, ALU.mult).then_inc(widened, 1)
            dve.wait_ge(product, 1)
            dve.tensor_copy(full[:, :, :].rearrange("p (a h) u -> p a (h u)", a=2), ps[:, :, 0:G // 2 * UN]).then_inc(copied, 1)

        @block.tensor
        def _(pe):
            pe.wait_ge(loaded, 32)
            pe.wait_ge(widened, 3)
            w = wide[:, :, :].rearrange("p (a h) u -> p a (h u)", a=2)
            for a in range(2):
                mm = pe.matmul(ps[:, a, 0:G // 2 * UN], up[:, :], w[:, a, :], start=True, stop=True)
            mm.then_inc(product, 1)


def write_quads(pool, d, b, r, done):
    src = d["xn_scr"].rearrange("(b y x) (g c) -> b g y x c", b=B, x=W, g=G)
    dst = d["quads"].rearrange("(b g) y x r c -> b g y x r c", b=B)
    for g in range(G):
        pool.dma_start(dst[bass.ds(b, 1), g, 1 - r:H + 1 - r, 1:W + 1, r, :].rearrange("b y x c -> (b y) x c"),
                       src[bass.ds(b, 1), g].rearrange("b y x c -> (b y) x c")).then_inc(done, 16)


def mixer_q(nc, sem, d, keep):
    with ExitStack() as ctx:
        sb = lambda n, s, t=F32: ctx.enter_context(nc.sbuf_tensor(n, s, t))
        x_sb = sb("mq_x", [P, 2, HT, NC])
        stats = sb("mq_stats", [P, HT, 6])
        mv = sb("mq_mv", [P, HT, 2])
        var = sb("mq_var", [P, HT])
        half = sb("mq_half", [P, HT])
        rstd = sb("mq_rstd", [P, HT])
        xn = sb("mq_xn", [P, 2, HT, NC])
        wq = sb("mq_wq", [P, CH, NC])
        bq = sb("mq_bq", [P, CH])
        ident = sb("mq_ident", [P, P])
        xnT = sb("mq_xnT", [P, CH, HN])
        qT = sb("mq_qT", [P, 2, CH, HN])
        qparts = sb("mq_qparts", [P, 2, 2, CH, HN], F32R)
        psT = ctx.enter_context(nc.psum_tensor("mq_psT", [P, CH, HN], F32))
        psQ = ctx.enter_context(nc.psum_tensor("mq_psQ", [P, CH, HN], F32))
        var_ready, rstd_ready, weights, norm_steps, xn_ready, t_done, t_copied, q_done, q_copied, q_high, q_low, q_padded, memsets = (
            sem("mq_" + x) for x in ("var_ready", "rstd_ready", "weights", "norm_steps", "xn_ready", "t_done", "t_copied", "q_done", "q_copied", "q_high", "q_low", "q_padded", "memsets"))
        x_in, xn_out, q_out = ([sem(f"mq_{x}{f}") for f in range(2)] for x in ("x_in", "xn_out", "q_out"))
        taps_in = sem("mq_taps_in")
        passed = keep["passed"]
        block = ctx.enter_context(nc.Block())
        x_v = d["x"].rearrange("b h w c -> (b h w) c").rearrange("(s t p) c -> s p t c", p=P, t=HT)
        q_v = d["q_scr"].rearrange("(b j) z p (f n) -> b f z p j n", j=CH, f=2)
        xn_v = d["xn_scr"].rearrange("(s t p) c -> s p t c", p=P, t=HT)

        @block.sync
        def _(sp):
            sp.dma_start(ident[:, :], d["c_ident"]).then_inc(weights, 16)
            sp.dma_start(wq[:, :, :], chunks(d["w_q"])).then_inc(weights, 16)
            sp.dma_start(bq[:, :], d["b_q"].rearrange("(c p) -> p c", p=P), allow_slow_non_contiguous=True).then_inc(weights, 16)
            sp.sem_inc(xn_ready, 2 * HT)

            def load(b, f):
                sp.dma_start(x_sb[:, f], x_v[bass.ds(b * 2 + f, 1)].rearrange("s p t c -> (s p) t c")).then_inc(x_in[f], 16)

            def norm_out(b, f):
                sp.wait_ge(xn_ready, b * 2 * HT + (3 + f) * HT)
                sp.dma_start(xn_v[bass.ds(b * 2 + f, 1)].rearrange("s p t c -> (s p) t c"), xn[:, f]).then_inc(xn_out[f], 16)

            def queries_out(b, f):
                sp.wait_ge(q_high, b * 2 * CH + f * CH + CH)
                sp.sem_inc(passed, 1)
                sp.wait_ge(q_low, b * 2 * CH + f * CH + 3 * CH)
                for z in range(2):
                    sp.dma_start(q_v[bass.ds(b, 1), f, z].rearrange("b p j n -> (b p) j n"), qparts[:, f, z].bitcast(F32)).then_inc(q_out[f], 16)

            for f in range(2):
                load(0, f)
            sp.wait_ge(memsets, 4)
            w = d["w_off0"].rearrange("y x i (j g o) -> g i (y x) j o", g=2, o=GC)
            for g in range(2):
                for j in range(CH):
                    sp.dma_start(keep["taps"][g * GC:(g + 1) * GC, :, j, g * GC:(g + 1) * GC], w[g, :, :, j]).then_inc(taps_in, 16)
            with sp.Fori(0, B - 1) as b:
                for f in range(2):
                    norm_out(b, f)
                    load(b + 1, f)
                for f in range(2):
                    queries_out(b, f)
            for f in range(2):
                norm_out(B - 1, f)
            for f in range(2):
                queries_out(B - 1, f)
            sp.wait_ge(taps_in, 2 * CH * 16)
            sp.wait_ge(keep["table_out"], 16 * (6 + G))
            for f in range(2):
                sp.wait_ge(xn_out[f], (B + 1) * 16)
                sp.wait_ge(q_out[f], (B + 1) * 32)

        @block.gpsimd
        def _(pool):
            pool.memset(half[:, :], -0.5).then_inc(memsets, 1)
            padded = keep["q_pad"][:, :, :, :, :, :].bitcast(F32).rearrange("p z j b y x -> p (z j b) y x")
            pool.memset(padded[:, :, 0:H + 2:H + 1, :], 0.0).then_inc(memsets, 1)
            pool.memset(padded[:, :, 1:H + 1, 0:W + 2:W + 1], 0.0).then_inc(memsets, 1)
            pool.memset(keep["taps"][:, :, :, :], 0.0).then_inc(memsets, 1)
            pool.wait_ge(memsets, 1)
            def inverse_root(b, f):
                pool.wait_ge(var_ready, b * 2 + f + 1)
                pool.tensor_tensor(rstd[:, :], var[:, :], half[:, :], ALU.pow).then_inc(rstd_ready, 1)

            def quads(b, r):
                for f in range(2):
                    pool.wait_ge(xn_out[f], b * 16 + 32)
                    pool.sem_inc(passed, 1)
                write_quads(pool, d, b, r, keep["quad_out"])

            for f in range(2):
                inverse_root(0, f)
            with pool.Fori(1, B) as b:
                inverse_root(b, 0)
                for r in range(2):
                    quads(b - 1, r)
                inverse_root(b, 1)
        @block.vector
        def _(dve):
            K = 2 * 2 * HT
            dve.sem_inc(t_done, 2)
            for f in range(2):
                dve.sem_inc(xn_out[f], 16)

            def pad(b, f):
                for j in range(CH):
                    dve.wait_ge(q_high, b * 2 * CH + f * CH + j + 1)
                    dve.tensor_tensor(qparts[:, f, 1, j, :], qT[:, f, j, :], qparts[:, f, 0, j, :].bitcast(F32), ALU.subtract).then_inc(q_low, 1)
                    for z in range(2):
                        dve.wait_ge(q_low, b * 2 * CH + f * CH + 2 * CH + j + 1)
                        dst = keep["q_pad"][:, z, j, bass.ds(b, 1), f * HROWS + 1:(f + 1) * HROWS + 1, 1:W + 1]
                        dve.tensor_copy(dst.rearrange("p b y x -> p (b y) x"), qparts[:, f, z, j, :].bitcast(F32).rearrange("p (y x) -> p y x", x=W)).then_inc(q_padded, 1)

            def norm(b, f):
                n = Count()
                dve.wait_ge(x_in[f], b * 16 + 16)
                for t in range(HT):
                    dve.bn_stats(stats[:, t, :], x_sb[:, f, t, :]).then_inc(norm_steps, n.up())
                dve.wait_ge(norm_steps, b * K + f * (K // 2) + n.now)
                dve.sem_inc(passed, 1)
                for t in range(HT):
                    dve.bn_aggr(mv[:, t, :], stats[:, t, :]).then_inc(norm_steps, n.up())
                dve.wait_ge(norm_steps, b * K + f * (K // 2) + n.now)
                dve.tensor_scalar(var[:, :], mv[:, :, 1], 1e-6, None, ALU.add).then_inc(var_ready, 1)
                dve.wait_ge(rstd_ready, b * 2 + f + 1)
                dve.wait_ge(xn_out[f], b * 16 + 16)
                dve.wait_ge(t_done, b * 2 + f + 1)
                for t in range(HT):
                    dve.tensor_scalar(xn[:, f, t, :], x_sb[:, f, t, :], mv[:, t, 0:1], rstd[:, t:t + 1],
                                      ALU.subtract, ALU.mult).then_inc(xn_ready, 1)
                dve.wait_ge(xn_ready, b * 2 * HT + (3 + f) * HT)
                assert n.now == K // 2

            norm(0, 0)
            norm(0, 1)
            pad(0, 0)
            with dve.Fori(1, B) as b:
                norm(b, 0)
                pad(b - 1, 1)
                norm(b, 1)
                pad(b, 0)
            pad(B - 1, 1)

        @block.tensor
        def _(pe):
            pe.wait_ge(weights, 48)
            pe.sem_inc(t_copied, 1)
            pe.sem_inc(q_copied, CH)
            with pe.Fori(0, B) as b:
                for f in range(2):
                    for t in range(HT):
                        pe.wait_ge(xn_ready, b * 2 * HT + (2 + f) * HT + t + 1)
                        if t == 0:
                            pe.wait_ge(t_copied, b * 2 + f + 1)
                        for j in range(CH):
                            mm = pe.transpose(psT[:, j, t * P:(t + 1) * P], xn[:, f, t, j * P:(j + 1) * P], ident[:, :])
                    mm.then_inc(t_done, 1)
                    pe.wait_ge(t_copied, b * 2 + f + 2)
                    for j in range(CH):
                        pe.wait_ge(q_copied, b * 2 * CH + f * CH + j + 1)
                        for c in range(CH):
                            mm = pe.matmul(psQ[:, j, :], wq[:, c, j * P:(j + 1) * P], xnT[:, c, :], start=c == 0, stop=c == CH - 1)
                        mm.then_inc(q_done, 1)

        @block.scalar
        def _(act):
            act.wait_ge(weights, 48)
            act.sem_inc(q_done, CH)
            act.sem_inc(q_padded, 4 * CH)
            act.sem_inc(q_low, 2 * CH)
            for f in range(2):
                act.sem_inc(q_out[f], 32)
            with act.Fori(0, B) as b:
                for f in range(2):
                    act.wait_ge(t_done, b * 2 + f + 3)
                    act.wait_ge(q_done, b * 2 * CH + f * CH + CH)
                    act.activation(xnT[:, :, :], psT[:, :, :], ACT.Copy).then_inc(t_copied, 1)
                    act.wait_ge(q_out[f], b * 32 + 32)
                    act.wait_ge(q_padded, b * 4 * CH + f * 2 * CH + 2 * CH)
                    act.wait_ge(q_low, b * 2 * CH + f * CH + CH)
                    for j in range(CH):
                        act.wait_ge(q_done, b * 2 * CH + f * CH + CH + j + 1)
                        act.activation(qT[:, f, j, :], psQ[:, j, :], ACT.Identity, bias=bq[:, j:j + 1]).then_inc(q_copied, 1)
                        act.wait_ge(q_copied, b * 2 * CH + f * CH + CH + j + 1)
                        act.activation(qparts[:, f, 0, j, :], qT[:, f, j, :], ACT.Copy).then_inc(q_high, 1)


def offsets(nc, sem, d, keep):
    TAPS = 9
    with ExitStack() as ctx:
        sb = lambda n, s, t=F32: ctx.enter_context(nc.sbuf_tensor(n, s, t))
        wc = sb("of_wc", [P, 2, TAPS, CH, P], F32R)
        bo = sb("of_bo", [P, CH])
        gain, shift = sb("of_gain", [P, NC]), sb("of_shift", [P, NC])
        woff = sb("of_woff", [P, GC, 2])
        ident = sb("of_ident", [P, P])
        cell, base = sb("of_cell", [P, TI, 2]), sb("of_base", [P, 2, B * G])
        oT = sb("of_oT", [P, CH, HN])
        on = sb("of_on", [P, 2, HT, NC])
        ge = sb("of_ge", [P, 2, HT, NC])
        part = sb("of_part", [P, HT * G, GC])
        stats, mv = sb("of_stats", [P, HT, 6]), sb("of_mv", [P, HT, 2])
        var, half, rstd = sb("of_var", [P, HT]), sb("of_half", [P, HT]), sb("of_rstd", [P, HT])
        off, th = sb("of_off", [P, 2, G, HT]), sb("of_th", [P, 2, G, HT])
        pos = sb("of_pos", [P, 2, G, HT])
        v, fl, fr, co = (sb("of_" + x, [P, 2, 2, G, HT]) for x in ("v", "fl", "fr", "co"))
        whole = sb("of_whole", [P, 2, 2, G, HT], I32)
        flat = sb("of_flat", [P, 2, G, HT])
        ws, wb = sb("of_ws", [P, G, HT, 4]), sb("of_wb", [P, G, HT, 4])
        psC = ctx.enter_context(nc.psum_tensor("of_psC", [P, CH, HN], F32))
        psO = ctx.enter_context(nc.psum_tensor("of_psO", [P, HT, 512], F32))
        (weights, taps_split, conv_done, oT_ready, back_done, steps, half_set, var_ready, rstd_ready, normed, scaled, off_steps, gelu_done,
         off_ready, tanh_done) = (sem("of_" + x) for x in (
             "weights", "taps_split", "conv_done", "oT_ready", "back_done", "steps", "half_set", "var_ready", "rstd_ready",
             "normed", "scaled", "off_steps", "gelu_done", "off_ready", "tanh_done"))
        passed = keep["passed"]
        each_tile = lambda v: v[:, :].rearrange("p (o c) -> p o c", o=1).broadcast_to([P, HT, NC])
        block = ctx.enter_context(nc.Block())

        @block.sync
        def _(sp):
            sp.dma_start(ident[:, :], d["c_ident"]).then_inc(weights, 16)
            sp.dma_start(bo[:, :], d["b_off0"].rearrange("(c p) -> p c", p=P), allow_slow_non_contiguous=True).then_inc(weights, 16)
            sp.dma_start(gain[:, :], rows(d["ln_g"], P)).then_inc(weights, 16)
            sp.dma_start(shift[:, :], rows(d["ln_b"], P)).then_inc(weights, 16)
            sp.dma_start(woff[:, :, :].rearrange("p c k -> p (c k)"), rows(d["w_offp"].rearrange("c k -> (c k)"), P)).then_inc(weights, 16)
            sp.dma_start(cell[:, :, :], d["c_cell"]).then_inc(weights, 16)
            sp.dma_start(base[:, :, :], d["c_base"]).then_inc(weights, 16)
            sp.wait_ge(weights, 16 * 7)

        @block.gpsimd
        def _(pool):
            pool.memset(half[:, :], -0.5).then_inc(half_set, 1)
            pool.wait_ge(half_set, 1)
            for r in range(2):
                write_quads(pool, d, B - 1, r, keep["quad_out"])
            pool.wait_ge(weights, 16 * 7)
            with pool.Fori(0, B) as b:
                for f in range(2):
                    pool.wait_ge(var_ready, b * 2 + f + 1)
                    pool.tensor_tensor(rstd[:, :], var[:, :], half[:, :], ALU.pow).then_inc(rstd_ready, 1)
                    pool.wait_ge(steps, (b * 2 + f + 1) * NORM_K)
                    pool.tensor_tensor(on[:, f], on[:, f], each_tile(gain), ALU.mult).then_inc(scaled, 1)
                    pool.wait_ge(scaled, (b * 2 + f) * 2 + 1)
                    pool.tensor_tensor(on[:, f], on[:, f], each_tile(shift), ALU.add).then_inc(scaled, 1)

            pool.wait_ge(keep["quad_out"], B * 2 * G * 16)

        @block.tensor
        def _(pe):
            pe.wait_ge(weights, 16 * 7)
            pe.wait_ge(taps_split, 2)
            pe.sem_inc(oT_ready, CH)
            pe.sem_inc(normed, 1)
            with pe.Fori(0, B) as b:
                for f in range(2):
                    for j in range(CH):
                        pe.wait_ge(oT_ready, b * 2 * CH + f * CH + j + 1)
                        for tap in range(TAPS):
                            y, x = f * HROWS + tap // 3, tap % 3
                            for a, z in PASSES:
                                q = keep["q_pad"][:, z, j, bass.ds(b, 1), y:y + HROWS, x:x + W].rearrange("p b y x -> p (b y) x")
                                mm = pe.matmul(psC[:, j, :].rearrange("p (y x) -> p y x", x=W), wc[:, a, tap, j, :], q,
                                               start=tap == 0 and (a, z) == (0, 0), stop=tap == TAPS - 1 and a == 1)
                        mm.then_inc(conv_done, 1)
                    pe.wait_ge(normed, b * 2 + f + 1)
                    for j in range(CH):
                        pe.wait_ge(oT_ready, b * 2 * CH + f * CH + CH + j + 1)
                        for t in range(HT):
                            mm = pe.transpose(psO[:, t, j * P:(j + 1) * P], oT[:, j, t * P:(t + 1) * P], ident[:, :])
                    mm.then_inc(back_done, 1)

        @block.scalar
        def _(act):
            act.wait_ge(weights, 16 * 7)
            act.sem_inc(back_done, 1)
            act.sem_inc(off_ready, 4)

            def activate(b, f):
                act.wait_ge(back_done, b * 2 + f + 1)
                for j in range(CH):
                    act.wait_ge(conv_done, b * 2 * CH + f * CH + j + 1)
                    act.activation(oT[:, j, :], psC[:, j, :], ACT.Identity, bias=bo[:, j:j + 1]).then_inc(oT_ready, 1)
                act.wait_ge(scaled, (b * 2 + f) * 2 + 2)
                act.wait_ge(off_ready, b * 4 + f * 2 + 2)
                act.activation(ge[:, f], on[:, f], ACT.Gelu).then_inc(gelu_done, 1)

            def squash(b, f):
                act.wait_ge(off_ready, b * 4 + f * 2 + 6)
                act.activation(th[:, :, :, :], off[:, :, :, :], ACT.Tanh).then_inc(tanh_done, 1)

            every_half(act, activate, squash)

        @block.vector
        def _(dve):
            dve.tensor_copy(wc[:, 0], keep["taps"][:, :, :, :]).then_inc(taps_split, 1)
            dve.wait_ge(taps_split, 1)
            dve.tensor_tensor(wc[:, 1], keep["taps"][:, :, :, :], wc[:, 0].bitcast(F32), ALU.subtract).then_inc(taps_split, 1)
            dve.wait_ge(weights, 16 * 7)

            def norm(b, f):
                n = Count()
                dve.wait_ge(back_done, b * 2 + f + 2)
                for t in range(HT):
                    dve.bn_stats(stats[:, t, :], psO[:, t, 0:NC]).then_inc(steps, n.up())
                dve.wait_ge(steps, (b * 2 + f) * NORM_K + n.now)
                dve.sem_inc(passed, 1)
                for t in range(HT):
                    dve.bn_aggr(mv[:, t, :], stats[:, t, :]).then_inc(steps, n.up())
                dve.wait_ge(steps, (b * 2 + f) * NORM_K + n.now)
                dve.tensor_scalar(var[:, :], mv[:, :, 1], 1e-3, None, ALU.add).then_inc(var_ready, 1)
                dve.wait_ge(rstd_ready, b * 2 + f + 1)
                for t in range(HT):
                    dve.tensor_scalar(on[:, f, t, :], psO[:, t, 0:NC], mv[:, t, 0:1], rstd[:, t:t + 1],
                                      ALU.subtract, ALU.mult).then_inc(steps, n.up())
                dve.wait_ge(steps, (b * 2 + f) * NORM_K + n.now)
                dve.sem_inc(normed, 1)
                assert n.now == NORM_K

            def positions(b, f):
                n = Count()

                def after():
                    dve.wait_ge(off_steps, (b * 2 + f) * OFF_K + n.now)

                dve.wait_ge(gelu_done, b * 2 + f + 1)
                ge3 = ge[:, f].rearrange("p t (g c) -> p (t g) c", g=G)
                for k in range(2):
                    w3 = woff[:, :, k].rearrange("p (o c) -> p o c", o=1).broadcast_to([P, HT * G, GC])
                    dve.tensor_tensor(part[:, :, :], ge3, w3, ALU.mult).then_inc(off_steps, n.up())
                    after()
                    dve.tensor_reduce(off[:, k].rearrange("p g t -> p t g"), part[:, :, :].rearrange("p (t g) c -> p t g c", g=G),
                                      AX.X, ALU.add).then_inc(off_ready, 1)
                    dve.wait_ge(off_ready, b * 4 + (f * 2 + k + 5))
                dve.wait_ge(tanh_done, b * 2 + f + 1)
                for k in range(2):
                    c3 = cell[:, f * HT:(f + 1) * HT, k].rearrange("p (o t) -> p o t", o=1).broadcast_to([P, G, HT])
                    dve.scalar_tensor_tensor(pos[:, k], th[:, k], float(W // 2), c3, ALU.mult, ALU.add).then_inc(off_steps, n.up())
                after()
                dve.tensor_scalar(v[:, 0], pos[:, :, :, :], 0.5, None, ALU.add).then_inc(off_steps, n.up())
                dve.tensor_scalar(v[:, 1], pos[:, :, :, :], -1.0, float(1 - SLO), ALU.mult, ALU.add).then_inc(off_steps, n.up())
                after()
                dve.tensor_copy(whole[:, :, :, :, :], v[:, :, :, :, :]).then_inc(off_steps, n.up())
                after()
                dve.tensor_copy(fl[:, :, :, :, :], whole[:, :, :, :, :]).then_inc(off_steps, n.up())
                after()
                dve.tensor_tensor(co[:, :, :, :, :], fl[:, :, :, :, :], v[:, :, :, :, :], ALU.is_gt).then_inc(off_steps, n.up())
                after()
                dve.tensor_tensor(fl[:, :, :, :, :], fl[:, :, :, :, :], co[:, :, :, :, :], ALU.subtract).then_inc(off_steps, n.up())
                after()
                dve.tensor_scalar(fl[:, 0], fl[:, 0], 0.0, float(H), ALU.max, ALU.min).then_inc(off_steps, n.up())
                dve.tensor_scalar(fl[:, 1], fl[:, 1], 0.0, float(SN - 1), ALU.max, ALU.min).then_inc(off_steps, n.up())
                after()
                dve.tensor_tensor(fr[:, :, :, :, :], v[:, :, :, :, :], fl[:, :, :, :, :], ALU.subtract).then_inc(off_steps, n.up())
                dve.scalar_tensor_tensor(flat[:, 0], fl[:, 0, 1], float(QX), fl[:, 0, 0], ALU.mult, ALU.add).then_inc(off_steps, n.up())
                dve.scalar_tensor_tensor(flat[:, 1], fl[:, 1, 0], float(UN), fl[:, 1, 1], ALU.mult, ALU.add).then_inc(off_steps, n.up())
                after()
                dve.tensor_scalar(fr[:, :, :, :, :], fr[:, :, :, :, :], 0.0, 1.0, ALU.max, ALU.min).then_inc(off_steps, n.up())
                for k, pitch in ((0, 2 * GC), (1, UW)):
                    dve.tensor_scalar(flat[:, k], flat[:, k], float(pitch), None, ALU.mult).then_inc(off_steps, n.up())
                after()
                dve.tensor_scalar(co[:, :, :, :, :], fr[:, :, :, :, :], -1.0, 1.0, ALU.mult, ALU.add).then_inc(off_steps, n.up())
                for k in range(2):
                    dst = (keep["quad_at"], keep["shift_at"])[k][:, bass.ds(b, 1), :, f * HT:(f + 1) * HT].rearrange("p b g t -> p (b g) t")
                    b3 = inner(base[:, k, bass.ds(b * G, G)], HT)
                    dve.tensor_tensor(dst, flat[:, k], b3, ALU.add).then_inc(off_steps, n.up())
                after()
                for q, (x, y) in enumerate(((co, co), (co, fr), (fr, co), (fr, fr))):
                    dve.tensor_tensor(ws[:, :, :, q], x[:, 0, 0], y[:, 0, 1], ALU.mult).then_inc(off_steps, n.up())
                for q, x in enumerate((co[:, 1, 0], fr[:, 1, 0], co[:, 1, 1], fr[:, 1, 1])):
                    dve.tensor_copy(wb[:, :, :, q], x).then_inc(off_steps, n.up())
                after()
                for w, name in ((ws, "quad_w"), (wb, "shift_w")):
                    dst = keep[name][:, bass.ds(b, 1), :, f * HT:(f + 1) * HT, :].rearrange("p b g t k -> p (b g) (t k)")
                    dve.tensor_copy(dst, w[:, :, :, :].rearrange("p g t k -> p g (t k)")).then_inc(off_steps, n.up())
                after()
                assert n.now == OFF_K, n.now

            every_half(dve, norm, positions)


NORM_K = 3 * HT
OFF_K = 31


def keys(nc, sem, d, keep):
    QUAD = 4 * GC
    with ExitStack() as ctx:
        sb = lambda n, s, t=F32: ctx.enter_context(nc.sbuf_tensor(n, s, t))
        at = sb("ke_at", [P, 2, G, HT], I32)
        quad = sb("ke_quad", [P, HT, G, QUAD])
        prod = sb("ke_prod", [P, G, 4, GC])
        side = sb("ke_side", [P, G, 2, GC])
        xs = sb("ke_xs", [P, HT, G, GC])
        xsT = sb("ke_xsT", [P, CH, HN])
        wk, wv = sb("ke_wk", [P, CH, NC]), sb("ke_wv", [P, CH, NC])
        bk, bks, bv = sb("ke_bk", [P, CH]), sb("ke_bks", [P, CH]), sb("ke_bv", [P, NC])
        ident = sb("ke_ident", [P, P])
        kT, kparts = sb("ke_kT", [P, CH, HN]), sb("ke_kparts", [P, 2, 2, CH, HN], F32R)
        vt = sb("ke_vt", [P, 2, HT, NC])
        psT = ctx.enter_context(nc.psum_tensor("ke_psT", [P, CH, HN], F32))
        psK = ctx.enter_context(nc.psum_tensor("ke_psK", [P, CH, HN], F32))
        psV = ctx.enter_context(nc.psum_tensor("ke_psV", [P, 2, 512], F32))
        (weights, bks_ready, staged, prod_done, side_done, xs_ready, t_done, t_copied, k_done, k_ready, k_high, k_low, v_done, v_ready) = (
            sem("ke_" + x) for x in ("weights", "bks_ready", "staged", "prod_done", "side_done", "xs_ready", "t_done",
                                     "t_copied", "k_done", "k_ready", "k_high", "k_low", "v_done", "v_ready"))
        gathered = [sem(f"ke_gathered{t}") for t in range(HT)]
        k_out, v_out = ([sem(f"ke_{x}{f}") for f in range(2)] for x in ("k_out", "v_out"))
        passed = keep["passed"]
        block = ctx.enter_context(nc.Block())
        flat = d["quads"].rearrange("n y x r c -> (n y x r c)").rearrange("(n o) -> n o", o=1)
        k_v = d["k_scr"].rearrange("(b j) z p (f n) -> b f z p j n", j=CH, f=2)

        @block.sync
        def _(sp):
            sp.dma_start(ident[:, :], d["c_ident"]).then_inc(weights, 16)
            sp.dma_start(wk[:, :, :], chunks(d["w_k"])).then_inc(weights, 16)
            sp.dma_start(wv[:, :, :], chunks(d["w_v"])).then_inc(weights, 16)
            sp.dma_start(bk[:, :], d["b_k"].rearrange("(c p) -> p c", p=P), allow_slow_non_contiguous=True).then_inc(weights, 16)
            sp.dma_start(bv[:, :], rows(d["b_v"], P)).then_inc(weights, 16)
            with sp.Fori(0, B) as b:
                for f in range(2):
                    sp.wait_ge(k_high, b * 2 * CH + (f + 1) * CH)
                    sp.sem_inc(passed, 1)
                    sp.wait_ge(k_low, b * 2 * CH + (f + 2) * CH)
                    for z in range(2):
                        sp.dma_start(k_v[bass.ds(b, 1), f, z].rearrange("b p j n -> (b p) j n"), kparts[:, f, z].bitcast(F32)).then_inc(k_out[f], 16)
                    for t in range(HT):
                        sp.wait_ge(v_ready, b * 2 * HT + f * HT + t + 3)
                        dst = d["v_scr"][bass.ds(b * CH, CH), f * HT + t].rearrange("j p c -> p j c")
                        sp.dma_start(dst, vt[:, f, t, :].rearrange("p (j c) -> p j c", j=CH)).then_inc(v_out[f], 16)
            for f in range(2):
                sp.wait_ge(k_out[f], (B + 1) * 32)
                sp.wait_ge(v_out[f], (B + 1) * 16 * HT)

        @block.gpsimd
        def _(pool):
            pool.sem_inc(xs_ready, 2 * HT)
            with pool.Fori(0, B) as b:
                for f in range(2):
                    pool.wait_ge(xs_ready, b * 2 * HT + (f + 1) * HT)
                    pool.sem_inc(passed, 1)
                    src = keep["quad_at"][:, bass.ds(b, 1), :, f * HT:(f + 1) * HT].rearrange("p b g t -> p (b g) t")
                    pool.tensor_copy(at[:, f], src).then_inc(staged, 1)
                    pool.wait_ge(staged, b * 2 + f + 1)
                    for t in range(HT):
                        pool.wait_ge(xs_ready, b * 2 * HT + (f + 1) * HT + t + 1)
                        pool.sem_inc(passed, 1)
                        for g in range(G):
                            pool.indirect_dma_start(out=quad[:, t, g, :], out_offset=None, in_=flat,
                                                    in_offset=bass.IndirectOffsetOnAxis(ap=at[:, f, g, t:t + 1], axis=0)
                                                    ).then_inc(gathered[t], 16)

        @block.vector
        def _(dve):
            dve.wait_ge(weights, 16 * 5)
            dve.sem_inc(t_done, 1)
            dve.sem_inc(k_low, CH)
            for f in range(2):
                dve.sem_inc(v_out[f], 16 * HT)

            def sample(b, f, t):
                s = b * 2 * HT + (f * HT + t)
                dve.wait_ge(gathered[t], b * (2 * G * 16) + (f + 1) * G * 16)
                w = keep["quad_w"][:, bass.ds(b, 1), :, f * HT + t, :].rearrange("p b g q -> p (b g) q")
                dve.tensor_tensor(prod[:, :, :, :], quad[:, t].rearrange("p g (q c) -> p g q c", c=GC), inner(w, GC), ALU.mult).then_inc(prod_done, 1)
                dve.wait_ge(prod_done, s + 1)
                dve.tensor_tensor(side[:, :, :, :], prod[:, :, 0:2], prod[:, :, 2:4], ALU.add).then_inc(side_done, 1)
                dve.wait_ge(side_done, s + 1)
                if t == 0:
                    dve.wait_ge(t_done, b * 2 + f + 1)
                dve.tensor_tensor(xs[:, t], side[:, :, 0], side[:, :, 1], ALU.add).then_inc(xs_ready, 1)
                dve.wait_ge(xs_ready, s + (2 * HT + 1))

            def value(b, f, t):
                if t == 0:
                    dve.wait_ge(v_out[f], b * (16 * HT) + 16 * HT)
                dve.wait_ge(v_done, b * 2 * HT + (f * HT + t + 1))
                dve.tensor_tensor(vt[:, f, t, :], psV[:, t % 2, 0:NC], bv[:, :], ALU.add).then_inc(v_ready, 1)

            def low_key(b, f, j):
                dve.wait_ge(k_high, b * 2 * CH + (f * CH + j + 1))
                dve.tensor_tensor(kparts[:, f, 1, j, :], kT[:, j, :], kparts[:, f, 0, j, :].bitcast(F32), ALU.subtract).then_inc(k_low, 1)

            def half(b, f, behind):
                for t in range(HT):
                    sample(b, f, t)
                    if behind and t < 2:
                        value(*behind, 2 * t)
                        value(*behind, 2 * t + 1)
                    elif behind:
                        for j in ((0,), (1, 2))[t - 2]:
                            low_key(*behind, j)

            half(0, 0, None)
            half(0, 1, (0, 0))
            with dve.Fori(1, B) as b:
                half(b, 0, (b - 1, 1))
                half(b, 1, (b, 0))
            for t in range(HT):
                value(B - 1, 1, t)
            for j in range(CH):
                low_key(B - 1, 1, j)

        @block.tensor
        def _(pe):
            pe.wait_ge(weights, 16 * 5)
            pe.sem_inc(t_copied, 1)
            pe.sem_inc(k_ready, CH)
            pe.sem_inc(v_ready, 2)
            with pe.Fori(0, B) as b:
                for f in range(2):
                    for t in range(HT):
                        if t == 0:
                            pe.wait_ge(t_copied, b * 2 + f + 1)
                        pe.wait_ge(xs_ready, b * 2 * HT + (f * HT + t + 1 + 2 * HT))
                        for j in range(CH):
                            mm = pe.transpose(psT[:, j, t * P:(t + 1) * P], xs[:, t, 2 * j:2 * j + 2, :].rearrange("p g c -> p (g c)"), ident[:, :])
                    mm.then_inc(t_done, 1)
                    pe.wait_ge(t_copied, b * 2 + f + 2)
                    for t in range(HT):
                        pe.wait_ge(v_ready, b * 2 * HT + (f * HT + t + 1))
                        for c in range(CH):
                            mm = pe.matmul(psV[:, t % 2, 0:NC], xsT[:, c, t * P:(t + 1) * P], wv[:, c, :], start=c == 0, stop=c == CH - 1)
                        mm.then_inc(v_done, 1)
                    for j in range(CH):
                        pe.wait_ge(k_ready, b * 2 * CH + (f * CH + j + 1))
                        for c in range(CH):
                            mm = pe.matmul(psK[:, j, :], wk[:, c, j * P:(j + 1) * P], xsT[:, c, :], start=c == 0, stop=c == CH - 1)
                        mm.then_inc(k_done, 1)

        @block.scalar
        def _(act):
            act.wait_ge(weights, 16 * 5)
            act.activation(bks[:, :], bk[:, :], ACT.Copy, scale=SCALE).then_inc(bks_ready, 1)
            act.wait_ge(bks_ready, 1)
            act.sem_inc(k_done, CH)
            for f in range(2):
                act.sem_inc(k_out[f], 32)
            with act.Fori(0, B) as b:
                for f in range(2):
                    act.wait_ge(t_done, b * 2 + f + 2)
                    act.wait_ge(k_done, b * 2 * CH + (f + 1) * CH)
                    act.activation(xsT[:, :, :], psT[:, :, :], ACT.Copy).then_inc(t_copied, 1)
                    act.wait_ge(k_out[f], b * 32 + 32)
                    for j in range(CH):
                        act.wait_ge(k_done, b * 2 * CH + ((f + 1) * CH + j + 1))
                        act.wait_ge(k_low, b * 2 * CH + (f * CH + j + 1))
                        act.activation(kT[:, j, :], psK[:, j, :], ACT.Identity, bias=bks[:, j:j + 1], scale=SCALE).then_inc(k_ready, 1)
                        act.wait_ge(k_ready, b * 2 * CH + ((f + 1) * CH + j + 1))
                        act.activation(kparts[:, f, 0, j, :], kT[:, j, :], ACT.Copy).then_inc(k_high, 1)


def attend(nc, sem, d, keep):
    WB = 4
    ON_PE = ATTEND_ON_PE
    ON_DVE = [t for t in range(TI) if t not in ON_PE]
    LAG = 6
    ISSUE = [[t] if t < LAG else list(range(LAG, TI)) if t == LAG else [] for t in range(TI)]
    MAX_AT, DIAG_AT, SPREAD_AT = 2, 4, 4
    with ExitStack() as ctx:
        sb = lambda n, s, t=F32: ctx.enter_context(nc.sbuf_tensor(n, s, t))
        at = sb("at_at", [P, 2, TI], I32)
        wt = sb("at_wt", [P, 2, TI, 4])
        window = sb("at_window", [P, WB, UW, UW])
        rowx = sb("at_rowx", [P, WB, UW, W])
        below = sb("at_below", [P, WB, P])
        logit = sb("at_logit", [P, 2, TI, N])
        most = sb("at_most", [P, 2, N])
        mx = sb("at_mx", [P, TI])
        diag = sb("at_diag", [P, TI, P])
        neg = sb("at_neg", [P, N])
        ident, minus, ones = sb("at_ident", [P, P]), sb("at_minus", [P, P]), sb("at_ones", [P, P])
        qs, ks = sb("at_qs", [P, 2, 2, N], F32R), sb("at_ks", [P, 2, N], F32R)
        val = sb("at_val", [P, 2, TI, P])
        raw = sb("at_raw", [P, N])
        inverse = diag[:, :, :].rearrange("p t q -> p (t q)")
        psS = ctx.enter_context(nc.psum_tensor("at_psS", [P, 2, N], F32))
        psM = ctx.enter_context(nc.psum_tensor("at_psM", [P, N], F32))
        psO = ctx.enter_context(nc.psum_tensor("at_psO", [P, N], F32))
        (consts, ones_set, minus_set, staged, x0_done, below_ready, x_done, y0_done, logit_done, most_done, sum_ready, turned, mx_ready,
         diag_ready, spread, neg_ready, sub_done, p_done, pv_done, raw_ready, inverse_ready, o_done) = (sem("at_" + x) for x in (
             "consts", "ones_set", "minus_set", "staged", "x0_done", "below_ready", "x_done", "y0_done", "logit_done", "most_done",
             "sum_ready", "turned", "mx_ready", "diag_ready", "spread", "neg_ready", "sub_done", "p_done", "pv_done", "raw_ready",
             "inverse_ready", "o_done"))
        gathered = [sem(f"at_gathered{w}") for w in range(WB)]
        qk_in, v_in = ([sem(f"at_{n}{h}") for h in range(2)] for n in ("qk_in", "v_in"))
        passed = keep["passed"]
        block = ctx.enter_context(nc.Block())
        flat = d["shifts"].rearrange("h f u j -> (h f u j)").rearrange("(n o) -> n o", o=1)
        half = lambda h: slice(h * GC, (h + 1) * GC)

        def every_pair(eng, pair):
            pair(0, True)
            with eng.Fori(1, PAIRS) as i:
                pair(i, False)

        @block.sync
        def _(sp):
            sp.dma_start(ident[:, :], d["c_ident"]).then_inc(consts, 16)

            def pair(i, first):
                for h in range(2):
                    s = i * 2 + h
                    if not first:
                        sp.wait_ge(sum_ready, s * TI - TI)
                        sp.sem_inc(passed, 1)
                    k = d["k_scr"][bass.ds(i, 1), :, half(h), :].rearrange("a z c n -> (a z) c n")
                    sp.dma_start(ks[:, h, :].bitcast(F32), k).then_inc(qk_in[h], 16)
                    for z in range(2):
                        q = d["q_scr"][bass.ds(i, 1), z, half(h), :].rearrange("a c n -> (a c) n")
                        for a in range(2):
                            sp.dma_start(qs[half(a), h, z, :].bitcast(F32), q).then_inc(qk_in[h], 16)
                if first:
                    sp.wait_ge(ones_set, 3)
                for h in range(2):
                    if not first:
                        sp.wait_ge(pv_done, (i * 2 + h) * TI - TI)
                        sp.sem_inc(passed, 1)
                    src = d["v_scr"][bass.ds(i, 1), :, :, half(h)].rearrange("a t p c -> (a p) t c")
                    sp.dma_start(val[:, h, :, half(h)], src).then_inc(v_in[h], 16)

            every_pair(sp, pair)

        @block.gpsimd
        def _(pool):
            pool.memset(ones[:, :], 1.0).then_inc(ones_set, 1)
            for h in range(2):
                pool.memset(val[:, h, :, half(1 - h)], 1.0).then_inc(ones_set, 1)

            def subtract(s, h, k):
                if k == 0:
                    pool.wait_ge(neg_ready, s + 1)
                pool.tensor_tensor(logit[:, h, k, :], logit[:, h, k, :], neg[:, :], ALU.add).then_inc(sub_done, 1)

            def pair(i, first):
                for h in range(2):
                    s = i * 2 + h
                    if not first:
                        pool.wait_ge(logit_done, s * TI - TI)
                    pool.sem_inc(passed, 1)
                    pool.tensor_copy(at[:, h, :], keep["shift_at"][:, :, :, :].rearrange("p b g t -> p (b g) t")[:, bass.ds(s, 1), :].rearrange("p s t -> p (s t)")).then_inc(staged, 1)
                    pool.tensor_copy(wt[:, h].rearrange("p t k -> p (t k)"), keep["shift_w"][:, :, :, :, :].rearrange("p b g t k -> p (b g) (t k)")[:, bass.ds(s, 1), :].rearrange("p s t -> p (s t)")).then_inc(staged, 1)
                    pool.wait_ge(staged, s * 2 + 2)
                    pool.sem_inc(passed, 1)

                    def gather(t):
                        if not first or h or t >= WB:
                            pool.wait_ge(x_done, s * TI + (t - WB + 1))
                            pool.sem_inc(passed, 1)
                        pool.indirect_dma_start(out=window[:, t % WB].rearrange("p u j -> p (u j)"), out_offset=None, in_=flat,
                                                in_offset=bass.IndirectOffsetOnAxis(ap=at[:, h, t:t + 1], axis=0)
                                                ).then_inc(gathered[t % WB], 16)

                    for t in range(TI):
                        for ahead in ISSUE[t]:
                            gather(ahead)
                        if t < LAG and not first:
                            subtract(s - 2, h, t + TI - LAG)
                        if t >= LAG and (not first or h):
                            subtract(s - 1, 1 - h, t - LAG)

            every_pair(pool, pair)
            last = 2 * PAIRS - 1
            for k in range(TI - LAG, TI):
                subtract(last - 1, 0, k)
            for k in range(TI):
                subtract(last, 1, k)

        @block.scalar
        def _(act):
            act.wait_ge(consts, 16)
            act.wait_ge(minus_set, 1)

            def diagonals(s):
                act.wait_ge(mx_ready, s + 1)
                for k in range(TI):
                    act.activation(diag[:, k, :], minus[:, :], ACT.Copy, scale=mx[:, k:k + 1]).then_inc(diag_ready, 1)

            def spread_max(s):
                act.wait_ge(spread, s + 1)
                act.wait_ge(sub_done, s * TI)
                act.activation(neg[:, :], psM[:, :], ACT.Copy).then_inc(neg_ready, 1)

            def exps(s, h, k):
                act.wait_ge(sub_done, s * TI + (k + 1))
                act.activation(logit[:, h, k, :], logit[:, h, k, :], ACT.Exp).then_inc(p_done, 1)

            def take(s, h):
                act.wait_ge(pv_done, s * TI + TI)
                act.activation(raw[half(h), :], psO[half(h), :], ACT.Copy).then_inc(raw_ready, 1)
                act.activation(inverse[half(h), :], psO[half(1 - h), :], ACT.Ln).then_inc(raw_ready, 1)
                act.wait_ge(raw_ready, s * 2 + 2)
                act.activation(inverse[half(h), :], inverse[half(h), :], ACT.Exp, scale=-1.0).then_inc(inverse_ready, 1)

            def pair(i, first):
                for h in range(2):
                    s = i * 2 + h
                    act.wait_ge(staged, s * 2 + 2)

                    def across_left(t):
                        act.wait_ge(gathered[t % WB], s * (TI // WB * 16) + (t // WB + 1) * 16)
                        if not first or h or t >= WB:
                            act.wait_ge(logit_done, s * TI + (t - WB + 1))
                        act.activation(rowx[:, t % WB], window[:, t % WB, :, 0:W], ACT.Copy, scale=wt[:, h, t, 0:1]).then_inc(x0_done, 1)
                        if t in ON_PE:
                            act.activation(below[:, t % WB], ident[:, :], ACT.Copy, scale=wt[:, h, t, 3:4]).then_inc(below_ready, 1)

                    for t in range(TI):
                        for ahead in ISSUE[t]:
                            across_left(ahead)
                        if t == DIAG_AT and (not first or h):
                            diagonals(s - 1)
                        if t == LAG and (not first or h):
                            if first:
                                act.wait_ge(spread, 1)
                                act.activation(neg[:, :], psM[:, :], ACT.Copy).then_inc(neg_ready, 1)
                            else:
                                spread_max(s - 1)
                        if t == LAG + 1 and not first:
                            take(s - 2, h)
                        if t < LAG and not first:
                            exps(s - 2, h, t + TI - LAG)
                        if t >= LAG and (not first or h):
                            exps(s - 1, 1 - h, t - LAG)

            every_pair(act, pair)
            last = 2 * PAIRS - 1
            for k in range(TI - LAG, TI):
                exps(last - 1, 0, k)
            diagonals(last)
            spread_max(last)
            act.wait_ge(o_done, last - 1)
            take(last - 1, 0)
            for k in range(TI):
                exps(last, 1, k)
            act.wait_ge(o_done, last)
            take(last, 1)

        @block.tensor
        def _(pe):
            pe.wait_ge(consts, 16)
            pe.wait_ge(ones_set, 3)

            def turn_max(s, h, first):
                pe.wait_ge(most_done, s * (TI - 1) + (TI - 1))
                if not first:
                    pe.wait_ge(neg_ready, s)
                for k in range(TI):
                    mm = pe.transpose(psM[:, k * P:(k + 1) * P], most[:, h, k * P:(k + 1) * P], ident[:, :])
                mm.then_inc(turned, 1)

            def spread_max(s):
                pe.wait_ge(diag_ready, s * TI + TI)
                dg = diag[:, :, :].rearrange("p t q -> p (t q)")
                for a in range(2):
                    mm = pe.matmul(psM[:, a * 512:(a + 1) * 512], ones[:, :], dg[:, a * 512:(a + 1) * 512], start=True, stop=True)
                mm.then_inc(spread, 1)

            def values(s, h, k, i, first):
                pe.wait_ge(p_done, s * TI + (k + 1))
                if k == 0:
                    pe.wait_ge(v_in[h], i * 16 + 16)
                    if not first:
                        pe.wait_ge(raw_ready, s * 2)
                for a in range(2):
                    mm = pe.matmul(psO[:, a * 512:(a + 1) * 512], val[:, h, k, :], logit[:, h, k, a * 512:(a + 1) * 512],
                                   start=k == 0, stop=k == TI - 1)
                mm.then_inc(pv_done, 1)

            def product(s, h, t, first):
                if not first or h or t >= 2:
                    pe.wait_ge(logit_done, s * TI + (t - 1))
                for a in range(2):
                    for z in range(2):
                        mm = pe.matmul(psS[:, t % 2, a * 512:(a + 1) * 512], ks[:, h, t * P:(t + 1) * P], qs[:, h, z, a * 512:(a + 1) * 512],
                                       start=z == 0, stop=z == 1 and t not in ON_PE, skip_group_check=True)
                if t not in ON_PE:
                    mm.then_inc(sum_ready, 1)

            def lower_row(s, t):
                pe.wait_ge(below_ready, s * len(ON_PE) + ON_PE.index(t) + 1)
                pe.wait_ge(x_done, s * TI + (t + 1))
                flat_row = rowx[:, t % WB].rearrange("p u j -> p (u j)")
                for a in range(2):
                    mm = pe.matmul(psS[:, t % 2, a * 512:(a + 1) * 512], below[:, t % WB, :], flat_row[:, W + a * 512:W + (a + 1) * 512],
                                   start=False, stop=True, skip_group_check=True)
                mm.then_inc(sum_ready, 1)

            def pair(i, first):
                for h in range(2):
                    s = i * 2 + h
                    pe.wait_ge(qk_in[h], i * 80 + 80)
                    for t in range(TI):
                        product(s, h, t, first)
                        if t < LAG and not first:
                            values(s - 2, h, t + TI - LAG, i - 1, False)
                        if not first or h:
                            if t == MAX_AT:
                                turn_max(s - 1, 1 - h, first)
                            if t == SPREAD_AT:
                                spread_max(s - 1)
                        if t in ON_PE:
                            lower_row(s, t)
                        if t >= LAG and (not first or h):
                            values(s - 1, 1 - h, t - LAG, i if h else i - 1, first)

            every_pair(pe, pair)
            last = 2 * PAIRS - 1
            for k in range(TI - LAG, TI):
                values(last - 1, 0, k, PAIRS - 1, False)
            turn_max(last, 1, False)
            spread_max(last)
            for k in range(TI):
                values(last, 1, k, PAIRS - 1, False)

        @block.vector
        def _(dve):
            dve.wait_ge(consts, 16)
            dve.tensor_scalar(minus[:, :], ident[:, :], -1.0, None, ALU.mult).then_inc(minus_set, 1)
            dve.wait_ge(minus_set, 1)

            def reduce_max(s):
                dve.wait_ge(turned, s + 1)
                dve.tensor_reduce(mx[:, :], psM[:, :].rearrange("p (t q) -> p t q", t=TI), AX.X, ALU.max).then_inc(mx_ready, 1)

            def output(s, h, i):
                dve.wait_ge(inverse_ready, s + 1)
                dst = keep["o"][half(h), bass.ds(i // CH, 1), :, bass.ds(i % CH, 1), :, :].rearrange("p b f j t c -> p (b f j) (t c)")
                dve.tensor_tensor(dst, raw[half(h), :].rearrange("p (f n) -> p f n", f=2), inverse[half(h), :].rearrange("p (f n) -> p f n", f=2),
                                  ALU.mult).then_inc(o_done, 1)

            def across(s, h, t):
                dve.wait_ge(x0_done, s * TI + (t + 1))
                dve.scalar_tensor_tensor(rowx[:, t % WB], window[:, t % WB, :, 1:UW], wt[:, h, t, 1:2], rowx[:, t % WB],
                                         ALU.mult, ALU.add).then_inc(x_done, 1)

            def logits(s, h, t, fresh):
                n = s * TI + t
                dve.wait_ge(x_done, n + 1)
                dve.wait_ge(sum_ready, n + 1)
                if not fresh:
                    dve.wait_ge(pv_done, n - (2 * TI - 1))
                flat_row = rowx[:, t % WB].rearrange("p u j -> p (u j)")
                lt = logit[:, h, t, :]
                dve.scalar_tensor_tensor(lt, flat_row[:, 0:N], wt[:, h, t, 2:3], psS[:, t % 2, :],
                                         ALU.mult, ALU.add).then_inc(logit_done if t in ON_PE else y0_done, 1)
                if t in ON_DVE:
                    dve.wait_ge(y0_done, s * len(ON_DVE) + ON_DVE.index(t) + 1)
                    dve.scalar_tensor_tensor(lt, flat_row[:, W:W + N], wt[:, h, t, 3:4], lt, ALU.mult, ALU.add).then_inc(logit_done, 1)

            def running_max(s, h, t):
                dve.wait_ge(logit_done, s * TI + (t + 1))
                if t >= 2:
                    dve.wait_ge(most_done, s * (TI - 1) + (t - 1))
                so_far = logit[:, h, 0, :] if t == 1 else most[:, h, :]
                dve.tensor_tensor(most[:, h, :], so_far, logit[:, h, t, :], ALU.max).then_inc(most_done, 1)

            def pair(i, first):
                for h in range(2):
                    s = i * 2 + h
                    for t in range(TI):
                        across(s, h, t)
                        if t == MAX_AT + 1 and (not first or h):
                            reduce_max(s - 1)
                        if t >= 3:
                            running_max(s, h, t - 2)
                        elif t < 2 and (not first or h):
                            running_max(s - 1, 1 - h, t + TI - 2)
                        if t >= 1:
                            logits(s, h, t - 1, first)
                        elif not first or h:
                            logits(s - 1, 1 - h, TI - 1, True)
                        if t == LAG + 1 and not first:
                            output(s - 2, h, i - 1)

            every_pair(dve, pair)
            last = 2 * PAIRS - 1
            running_max(last, 1, TI - 2)
            logits(last, 1, TI - 1, False)
            running_max(last, 1, TI - 1)
            reduce_max(last)
            output(last - 1, 0, PAIRS - 1)
            output(last, 1, PAIRS - 1)


ATTEND_ON_PE = (0, 2, 4, 5, 6, 7)


def join(nc, sem, d, keep):
    with ExitStack() as ctx:
        sb = lambda n, s, t=F32: ctx.enter_context(nc.sbuf_tensor(n, s, t))
        ident, wo, wg = sb("jo_ident", [P, P]), sb("jo_wo", [P, CH, NC]), sb("jo_wg", [P, CH, E])
        bo, bg = sb("jo_bo", [P, NC]), sb("jo_bg", [P, E])
        x = sb("jo_x", [P, 2, HT, NC])
        oT = sb("jo_oT", [P, CH, HN])
        stats, mv = sb("jo_stats", [P, HT, 6]), sb("jo_mv", [P, HT, 2])
        var, half, rstd = sb("jo_var", [P, HT]), sb("jo_half", [P, HT]), sb("jo_rstd", [P, HT])
        tn = sb("jo_tn", [P, 2, HT, NC])
        tnT = sb("jo_tnT", [P, CH, HN])
        earlier, ones, region = sb("jo_earlier", [P, P]), sb("jo_ones", [P, P]), sb("jo_region", [P, E])
        chosen, before, place = sb("jo_chosen", [P, HT, E]), sb("jo_before", [P, HT, E]), sb("jo_place", [P, HT, E])
        run = sb("jo_run", [P, HT + 1, E])
        pick, picked = sb("jo_pick", [P, HT, 2, E]), sb("jo_picked", [P, HT, 2, E])
        slot = sb("jo_slot", [P, HT, 2])
        at = sb("jo_at", [P, 2, HT, 2], I32)
        score, prob, top = sb("jo_score", [P, HT, E]), sb("jo_prob", [P, HT, E]), sb("jo_top", [P, HT, E])
        one = sb("jo_one", [P, HT])
        above = sb("jo_above", [P, HT, E, E])
        psT = ctx.enter_context(nc.psum_tensor("jo_psT", [P, CH, HN], F32))
        psY = ctx.enter_context(nc.psum_tensor("jo_psY", [P, 2, 512], F32))
        psG = ctx.enter_context(nc.psum_tensor("jo_psG", [P, 2, 512], F32))
        psR = ctx.enter_context(nc.psum_tensor("jo_psR", [P, 2, HT, E], F32))
        (weights, gate_steps, memsets, oT_ready, y_done, t_ready, steps, var_ready, rstd_ready, tn_ready,
         tn_turned, tnT_ready, gate_done, score_ready, exp_done, chosen_ready, ranked, at_ready) = (sem("jo_" + n) for n in (
             "weights", "gate_steps", "memsets", "oT_ready", "y_done", "t_ready", "steps", "var_ready",
             "rstd_ready", "tn_ready", "tn_turned", "tnT_ready", "gate_done", "score_ready", "exp_done", "chosen_ready", "ranked", "at_ready"))
        x_in, rows_out = ([sem(f"jo_{n}{f}") for f in range(2)] for n in ("x_in", "rows_out"))
        passed = keep["passed"]
        block = ctx.enter_context(nc.Block())
        x_v = d["x"].rearrange("b h w c -> (b h w) c").rearrange("(s t p) c -> s p t c", p=P, t=HT)
        LOADS = 7 * 16

        @block.sync
        def _(sp):
            sp.dma_start(ident[:, :], d["c_ident"]).then_inc(weights, 16)
            sp.dma_start(wo[:, :, :], chunks(d["w_out"])).then_inc(weights, 16)
            sp.dma_start(wg[:, :, :], chunks(d["gate_w"])).then_inc(weights, 16)
            sp.dma_start(bo[:, :], rows(d["b_out"], P)).then_inc(weights, 16)
            sp.dma_start(bg[:, :], rows(d["gate_b"], P)).then_inc(weights, 16)
            sp.dma_start(earlier[:, :], d["c_earlier"]).then_inc(weights, 16)
            sp.dma_start(region[:, :], d["c_region"]).then_inc(weights, 16)
            sp.sem_inc(t_ready, 2 * HT)
            with sp.Fori(0, B) as b:
                for f in range(2):
                    sp.wait_ge(t_ready, b * 2 * HT + ((f + 1) * HT + 2))
                    sp.dma_start(x[:, f], x_v[bass.ds(b * 2 + f, 1)].rearrange("s p t c -> (s p) t c")).then_inc(x_in[f], 16)
            ready = keep["biases_in"]
            sp.dma_start(keep["b1"][:, :, :], d["b1"].rearrange("e (k p) -> p e k", p=P), allow_slow_non_contiguous=True).then_inc(ready, 16)
            sp.dma_start(keep["b2"][:, :, :].rearrange("p e c -> p (e c)"), rows(d["b2"].rearrange("e c -> (e c)"), P)).then_inc(ready, 16)
            sp.dma_start(keep["ident"][:, :], d["c_ident"]).then_inc(ready, 16)

        @block.gpsimd
        def _(pool):
            pool.memset(half[:, :], -0.5).then_inc(memsets, 1)
            pool.memset(above[:, :, :, :], 0.0).then_inc(memsets, 1)
            pool.memset(before[:, :, :], 0.0).then_inc(memsets, 1)
            pool.memset(run[:, :, :], 0.0).then_inc(memsets, 1)
            pool.memset(ones[:, :], 1.0).then_inc(memsets, 1)
            pool.wait_ge(memsets, 1)

            def inverse_root(b, f):
                pool.wait_ge(var_ready, b * 2 + f + 1)
                pool.tensor_tensor(rstd[:, :], var[:, :], half[:, :], ALU.pow).then_inc(rstd_ready, 1)

            def queue(b, f):
                pool.wait_ge(at_ready, b * 2 + f + 1)
                pool.sem_inc(passed, 1)
                for t in range(HT):
                    for k in range(2):
                        pool.indirect_dma_start(out=d["rows"], out_offset=bass.IndirectOffsetOnAxis(ap=at[:, f, t, k:k + 1], axis=0),
                                                in_=tn[:, f, t, :], in_offset=None).then_inc(rows_out[f], 16)

            every_half(pool, inverse_root, queue)
            for f in range(2):
                pool.wait_ge(rows_out[f], B * 2 * HT * 16)

        @block.scalar
        def _(act):
            act.wait_ge(weights, LOADS)
            act.sem_inc(y_done, HT)
            act.sem_inc(gate_done, HT)

            def copies(b, f):
                s = b * 2 + f
                act.wait_ge(y_done, s * HT + HT)
                act.sem_inc(passed, 1)
                act.activation(oT[:, :, :], keep["o"][:, bass.ds(b, 1), f].rearrange("p b j t c -> p (b j) (t c)"), ACT.Copy).then_inc(oT_ready, 1)
                act.wait_ge(tn_turned, s + 1)
                act.wait_ge(gate_done, s * HT + HT)
                act.activation(tnT[:, :, :], psT[:, :, :], ACT.Copy).then_inc(tnT_ready, 1)

            def exps(b, f):
                act.wait_ge(score_ready, b * 2 + f + 3)
                act.activation(prob[:, :, :], score[:, :, :], ACT.Exp).then_inc(exp_done, 1)

            every_half(act, copies, exps)

        @block.tensor
        def _(pe):
            pe.wait_ge(weights, LOADS)
            pe.sem_inc(tnT_ready, 1)
            pe.sem_inc(t_ready, 2)
            pe.sem_inc(score_ready, 2)
            pe.wait_ge(memsets, 5)

            def products(b, f):
                s = b * 2 + f
                pe.wait_ge(oT_ready, s + 1)
                for t in range(HT):
                    pe.wait_ge(t_ready, s * HT + (2 * HT + 1 + t))
                    for c in range(CH):
                        mm = pe.matmul(psY[:, t % 2, 0:NC], oT[:, c, t * P:(t + 1) * P], wo[:, c, :], start=c == 0, stop=c == CH - 1)
                    mm.then_inc(y_done, 1)
                pe.wait_ge(tnT_ready, s + 1)
                for t in range(HT):
                    pe.wait_ge(tn_ready, s * HT + (t + 1))
                    for j in range(CH):
                        mm = pe.transpose(psT[:, j, t * P:(t + 1) * P], tn[:, f, t, j * P:(j + 1) * P], ident[:, :])
                mm.then_inc(tn_turned, 1)
                pe.wait_ge(tnT_ready, s + 2)
                pe.wait_ge(score_ready, s + 1)
                for t in range(HT):
                    for c in range(CH):
                        mm = pe.matmul(psG[:, f, t * E:(t + 1) * E], tnT[:, c, t * P:(t + 1) * P], wg[:, c, :], start=c == 0, stop=c == CH - 1)
                    mm.then_inc(gate_done, 1)

            def ranks(b, f):
                s = b * 2 + f
                pe.wait_ge(chosen_ready, s + 1)
                c2 = chosen[:, :, :].rearrange("p t e -> p (t e)")
                pe.matmul(psR[:, 0].rearrange("p t e -> p (t e)"), earlier[:, :], c2, start=True, stop=True)
                pe.matmul(psR[:, 1].rearrange("p t e -> p (t e)"), ones[:, :], c2, start=True, stop=True).then_inc(ranked, 1)

            every_half(pe, products, ranks)

        @block.vector
        def _(dve):
            dve.wait_ge(weights, LOADS)
            dve.wait_ge(memsets, 5)

            def tokens(b, f):
                n = Count()
                s = b * 2 + f
                tile = lambda t: keep["acc"][:, bass.ds(b * TI + (f * HT + t), 1), :].rearrange("p o c -> p (o c)")
                dve.wait_ge(x_in[f], b * 16 + 16)
                b3 = bo[:, :].rearrange("p (o c) -> p o c", o=1).broadcast_to([P, HT, NC])
                dve.tensor_tensor(x[:, f], x[:, f], b3, ALU.add).then_inc(steps, n.up())
                dve.wait_ge(steps, s * JOIN_K + n.now)
                for t in range(HT):
                    dve.wait_ge(y_done, s * HT + (HT + t + 1))
                    dve.tensor_tensor(tile(t), psY[:, t % 2, 0:NC], x[:, f, t, :], ALU.add).then_inc(t_ready, 1)
                dve.wait_ge(t_ready, s * HT + (3 * HT + 2))
                dve.sem_inc(passed, 1)
                for t in range(HT):
                    dve.bn_stats(stats[:, t, :], tile(t)).then_inc(steps, n.up())
                dve.wait_ge(steps, s * JOIN_K + n.now)
                dve.sem_inc(passed, 1)
                for t in range(HT):
                    dve.bn_aggr(mv[:, t, :], stats[:, t, :]).then_inc(steps, n.up())
                dve.wait_ge(steps, s * JOIN_K + n.now)
                dve.tensor_scalar(var[:, :], mv[:, :, 1], 1e-5, None, ALU.add).then_inc(var_ready, 1)
                dve.wait_ge(rstd_ready, s + 1)
                if not isinstance(b, int):
                    dve.wait_ge(rows_out[f], b * (2 * HT * 16))
                for t in range(HT):
                    dve.tensor_scalar(tn[:, f, t, :], tile(t), mv[:, t, 0:1], rstd[:, t:t + 1], ALU.subtract, ALU.mult).then_inc(tn_ready, 1)
                assert n.now == JOIN_K, n.now

            def gates(b, f):
                n = Count()
                s = b * 2 + f

                def after():
                    dve.wait_ge(gate_steps, s * GATE_K + n.now)

                dve.wait_ge(gate_done, s * HT + 2 * HT)
                g3 = bg[:, :].rearrange("p (o e) -> p o e", o=1).broadcast_to([P, HT, E])
                dve.tensor_tensor(score[:, :, :], psG[:, f, 0:HT * E].rearrange("p (t e) -> p t e", e=E), g3, ALU.add).then_inc(gate_steps, n.up())
                after()
                dve.tensor_reduce(one[:, :], score[:, :, :], AX.X, ALU.max).then_inc(gate_steps, n.up())
                after()
                dve.tensor_tensor(score[:, :, :], score[:, :, :], inner(one[:, :], E), ALU.subtract).then_inc(score_ready, 1)
                dve.wait_ge(exp_done, s + 1)
                dve.tensor_reduce(one[:, :], prob[:, :, :], AX.X, ALU.add).then_inc(gate_steps, n.up())
                after()
                dve.reciprocal(one[:, :], one[:, :]).then_inc(gate_steps, n.up())
                after()
                dve.tensor_tensor(prob[:, :, :], prob[:, :, :], inner(one[:, :], E), ALU.mult).then_inc(gate_steps, n.up())
                after()
                for e in range(E):
                    for lo, hi, op in ((0, e, ALU.is_ge), (e + 1, E, ALU.is_gt)):
                        if lo < hi:
                            dve.tensor_tensor(above[:, :, e, lo:hi], prob[:, :, lo:hi], prob[:, :, e:e + 1].broadcast_to([P, HT, hi - lo]), op
                                              ).then_inc(gate_steps, n.up())
                after()
                dve.tensor_reduce(top[:, :, :], above[:, :, :, :], AX.X, ALU.add).then_inc(gate_steps, n.up())
                after()
                dve.tensor_scalar(chosen[:, :, :], top[:, :, :], 1.5, None, ALU.is_lt).then_inc(chosen_ready, 1)
                dve.wait_ge(chosen_ready, s + 1)
                dve.tensor_copy(before[:, :, 1:2], chosen[:, :, 0:1]).then_inc(gate_steps, n.up())
                dve.tensor_tensor(before[:, :, 2], chosen[:, :, 0], chosen[:, :, 1], ALU.add).then_inc(gate_steps, n.up())
                after()
                dve.tensor_tensor(before[:, :, 3], before[:, :, 2], chosen[:, :, 2], ALU.add).then_inc(gate_steps, n.up())
                dve.tensor_tensor(top[:, :, :], chosen[:, :, :], prob[:, :, :], ALU.mult).then_inc(gate_steps, n.up())
                after()
                dve.scalar_tensor_tensor(pick[:, :, 0, :], before[:, :, :], 0.5, chosen[:, :, :], ALU.is_lt, ALU.mult).then_inc(gate_steps, n.up())
                dve.tensor_reduce(one[:, :], top[:, :, :], AX.X, ALU.add).then_inc(gate_steps, n.up())
                after()
                dve.tensor_tensor(pick[:, :, 1, :], chosen[:, :, :], pick[:, :, 0, :], ALU.subtract).then_inc(gate_steps, n.up())
                dve.tensor_scalar(one[:, :], one[:, :], 1e-9, None, ALU.add).then_inc(gate_steps, n.up())
                after()
                dve.reciprocal(one[:, :], one[:, :]).then_inc(gate_steps, n.up())
                after()
                dve.tensor_tensor(top[:, :, :], top[:, :, :], inner(one[:, :], E), ALU.mult).then_inc(gate_steps, n.up())
                after()
                two = lambda v: bass.AP(tensor=v.tensor, offset=v.offset, ap=[v.ap[0], v.ap[1], [0, 2], v.ap[2]])
                dve.tensor_tensor(picked[:, :, :, :], pick[:, :, :, :], two(top[:, :, :]), ALU.mult).then_inc(gate_steps, n.up())
                after()
                dst = keep["gates"][:, bass.ds(b * TI + f * HT, HT), :]
                dve.tensor_reduce(dst, picked[:, :, :, :], AX.X, ALU.add).then_inc(gate_steps, n.up())
                after()
                dve.wait_ge(ranked, s + 1)
                for t in range(HT):
                    dve.tensor_tensor(run[:, t + 1], run[:, t], psR[:, 1, t], ALU.add).then_inc(gate_steps, n.up())
                    after()
                dve.tensor_tensor(place[:, :, :], psR[:, 0], run[:, 0:HT], ALU.add).then_inc(gate_steps, n.up())
                after()
                r3 = region[:, :].rearrange("p (o e) -> p o e", o=1).broadcast_to([P, HT, E])
                dve.tensor_tensor(place[:, :, :], place[:, :, :], r3, ALU.add).then_inc(gate_steps, n.up())
                dve.tensor_copy(run[:, 0], run[:, HT]).then_inc(gate_steps, n.up())
                after()
                dve.tensor_tensor(picked[:, :, :, :], pick[:, :, :, :], two(place[:, :, :]), ALU.mult).then_inc(gate_steps, n.up())
                after()
                dve.tensor_reduce(slot[:, :, :], picked[:, :, :, :], AX.X, ALU.add).then_inc(gate_steps, n.up())
                after()
                dve.tensor_scalar(slot[:, :, :], slot[:, :, :], float(E * QUEUE - 1), None, ALU.min).then_inc(gate_steps, n.up())
                after()
                dve.tensor_copy(keep["slots"][:, bass.ds(b * TI + f * HT, HT), :], slot[:, :, :]).then_inc(gate_steps, n.up())
                dve.tensor_copy(at[:, f], slot[:, :, :]).then_inc(at_ready, 1)
                dve.wait_ge(at_ready, s + 1)
                after()
                assert n.now == GATE_K, n.now

            every_half(dve, tokens, gates)
            dve.tensor_copy(keep["counts"][:, :], run[:, 0]).then_inc(gate_steps, 1)


JOIN_K = 2 * HT + 1
GATE_K = 35


def plan(nc, sem, d, keep):
    with ExitStack() as ctx:
        sb = lambda n, s, t=F32: ctx.enter_context(nc.sbuf_tensor(n, s, t))
        v, fl, up = sb("pl_v", [P, E]), sb("pl_fl", [P, E]), sb("pl_up", [P, E])
        whole = sb("pl_whole", [P, E], I32)
        ends = sb("pl_ends", [P, E + 1])
        last = sb("pl_last", [P, 1])
        tile, past, skip, expert = (sb("pl_" + x, [P, SLOTS_T]) for x in ("tile", "past", "skip", "expert"))
        region = sb("pl_region", [P, E])
        tails = sb("pl_tails", [P, E], I32)
        jump, step = sb("pl_jump", [P, E]), sb("pl_step", [P, E - 1])
        beyond, row = sb("pl_beyond", [P, NT, 2]), sb("pl_row", [P, NT, 2])
        zero = sb("pl_zero", [P, TN // P, NC])
        loaded, steps, zeroed, tails_ready, tails_out = (sem("pl_" + n) for n in ("loaded", "steps", "zeroed", "tails_ready", "tails_out"))
        block = ctx.enter_context(nc.Block())

        @block.gpsimd
        def _(pool):
            pool.memset(zero[:, :, :], 0.0).then_inc(zeroed, 1)

        @block.sync
        def _(sp):
            sp.dma_start(tile[:, :], d["c_tile"]).then_inc(loaded, 16)
            sp.dma_start(region[:, :], d["c_region"]).then_inc(loaded, 16)
            sp.wait_ge(zeroed, 1)
            sp.wait_ge(tails_ready, 1)
            for e in range(E):
                tail = sp.value_load(tails[0:1, e:e + 1], min_val=e * QUEUE, max_val=e * QUEUE + QUEUE - TN)
                sp.dma_start(d["rows"][bass.ds(tail, TN), :].rearrange("(m p) c -> p m c", p=P), zero[:, :, :]).then_inc(tails_out, 16)
            sp.wait_ge(tails_out, 16 * E)

        @block.vector
        def _(dve):
            n = Count()

            def after():
                dve.wait_ge(steps, n.now)

            dve.wait_ge(loaded, 32)
            dve.tensor_scalar(v[:, :], keep["counts"][:, :], 1.0 / TN, float(TN - 1) / TN, ALU.mult, ALU.add).then_inc(steps, n.up())
            dve.tensor_tensor(up[:, :], keep["counts"][:, :], region[:, :], ALU.add).then_inc(steps, n.up())
            dve.memset(ends[:, 0:1], 0.0).then_inc(steps, n.up())
            after()
            dve.tensor_copy(tails[:, :], up[:, :]).then_inc(tails_ready, 1)
            dve.tensor_copy(whole[:, :], v[:, :]).then_inc(steps, n.up())
            after()
            dve.tensor_copy(fl[:, :], whole[:, :]).then_inc(steps, n.up())
            after()
            dve.wait_ge(tails_ready, 1)
            dve.tensor_tensor(up[:, :], fl[:, :], v[:, :], ALU.is_gt).then_inc(steps, n.up())
            after()
            dve.tensor_tensor(fl[:, :], fl[:, :], up[:, :], ALU.subtract).then_inc(steps, n.up())
            after()
            for e in range(E):
                dve.tensor_tensor(ends[:, e + 1:e + 2], ends[:, e:e + 1], fl[:, e:e + 1], ALU.add).then_inc(steps, n.up())
                after()
            dve.tensor_scalar(last[:, :], ends[:, E:E + 1], -1.0, None, ALU.add).then_inc(steps, n.up())
            after()
            dve.tensor_scalar(tile[:, :], tile[:, :], last[:, 0:1], None, ALU.min).then_inc(steps, n.up())
            dve.memset(expert[:, :], 0.0).then_inc(steps, n.up())
            dve.memset(skip[:, :], 0.0).then_inc(steps, n.up())
            after()
            for e in range(E - 1):
                dve.tensor_scalar(past[:, :], tile[:, :], ends[:, e + 1:e + 2], None, ALU.is_ge).then_inc(steps, n.up())
                after()
                dve.tensor_tensor(expert[:, :], expert[:, :], past[:, :], ALU.add).then_inc(steps, n.up())
                dve.scalar_tensor_tensor(skip[:, :], past[:, :], fl[:, e:e + 1], skip[:, :], ALU.mult, ALU.add).then_inc(steps, n.up())
                after()
            dve.tensor_tensor(skip[:, :], tile[:, :], skip[:, :], ALU.subtract).then_inc(steps, n.up())
            dve.tensor_copy(keep["expert"][:, :], expert[:, :]).then_inc(steps, n.up())
            after()
            dve.tensor_scalar(skip[:, :], skip[:, :], float(TN), None, ALU.mult).then_inc(steps, n.up())
            after()
            dve.scalar_tensor_tensor(skip[:, :], expert[:, :], float(QUEUE), skip[:, :], ALU.mult, ALU.add).then_inc(steps, n.up())
            after()
            dve.tensor_copy(keep["start"][:, :], skip[:, :]).then_inc(steps, n.up())
            dve.scalar_tensor_tensor(jump[:, :], ends[:, 0:E], float(TN), region[:, :], ALU.mult, ALU.subtract).then_inc(steps, n.up())
            dve.tensor_copy(row[:, :, :], keep["slots"][:, :, :]).then_inc(steps, n.up())
            after()
            dve.tensor_tensor(step[:, :], jump[:, 1:E], jump[:, 0:E - 1], ALU.subtract).then_inc(steps, n.up())
            after()
            for e in range(1, E):
                dve.tensor_scalar(beyond[:, :, :], keep["slots"][:, :, :], float(e * QUEUE), None, ALU.is_ge).then_inc(steps, n.up())
                after()
                dve.scalar_tensor_tensor(row[:, :, :], beyond[:, :, :], step[:, e - 1:e], row[:, :, :], ALU.mult, ALU.add).then_inc(steps, n.up())
                after()
            dve.tensor_copy(keep["result_at"][:, :, :], row[:, :, :]).then_inc(steps, n.up())
            after()


def experts(nc, sem, d, keep):
    TM = TN // P
    R = 4
    HB = 2
    YAT = 3 + R
    XAT = 6
    with ExitStack() as ctx:
        sb = lambda n, s, t=F32: ctx.enter_context(nc.sbuf_tensor(n, s, t))
        raw1, raw2 = sb("ex_raw1", [P, R, CH, P]), sb("ex_raw2", [P, R, NC])
        w1, w2 = sb("ex_w1", [P, R, 2, CH, P], F32R), sb("ex_w2", [P, R, 2, NC], F32R)
        xr = sb("ex_xr", [P, 2, TM, NC])
        xT = sb("ex_xT", [P, 2, 2, CH, TN], F32R)
        h, hp = sb("ex_h", [P, R, TN]), sb("ex_hp", [P, R, 2, TN], F32R)
        b1, b2, ident = keep["b1"], keep["b2"], keep["ident"]
        bias1, bias2 = sb("ex_bias1", [P, 2, KH]), sb("ex_bias2", [P, 2, NC])
        y = sb("ex_y", [P, 2, TM, NC])
        psX = ctx.enter_context(nc.psum_tensor("ex_psX", [P, 2, 512], F32))
        psH = ctx.enter_context(nc.psum_tensor("ex_psH", [P, HB, 512], F32))
        psY = ctx.enter_context(nc.psum_tensor("ex_psY", [P, TM, 512], F32))
        weights = keep["biases_in"]
        (split_done, h_done, gelu_done, hp_ready, y_done, y_ready, x_turned, x_high, x_low) = (sem("ex_" + n) for n in (
            "split_done", "h_done", "gelu_done", "hp_ready", "y_done", "y_ready", "x_turned", "x_high", "x_low"))
        raw_in = [sem(f"ex_raw_in{r}") for r in range(R)]
        x_in, b_in, y_out = ([sem(f"ex_{n}{u}") for u in range(2)] for n in ("x_in", "b_in", "y_out"))
        passed = keep["passed"]
        block = ctx.enter_context(nc.Block())
        LOADS = 3 * 16

        def every_two(eng, two):
            assert TILES % 2 == 1
            two(0, True)
            with eng.Fori(1, TILES // 2) as i:
                two(i, False)
            two(TILES // 2, False, True)

        def load_value(eng, name, n, most):
            return eng.value_load(keep[name][0:1, bass.ds(n, 1)], min_val=0, max_val=most)

        @block.sync
        def _(sp):
            w1_v = d["w1"].rearrange("e (c p) (k n) -> k e p c n", p=P, n=P)
            w2_v = d["w2"].rearrange("e (k p) c -> k e p c", p=P)
            results = d["results"].rearrange("(n m p) c -> n m p c", m=TM, p=P)

            def store(n, u):
                sp.wait_ge(y_ready, n * TM + TM)
                sp.dma_start(results[bass.ds(n, 1)].rearrange("n m p c -> p (n m) c"), y[:, u]).then_inc(y_out[u], 16)

            def two(i, first, last=False):
                for u in range(1 if last else 2):
                    n = i * 2 + u
                    e = load_value(sp, "expert", n, E - 1)
                    for k in range(KH):
                        if k == YAT and (not first or u):
                            store(n - 1, 1 - u)
                        if not first or u or k >= R:
                            sp.wait_ge(split_done, n * 4 * KH + 4 * (k - R + 1))
                        sp.dma_start(raw1[:, k % R], w1_v[k, bass.ds(e, 1)].rearrange("e p c n -> (e p) c n")).then_inc(raw_in[k % R], 16)
                        sp.dma_start(raw2[:, k % R], w2_v[k, bass.ds(e, 1)].rearrange("e p c -> (e p) c")).then_inc(raw_in[k % R], 16)

            every_two(sp, two)
            store(TILES - 1, 0)
            sp.wait_ge(y_out[0], (TILES // 2 + 2) * 16)
            sp.wait_ge(y_out[1], (TILES // 2 + 1) * 16)

        @block.gpsimd
        def _(pool):
            pool.wait_ge(weights, LOADS)

            def load(n, u):
                e = load_value(pool, "expert", n, E - 1)
                start = load_value(pool, "start", n, E * QUEUE - TN)
                pool.dma_start(xr[:, u], d["rows"][bass.ds(start, TN), :].rearrange("(m p) c -> p m c", p=P)).then_inc(x_in[u], 16)
                pool.dma_start(bias1[:, u, :], b1[:, bass.ds(e, 1), :].rearrange("p e k -> p (e k)")).then_inc(b_in[u], 16)
                pool.dma_start(bias2[:, u, :], b2[:, bass.ds(e, 1), :].rearrange("p e c -> p (e c)")).then_inc(b_in[u], 16)

            def two(i, first, last=False):
                for u in range(0 if last else 2):
                    n = i * 2 + u
                    if not first or u:
                        pool.wait_ge(x_turned, n * CH)
                        pool.wait_ge(y_ready, n * TM)
                        pool.wait_ge(gelu_done, n * KH)
                        pool.sem_inc(passed, 1)
                    load(n + 1, 1 - u)

            load(0, 0)
            every_two(pool, two)

        @block.scalar
        def _(act):
            def high(n, u, c, fresh):
                act.wait_ge(x_turned, n * CH + (c + 1))
                if not fresh:
                    act.wait_ge(h_done, n * KH - KH)
                act.activation(xT[:, u, 0, c, :], psX[:, (u + c) % 2, 0:TN], ACT.Copy).then_inc(x_high, 1)

            def two(i, first, last=False):
                for u in range(1 if last else 2):
                    n = i * 2 + u
                    act.wait_ge(b_in[u], i * 32 + 32)
                    for k in range(KH):
                        act.wait_ge(h_done, n * KH + (k + 1))
                        if not first or u or k >= R:
                            act.wait_ge(hp_ready, n * 2 * KH + 2 * (k - R + 1))
                        act.activation(h[:, k % R, :], psH[:, k % HB, 0:TN], ACT.Gelu, bias=bias1[:, u, k:k + 1]).then_inc(gelu_done, 1)
                        if XAT <= k < XAT + CH and not last:
                            high(n + 1, 1 - u, k - XAT, first and not u)

            for c in range(CH):
                high(0, 0, c, True)
            every_two(act, two)

        @block.tensor
        def _(pe):
            pe.wait_ge(weights, LOADS)

            def turn(n, u, c, seen, early):
                if c == 0:
                    pe.wait_ge(x_in[u], seen)
                if not early:
                    pe.wait_ge(x_low, n * CH + (c - 1))
                for m in range(TM):
                    mm = pe.transpose(psX[:, (u + c) % 2, m * P:(m + 1) * P], xr[:, u, m, c * P:(c + 1) * P], ident[:, :])
                mm.then_inc(x_turned, 1)

            def down(n, k, first):
                pe.wait_ge(hp_ready, n * 2 * KH + 2 * (k + 1))
                if k == 0 and not first:
                    pe.wait_ge(y_ready, n * TM)
                for m in range(TM):
                    for a, c in PASSES:
                        mm = pe.matmul(psY[:, m, 0:NC], hp[:, k % R, a, m * P:(m + 1) * P], w2[:, k % R, c, :],
                                       start=k == 0 and (a, c) == (0, 0), stop=k == KH - 1 and a == 1)
                mm.then_inc(y_done, 1)

            def two(i, first, last=False):
                for u in range(1 if last else 2):
                    n = i * 2 + u
                    pe.wait_ge(x_low, n * CH + CH)
                    for k in range(KH):
                        pe.wait_ge(split_done, n * 4 * KH + 4 * (k + 1))
                        if not first or u or k >= HB:
                            pe.wait_ge(gelu_done, n * KH + (k - HB + 1))
                        for c in range(CH):
                            for a, z in PASSES:
                                mm = pe.matmul(psH[:, k % HB, 0:TN], w1[:, k % R, a, c, :], xT[:, u, z, c, :],
                                               start=c == 0 and (a, z) == (0, 0), stop=c == CH - 1 and a == 1)
                        mm.then_inc(h_done, 1)
                        if k >= 2:
                            down(n, k - 2, first and not u)
                        elif not first or u:
                            down(n - 1, KH - 2 + k, False)
                        if XAT <= k < XAT + CH and not last:
                            turn(n + 1, 1 - u, k - XAT, i * 16 + u * 16 + 16, False)

            for c in range(CH):
                turn(0, 0, c, 16, c < 2)
            every_two(pe, two)
            for k in (KH - 2, KH - 1):
                down(TILES - 1, k, False)

        @block.vector
        def _(dve):
            for u in range(2):
                dve.sem_inc(y_out[u], 16)

            def low(n, u, c):
                dve.wait_ge(x_high, n * CH + (c + 1))
                dve.tensor_tensor(xT[:, u, 1, c, :], psX[:, (u + c) % 2, 0:TN], xT[:, u, 0, c, :].bitcast(F32), ALU.subtract).then_inc(x_low, 1)

            def split(n, k, early):
                dve.wait_ge(raw_in[k % R], n * (KH // R * 32) + (k // R + 1) * 32)
                if not early:
                    dve.wait_ge(y_done, n * KH + (k - R + 1))
                s = n * 4 * KH + 4 * k
                dve.tensor_copy(w1[:, k % R, 0], raw1[:, k % R]).then_inc(split_done, 1)
                dve.tensor_copy(w2[:, k % R, 0], raw2[:, k % R]).then_inc(split_done, 1)
                dve.wait_ge(split_done, s + 1)
                dve.tensor_tensor(w1[:, k % R, 1], raw1[:, k % R], w1[:, k % R, 0].bitcast(F32), ALU.subtract).then_inc(split_done, 1)
                dve.wait_ge(split_done, s + 2)
                dve.tensor_tensor(w2[:, k % R, 1], raw2[:, k % R], w2[:, k % R, 0].bitcast(F32), ALU.subtract).then_inc(split_done, 1)

            def hidden(n, k, early):
                dve.wait_ge(gelu_done, n * KH + (k + 1))
                if not early:
                    dve.wait_ge(y_done, n * KH + (k - R + 1))
                dve.tensor_copy(hp[:, k % R, 0, :], h[:, k % R, :]).then_inc(hp_ready, 1)
                dve.wait_ge(hp_ready, n * 2 * KH + (2 * k + 1))
                dve.tensor_tensor(hp[:, k % R, 1, :], h[:, k % R, :], hp[:, k % R, 0, :].bitcast(F32), ALU.subtract).then_inc(hp_ready, 1)

            def result(n, u, count):
                dve.wait_ge(y_done, n * KH + KH)
                dve.wait_ge(y_out[u], count)
                for m in range(TM):
                    dve.tensor_tensor(y[:, u, m, :], psY[:, m, 0:NC], bias2[:, u, :], ALU.add).then_inc(y_ready, 1)

            def two(i, first, last=False):
                for u in range(1 if last else 2):
                    n = i * 2 + u
                    dve.wait_ge(b_in[u], i * 32 + 32)
                    for k in range(KH):
                        early = first and not u and k < R
                        split(n, k, early)
                        if k == 2 and (not first or u):
                            result(n - 1, 1 - u, (i * 16 + 16) if u else i * 16)
                        if k >= 2:
                            hidden(n, k - 2, first and not u and k - 2 < R)
                        elif not first or u:
                            hidden(n - 1, KH - 2 + k, False)
                        if XAT < k <= XAT + CH and not last:
                            low(n + 1, 1 - u, k - XAT - 1)

            for c in range(CH):
                low(0, 0, c)
            every_two(dve, two)
            for k in (KH - 2, KH - 1):
                hidden(TILES - 1, k, False)
            result(TILES - 1, 0, TILES // 2 * 16 + 16)


def combine(nc, sem, d, keep):
    with ExitStack() as ctx:
        sb = lambda n, s, t=F32: ctx.enter_context(nc.sbuf_tensor(n, s, t))
        at = sb("co_at", [P, 2, HT, 2], I32)
        gate = sb("co_gate", [P, 2, HT, 2])
        r = sb("co_r", [P, 2, HT, 2, NC])
        part = sb("co_part", [P, 2, HT, NC])
        staged, part_done, sum_done = (sem("co_" + n) for n in ("staged", "part_done", "sum_done"))
        taken = [[sem(f"co_taken{f}{t}") for t in range(HT)] for f in range(2)]
        written = [sem(f"co_written{f}") for f in range(2)]
        passed = keep["passed"]
        block = ctx.enter_context(nc.Block())
        out_v = d["out"].rearrange("b h w c -> (b h w) c").rearrange("(t p) c -> t p c", p=P)

        @block.gpsimd
        def _(pool):
            pool.sem_inc(sum_done, 2 * HT)
            with pool.Fori(0, B) as b:
                for f in range(2):
                    pool.wait_ge(sum_done, b * 2 * HT + (f + 1) * HT)
                    pool.sem_inc(passed, 1)
                    pool.tensor_copy(at[:, f], keep["result_at"][:, bass.ds(b * TI + f * HT, HT), :]).then_inc(staged, 1)
                    pool.tensor_copy(gate[:, f], keep["gates"][:, bass.ds(b * TI + f * HT, HT), :]).then_inc(staged, 1)
                    pool.wait_ge(staged, b * 4 + 2 * f + 2)
                    pool.sem_inc(passed, 1)
                    for t in range(HT):
                        for k in range(2):
                            pool.indirect_dma_start(out=r[:, f, t, k, :], out_offset=None, in_=d["results"],
                                                    in_offset=bass.IndirectOffsetOnAxis(ap=at[:, f, t, k:k + 1], axis=0)
                                                    ).then_inc(taken[f][t], 16)

        @block.vector
        def _(dve):
            for f in range(2):
                dve.sem_inc(written[f], 16 * HT)
            with dve.Fori(0, B) as b:
                for f in range(2):
                    for t in range(HT):
                        s = b * 2 * HT + f * HT + t
                        dve.wait_ge(taken[f][t], b * 32 + 32)
                        if t == 0:
                            dve.wait_ge(written[f], b * (16 * HT) + 16 * HT)
                        acc = keep["acc"][:, bass.ds(s, 1), :].rearrange("p o c -> p (o c)")
                        dve.scalar_tensor_tensor(part[:, f, t, :], r[:, f, t, 0, :], gate[:, f, t, 0:1], acc, ALU.mult, ALU.add).then_inc(part_done, 1)
                        dve.wait_ge(part_done, s + 1)
                        dve.scalar_tensor_tensor(part[:, f, t, :], r[:, f, t, 1, :], gate[:, f, t, 1:2], part[:, f, t, :], ALU.mult, ALU.add).then_inc(sum_done, 1)

        @block.sync
        def _(sp):
            with sp.Fori(0, B) as b:
                for f in range(2):
                    for t in range(HT):
                        s = b * 2 * HT + f * HT + t
                        sp.wait_ge(sum_done, s + (2 * HT + 1))
                        sp.dma_start(out_v[bass.ds(s, 1)].rearrange("o p c -> (o p) c"), part[:, f, t, :]).then_inc(written[f], 16)
            for f in range(2):
                sp.wait_ge(written[f], (B + 1) * HT * 16)


NAMES = {"x": "x", "w_q": "L0_conv_w_q", "b_q": "L0_conv_b_q", "w_off0": "L0_conv_w_off0", "b_off0": "L0_conv_b_off0",
         "ln_g": "L0_conv_ln_g", "ln_b": "L0_conv_ln_b", "w_offp": "L0_conv_w_offp", "w_k": "L0_conv_w_k",
         "b_k": "L0_conv_b_k", "w_v": "L0_conv_w_v", "b_v": "L0_conv_b_v", "w_out": "L0_conv_w_out",
         "b_out": "L0_conv_b_out", "rpe": "L0_conv_rpe", "gate_w": "L0_ffn_gate_w", "gate_b": "L0_ffn_gate_b",
         "w1": "L0_ffn_w1", "b1": "L0_ffn_b1", "w2": "L0_ffn_w2", "b2": "L0_ffn_b2"}


def build(nc, d, out):
    def scratch(name, shape, dt=F32):
        d[name] = nc.dram_tensor("s_" + name, shape, dt, kind="Internal").ap()
    scratch("shifts", (G, SN, UN, UW))
    scratch("quads", (B * G, QY, QX, 2, GC))
    scratch("xn_scr", (NT * P, NC))
    scratch("q_scr", (PAIRS, 2, P, N))
    scratch("k_scr", (PAIRS, 2, P, N))
    scratch("v_scr", (PAIRS, TI, P, P))
    scratch("rows", (E * QUEUE, NC))
    scratch("results", (TILES * TN, NC))
    d["out"] = out
    with ExitStack() as ctx:
        sem = lambda name: ctx.enter_context(nc.semaphore(name))
        keep = {"passed": sem("passed")}
        with ExitStack() as held:
            for name, shape, dt in (("shift_at", [P, B, G, TI], I32), ("shift_w", [P, B, G, TI, 4], F32)):
                keep[name] = held.enter_context(nc.sbuf_tensor(name, shape, dt))
            keep["table_out"], keep["quad_out"] = sem("table_out"), sem("quad_out")
            with ExitStack() as front:
                for name, shape, dt in (("table", [UN, G, UN], F32), ("zero", [P, 8 * 2 * GC], F32),
                                        ("quad_at", [P, B, G, TI], I32), ("quad_w", [P, B, G, TI, 4], F32)):
                    keep[name] = front.enter_context(nc.sbuf_tensor(name, shape, dt))
                table(nc, sem, d, keep)
                with (nc.sbuf_tensor("q_pad", [P, 2, CH, B, H + 2, W + 2], F32R) as keep["q_pad"],
                      nc.sbuf_tensor("taps", [P, 9, CH, P], F32) as keep["taps"]):
                    mixer_q(nc, sem, d, keep)
                    offsets(nc, sem, d, keep)
                keys(nc, sem, d, keep)
            o_all = held.enter_context(nc.sbuf_tensor("o_all", [P, B, 2, CH, HT, P], F32))
            keep["o"] = o_all
            keep["acc"] = o_all[:, :, :, :, :, :].rearrange("p b f j t c -> p (b f j t c)").rearrange("p (t c) -> p t c", c=NC)
            attend(nc, sem, d, keep)
            keep["gates"] = held.enter_context(nc.sbuf_tensor("gates", [P, NT, 2], F32))
            keep["slots"] = held.enter_context(nc.sbuf_tensor("slots", [P, NT, 2], F32))
            keep["counts"] = held.enter_context(nc.sbuf_tensor("counts", [P, E], F32))
            for name, shape in (("b1", [P, E, KH]), ("b2", [P, E, NC]), ("ident", [P, P])):
                keep[name] = held.enter_context(nc.sbuf_tensor(name, shape, F32))
            keep["biases_in"] = sem("biases_in")
            join(nc, sem, d, keep)
            for name, shape, dt in (("expert", [P, SLOTS_T], I32), ("start", [P, SLOTS_T], I32),
                                    ("result_at", [P, NT, 2], I32)):
                keep[name] = held.enter_context(nc.sbuf_tensor(name, shape, dt))
            plan(nc, sem, d, keep)
            experts(nc, sem, d, keep)
            combine(nc, sem, d, keep)


def kernel(**inputs):
    import concourse.bacc as bacc
    from concourse.bass_utils import run_bass_kernel_spmd

    nc = bacc.Bacc("TRN2", target_bir_lowering=False, num_devices=1)
    arrays = {"in_" + n: np.ascontiguousarray(inputs[long]) for n, long in NAMES.items()}
    arrays |= {"in_" + n: a for n, a in constants().items()}
    d = {n[3:]: nc.dram_tensor(n, a.shape, mybir.dt.from_np(a.dtype), kind="ExternalInput").ap() for n, a in arrays.items()}
    out = nc.dram_tensor("out_0", (B, H, W, NC), F32, kind="ExternalOutput").ap()
    build(nc, d, out)
    r = run_bass_kernel_spmd(nc, [arrays], core_ids=[0])
    return r.results[0]["out_0"]
```
